# Optimizing a Trainium2 kernel written in Bass

```python
import numpy as np
import jax
import jax.numpy as jnp

def _softmax(x, axis=-1):
    return jax.nn.softmax(x, axis=axis)

def _gelu(x):
    return jax.nn.gelu(x, approximate=True)

def _silu(x):
    return jax.nn.silu(x)

def _sigmoid(x):
    return jax.nn.sigmoid(x)

def _layernorm(x, axis=-1, eps=1e-05):
    m = jnp.mean(x, axis=axis, keepdims=True)
    v = jnp.var(x, axis=axis, keepdims=True)
    return (x - m) / jnp.sqrt(v + eps)

def _scatter_add(tgt, idx, src, axis=0):
    return tgt.at[idx].add(src)

def _segment_sum(src, seg, n):
    return jax.ops.segment_sum(src, seg, n)
kernel_name = 'mk_decoder_preln_d1_seqx_r4_4040d3'

def setup_inputs(seed: int=0):
    np.random.seed(seed)
    _w = jnp.asarray

    def _rec_inputs():
        import jax
        import jax.numpy as jnp
        _rk = jax.random.key(seed)
        x = -0.0002928 + 1 * jax.random.normal(jax.random.fold_in(_rk, 1), (16, 128, 256), jnp.float32)
        _lenS = 128 - jax.random.randint(jax.random.fold_in(_rk, 7), (16,), 0, max(1, 128 // 4) + 1, jnp.int32)
        _lenS2 = 128 - jax.random.randint(jax.random.fold_in(_rk, 8), (16,), 0, max(1, 128 // 4) + 1, jnp.int32)
        _ctx_1024P = jax.random.normal(jax.random.fold_in(_rk, 11), (16, 16, 256), jnp.float32)
        _ctx_1024c = jax.random.dirichlet(jax.random.fold_in(_rk, 511), 0.3 * jnp.ones((16,), jnp.float32), (16, 128))
        _ctx_1024t = jnp.einsum('bsk,bkd->bsd', _ctx_1024c, _ctx_1024P)
        _ctx_1024t = _ctx_1024t * jax.lax.rsqrt(jnp.mean(jnp.square(_ctx_1024t)) + 1e-12) * 0.953939
        ctx_1024 = -1.39393e-06 + 0.999914 * (_ctx_1024t + 0.3 * jax.random.normal(jax.random.fold_in(_rk, 611), (16, 128, 256), jnp.float32))
        return (x, ctx_1024)
    x, ctx_1024 = _rec_inputs()

    def _L0_attn_setup():
        import jax, jax.numpy as jnp
        import numpy as np

        def _rope_cos_sin(m, d, dtype=jnp.float32):
            i = jnp.arange(d // 2, dtype=dtype)
            theta = jnp.power(jnp.asarray(10000.0, dtype), -2.0 * (i - 1.0) / d)
            pos = jnp.arange(m, dtype=dtype)
            ang = pos[:, None] * theta[None, :]
            return (jnp.cos(ang), jnp.sin(ang))

        def _rotate(t, cos, sin):
            te = t[..., 0::2]
            to = t[..., 1::2]
            re = te * cos + to * sin
            ro = -te * sin + to * cos
            return jnp.stack((re, ro), axis=-1).reshape(t.shape)
        key = jax.random.key(seed)
        k1, k2, k3, k4 = jax.random.split(key, 4)
        b, m, d = (4, 512, 256)
        scale = 1.0 / np.sqrt(d)
        return {'x': jax.random.normal(k1, (b, m, d), dtype=jnp.float32), 'w_q': jax.random.normal(k2, (d, d), dtype=jnp.float32) * scale, 'w_k': jax.random.normal(k3, (d, d), dtype=jnp.float32) * scale, 'w_v': jax.random.normal(k4, (d, d), dtype=jnp.float32) * scale}
    _L0_attn_all = _L0_attn_setup()
    _L0_attn_in = {k: v for k, v in _L0_attn_all.items() if k in ('w_q', 'w_k', 'w_v')}
    del _L0_attn_all

    def _L0_xattn_setup():
        import jax, jax.numpy as jnp
        import numpy as np
        B, L, D_MODEL = (2, 512, 256)
        HEADS, DH, K = (8, 128, 64)
        DILATIONS = np.array([1, 1, 2, 2, 4, 4, 8, 8], dtype=np.int32)
        key = jax.random.key(seed)
        ks = jax.random.split(key, 8)
        s_in = 1.0 / np.sqrt(D_MODEL)
        s_c = 1.0 / np.sqrt(HEADS * DH)
        return {'query': jax.random.normal(ks[0], (B, L, D_MODEL), dtype=jnp.float32), 'key': jax.random.normal(ks[1], (B, L, D_MODEL), dtype=jnp.float32), 'value': jax.random.normal(ks[2], (B, L, D_MODEL), dtype=jnp.float32), 'Wq': jax.random.uniform(ks[3], (HEADS, DH, D_MODEL), minval=-s_in, maxval=s_in), 'bq': jnp.zeros((HEADS, DH), dtype=jnp.float32), 'Wk': jax.random.uniform(ks[4], (HEADS, DH, D_MODEL), minval=-s_in, maxval=s_in), 'bk': jnp.zeros((HEADS, DH), dtype=jnp.float32), 'Wv': jax.random.uniform(ks[5], (HEADS, DH, D_MODEL), minval=-s_in, maxval=s_in), 'bv': jnp.zeros((HEADS, DH), dtype=jnp.float32), 'Wc': jax.random.uniform(ks[6], (D_MODEL, HEADS * DH), minval=-s_c, maxval=s_c), 'bc': jnp.zeros((D_MODEL,), dtype=jnp.float32)}
    _L0_xattn_all = _L0_xattn_setup()
    _L0_xattn_in = {k: v for k, v in _L0_xattn_all.items() if k in ('Wq', 'bq', 'Wk', 'bk', 'Wv', 'bv', 'Wc', 'bc')}
    del _L0_xattn_all

    def _L0_ffn_setup():
        import jax, jax.numpy as jnp
        import numpy as np
        B, F, D, H, E, K = (4, 512, 256, 512, 8, 2)
        key = jax.random.key(seed)
        ks = jax.random.split(key, 9)
        sc = lambda k, shape, fan_in: jax.random.normal(k, shape, jnp.float32) * fan_in ** (-0.5)
        return {'x': jax.random.normal(ks[0], (B, F, D), jnp.float32), 'rw1': sc(ks[1], (D, D), D), 'rb1': jnp.zeros((D,), jnp.float32), 'rw2': sc(ks[2], (D, E), D), 'rb2': jnp.zeros((E,), jnp.float32), 'ew1': sc(ks[3], (E, D, H), D), 'eb1': jnp.zeros((E, H), jnp.float32), 'ew2': sc(ks[4], (E, H, D), H), 'eb2': jnp.zeros((E, D), jnp.float32)}
    _L0_ffn_all = _L0_ffn_setup()
    _L0_ffn_in = {k: v for k, v in _L0_ffn_all.items() if k in ('rw1', 'rb1', 'rw2', 'rb2', 'ew1', 'eb1', 'ew2', 'eb2')}
    del _L0_ffn_all
    return {'x': x, 'ctx_1024': ctx_1024, 'L0_attn_w_q': _L0_attn_in['w_q'], 'L0_attn_w_k': _L0_attn_in['w_k'], 'L0_attn_w_v': _L0_attn_in['w_v'], 'L0_xattn_Wq': _L0_xattn_in['Wq'], 'L0_xattn_bq': _L0_xattn_in['bq'], 'L0_xattn_Wk': _L0_xattn_in['Wk'], 'L0_xattn_bk': _L0_xattn_in['bk'], 'L0_xattn_Wv': _L0_xattn_in['Wv'], 'L0_xattn_bv': _L0_xattn_in['bv'], 'L0_xattn_Wc': _L0_xattn_in['Wc'], 'L0_xattn_bc': _L0_xattn_in['bc'], 'L0_ffn_rw1': _L0_ffn_in['rw1'], 'L0_ffn_rb1': _L0_ffn_in['rb1'], 'L0_ffn_rw2': _L0_ffn_in['rw2'], 'L0_ffn_rb2': _L0_ffn_in['rb2'], 'L0_ffn_ew1': _L0_ffn_in['ew1'], 'L0_ffn_eb1': _L0_ffn_in['eb1'], 'L0_ffn_ew2': _L0_ffn_in['ew2'], 'L0_ffn_eb2': _L0_ffn_in['eb2']}

def reference(x, ctx_1024, L0_attn_w_q, L0_attn_w_k, L0_attn_w_v, L0_xattn_Wq, L0_xattn_bq, L0_xattn_Wk, L0_xattn_bk, L0_xattn_Wv, L0_xattn_bv, L0_xattn_Wc, L0_xattn_bc, L0_ffn_rw1, L0_ffn_rb1, L0_ffn_rw2, L0_ffn_rb2, L0_ffn_ew1, L0_ffn_eb1, L0_ffn_ew2, L0_ffn_eb2):
    import jax
    import jax.numpy as jnp

    def _L0_attn_ref(x, w_q, w_k, w_v):
        import jax, jax.numpy as jnp
        import numpy as np

        def _rope_cos_sin(m, d, dtype=jnp.float32):
            i = jnp.arange(d // 2, dtype=dtype)
            theta = jnp.power(jnp.asarray(10000.0, dtype), -2.0 * (i - 1.0) / d)
            pos = jnp.arange(m, dtype=dtype)
            ang = pos[:, None] * theta[None, :]
            return (jnp.cos(ang), jnp.sin(ang))

        def _rotate(t, cos, sin):
            te = t[..., 0::2]
            to = t[..., 1::2]
            re = te * cos + to * sin
            ro = -te * sin + to * cos
            return jnp.stack((re, ro), axis=-1).reshape(t.shape)
        b, m, d = x.shape
        q = jnp.einsum('bmd,ed->bme', x, w_q)
        k = jnp.einsum('bmd,ed->bme', x, w_k)
        v = jnp.einsum('bmd,ed->bme', x, w_v)
        cos, sin = _rope_cos_sin(m, d, x.dtype)
        q_rot = _rotate(q, cos, sin)
        k_rot = _rotate(k, cos, sin)
        scores = jnp.einsum('bqd,bkd->bqk', q_rot, k_rot) / jnp.sqrt(jnp.asarray(d, x.dtype))
        causal = jnp.tril(jnp.ones((m, m), dtype=bool))
        scores = jnp.where(causal[None], scores, jnp.asarray(-jnp.inf, scores.dtype))
        attn = jax.nn.softmax(scores, axis=-1)
        return jnp.einsum('bqk,bkd->bqd', attn, v)

    def _L0_xattn_ref(query, key, value, Wq, bq, Wk, bk, Wv, bv, Wc, bc):
        import jax, jax.numpy as jnp
        import numpy as np
        B, L, D_MODEL = (2, 512, 256)
        HEADS, DH, K = (8, 128, 64)
        DILATIONS = np.array([1, 1, 2, 2, 4, 4, 8, 8], dtype=np.int32)
        Lq = query.shape[-2]
        q = jnp.einsum('bld,hed->bhle', query, Wq) + bq[:, None, :]
        k = jnp.einsum('bld,hed->bhle', key, Wk) + bk[:, None, :]
        v = jnp.einsum('bld,hed->bhle', value, Wv) + bv[:, None, :]
        offsets = jnp.arange(K) - (K - 1) // 2
        dil = jnp.asarray(DILATIONS)
        idx = jnp.arange(Lq)[None, :, None] + offsets[None, None, :] * dil[:, None, None]
        valid = (idx >= 0) & (idx < Lq)
        idxc = jnp.clip(idx, 0, Lq - 1)
        gather = jax.vmap(lambda xh, ih: xh[:, ih], in_axes=(1, 0), out_axes=1)
        k_win = gather(k, idxc)
        v_win = gather(v, idxc)
        scores = jnp.einsum('bhld,bhlkd->bhlk', q, k_win)
        scores = jnp.where(valid[None], scores, jnp.asarray(-1000000000.0, scores.dtype))
        attn = jax.nn.softmax(scores, axis=-1)
        out = jnp.einsum('bhlk,bhlkd->bhld', attn, v_win)
        out = out.transpose(0, 2, 1, 3).reshape(out.shape[0], Lq, HEADS * DH)
        return out @ Wc.T + bc

    def _L0_ffn_ref(x, rw1, rb1, rw2, rb2, ew1, eb1, ew2, eb2):
        import jax, jax.numpy as jnp
        import numpy as np
        B, F, D, H, E, K = (4, 512, 256, 512, 8, 2)
        b, f, d = x.shape
        t = x.reshape(b * f, d)
        logits = jax.nn.silu(t @ rw1 + rb1) @ rw2 + rb2
        vals, idx = jax.lax.top_k(logits, K)
        rows = jnp.arange(t.shape[0])[:, None]
        masked = jnp.full_like(logits, -jnp.inf).at[rows, idx].set(vals)
        w = jax.nn.softmax(masked, axis=1)
        eh = jax.nn.silu(jnp.einsum('td,edh->teh', t, ew1) + eb1[None])
        eo = jnp.einsum('teh,ehd->ted', eh, ew2) + eb2[None]
        y = t + jnp.einsum('te,ted->td', w, eo)
        return y.reshape(b, f, d)
    x = x + _L0_attn_ref(_layernorm(x, axis=-1), L0_attn_w_q, L0_attn_w_k, L0_attn_w_v)
    x = x + _L0_xattn_ref(_layernorm(x, axis=-1), ctx_1024, ctx_1024, L0_xattn_Wq, L0_xattn_bq, L0_xattn_Wk, L0_xattn_bk, L0_xattn_Wv, L0_xattn_bv, L0_xattn_Wc, L0_xattn_bc)
    x = x + _L0_ffn_ref(_layernorm(x, axis=-1), L0_ffn_rw1, L0_ffn_rb1, L0_ffn_rw2, L0_ffn_rb2, L0_ffn_ew1, L0_ffn_eb1, L0_ffn_ew2, L0_ffn_eb2)
    return x

_drawn_inputs = setup_inputs


def setup_inputs(seed=0):
    import zlib

    import numpy as np

    out = dict(_drawn_inputs(seed))
    spreads = {'L0_xattn_bq': (0.0, 0.1),
     'L0_xattn_bk': (0.0, 0.8),
     'L0_xattn_bv': (0.0, 0.1),
     'L0_xattn_bc': (0.0, 0.1),
     'L0_ffn_rb1': (0.0, 0.1),
     'L0_ffn_rb2': (0.0, 0.1),
     'L0_ffn_eb1': (0.0, 0.386),
     'L0_ffn_eb2': (0.0, 0.1)}
    factors = {}
    for name, (base, spread) in spreads.items():
        noise = np.random.default_rng([zlib.crc32(name.encode()), seed]).standard_normal(out[name].shape)
        drawn = base * np.exp(spread * noise) if base else spread * noise
        out[name] = jnp.asarray(drawn.astype(out[name].dtype))
    for name, factor in factors.items():
        out[name] = (out[name] * factor).astype(out[name].dtype)
    return out
```

```python
from contextlib import ExitStack

import numpy as np

import concourse.bass as bass
from concourse import mybir

F32 = mybir.dt.float32
F16 = mybir.dt.float16
BF16 = mybir.dt.bfloat16
U32 = mybir.dt.uint32
ALU = mybir.AluOpType
ACT = mybir.ActivationFunctionType
AX = mybir.AxisListType.X

P = 128
B, L, D = 16, 128, 256
GB = 4
G = B // GB
TOK = GB * L
KC = D // P
H, DH = 8, 128
DILATIONS = (1, 1, 2, 2, 4, 4, 8, 8)
WIN = 64
E, HID = 8, 512
EPS = 1e-5
NEG = -1e30
UP = 256.0
DOWN = 1.0 / (UP * UP)
ATTN_SCALE = DOWN * DOWN / float(D) ** 0.5
ROW = 2 * D + 2 * E


def bc(ap, shape):
    return ap.to_broadcast(shape)


def attention_phase(nc, keep, dram, debug_out=None):
    (x, ctxt, w1a, w2a, wca, xbias, bcd, rw1, rb1, rw2, rb2, consts) = dram
    base, eidx, gate, rows = keep
    with ExitStack() as ctx:
        def sb(name, shape, dt=F32):
            return ctx.enter_context(nc.sbuf_tensor(name, shape, dt))

        def bank(name):
            return ctx.enter_context(nc.psum_tensor(name, [P, 512], F32))

        def sem(name):
            return ctx.enter_context(nc.semaphore(name))

        w1h, w1l = sb("w1h", [P, KC, 768], F16), sb("w1l", [P, KC, 768], F16)
        w2h, w2l = sb("w2h", [P, KC, 3072], F16), sb("w2l", [P, KC, 3072], F16)
        r1h, r1l = sb("r1h", [P, KC, D], F16), sb("r1l", [P, KC, D], F16)
        wc = sb("wc", [P, H, D])
        rw2s = sb("rw2s", [P, KC, E])
        rb1s, rb1half = sb("rb1s", [P, KC]), sb("rb1half", [P, KC])
        rb2s = sb("rb2s", [P, E])
        bias = sb("bias", [P, 3 * H])
        bcs = sb("bcs", [P, D])
        cst = sb("cst", [P, 2 * P + 5 * P + P + E])
        cosT = cst[:, 0:P]
        sinT = cst[:, P:2 * P]
        ident = cst[:, 7 * P:8 * P]
        iota8 = cst[:, 8 * P:8 * P + E]
        masks = sb("masks", [P, 5, P], BF16)
        identb = sb("identb", [P, P], BF16)
        identh = sb("identh", [P, P], F16)
        nhalf = sb("nhalf", [P, GB])
        xg, cg = sb("xg", [P, GB, D]), sb("cg", [P, GB, D])
        xn = sb("xn", [P, GB, D])
        nh, nl = sb("nh", [P, GB, D], F16), sb("nl", [P, GB, D], F16)
        ch, cl = sb("ch", [P, GB, D], F16), sb("cl", [P, GB, D], F16)
        xTh, xTl = sb("xTh", [P, KC, TOK], F16), sb("xTl", [P, KC, TOK], F16)
        cTh, cTl = sb("cTh", [P, KC, TOK], F16), sb("cTl", [P, KC, TOK], F16)
        stats, mv = sb("stats", [P, GB, 6]), sb("mv", [P, GB, 2])
        veps, rstd, rstd_up = sb("veps", [P, GB]), sb("rstd", [P, GB]), sb("rstd_up", [P, GB])
        rope = sb("rope", [P, 4, TOK])
        qr, kr = sb("qr", [P, KC, TOK]), sb("kr", [P, KC, TOK])
        v1 = sb("v1", [P, GB, D])
        p1, pT1 = sb("p1", [P, GB, P]), sb("pT1", [P, GB, P])
        mx1, nm1, sum1, inv1 = (sb(n, [P, GB]) for n in ("mx1", "nm1", "sum1", "inv1"))
        kT, qT = sb("kT", [P, H, TOK]), sb("qT", [P, H, TOK])
        v2 = sb("v2", [P, GB, H * DH])
        p2, pn2, pT2 = (sb(n, [P, 2, 4, P]) for n in ("p2", "pn2", "pT2"))
        mx2, nm2, sum2, inv2 = (sb(n, [P, 2, 4]) for n in ("mx2", "nm2", "sum2", "inv2"))
        oT = sb("oT", [P, 2, H, P])
        x1, x2 = sb("x1", [P, GB, D]), sb("x2", [P, GB, D])
        row = sb("row", [P, GB, ROW], F16)
        rTh, rTl = sb("rTh", [P, KC, TOK], F16), sb("rTl", [P, KC, TOK], F16)
        xb, th = rope[:, 0:2, :], rope[:, 2:4, :]
        lg, mx8 = sb("lg", [P, GB, E]), sb("mx8", [P, GB, E])
        ix8 = sb("ix8", [P, GB, E], U32)
        gd, ge, gs = sb("gd", [P, GB]), sb("ge", [P, GB]), sb("gs", [P, GB])
        g1, g2 = sb("g1", [P, GB]), sb("g2", [P, GB])
        ixf = sb("ixf", [P, GB, 2])
        m1, m2 = sb("m1", [P, GB, E]), sb("m2", [P, GB, E])

        w1f = kT[:, 0:3, :].rearrange("p a b -> p (a b)").rearrange("p (c n) -> p c n", c=KC)
        wkf = v2[:, 0:2, :]
        wvf = v2[:, 2:4, :]
        r1f = x2[:, 0:2, :]
        wqf = qT[:, 0:4, :].rearrange("p a b -> p (a b)").rearrange("p (c n) -> p c n", c=KC)

        tpA, tpB, pj0, pj1, sc0, sc1, ov, op = (
            bank(n) for n in ("tpA", "tpB", "pj0", "pj1", "sc0", "sc1", "ov", "op"))
        pj, sc = (pj0, pj1), (sc0, sc1)
        tpA_full, tpA_free = sem("tpA_full"), sem("tpA_free")
        tpB_full, tpB_free = sem("tpB_full"), sem("tpB_free")
        pj_full, pj_free = (sem("pj0_full"), sem("pj1_full")), (sem("pj0_free"), sem("pj1_free"))
        sc_full, sc_free = (sem("sc0_full"), sem("sc1_full")), (sem("sc0_free"), sem("sc1_free"))
        ov_full, ov_free = sem("ov_full"), sem("ov_free")
        op_full, op_free = sem("op_full"), sem("op_free")
        TPA, TPB, PJ, SC, OV, OP = 8, 7, 14, (7, 6), 12, 5

        const_in, w1_in, wk_in, wv_in, wq_in = (sem(n) for n in ("const_in", "w1_in", "wk_in", "wv_in", "wq_in"))
        wc_in, r_in, xg_in, cg_in = (sem(n) for n in ("wc_in", "r_in", "xg_in", "cg_in"))
        ready, nhalf_set = sem("ready"), sem("nhalf_set")
        w1_hi, w1_lo, w2_hi, w2_lo, r1_hi, r1_lo = (
            sem(n) for n in ("w1_hi", "w1_lo", "w2_hi", "w2_lo", "r1_hi", "r1_lo"))
        ln = {k: {s: sem(f"ln{k}_{s}") for s in ("stats", "aggr", "var", "pow", "rstd", "xn", "hi", "lo")}
              for k in (1, 2, 3)}
        c_hi, c_lo = sem("c_hi"), sem("c_lo")
        rope_add = sem("rope_add")
        max1, neg1, inv1_done, x1_bias = (
            sem(n) for n in ("max1", "neg1", "inv1_done", "x1_bias"))
        max2, neg2, inv2_done, norm2, x2_done = (
            sem(n) for n in ("max2", "neg2", "inv2_done", "norm2", "x2_done"))
        base_done, r_tanh, r_xb, r_hid = (sem(n) for n in ("base_done", "r_tanh", "r_xb", "r_hid"))
        lg_done, top8, top8i, gdiff, gexp, gsum, gate1, gate2, ixf_done, hot, wrow, wrow2, row_out = (
            sem(n) for n in ("lg_done", "top8", "top8i", "gdiff", "gexp", "gsum", "gate1", "gate2",
                             "ixf_done", "hot", "wrow", "wrow2", "row_out"))
        kept, dbg, waited = sem("kept"), sem("dbg"), sem("waited")

        x_t = x.rearrange("(g b) p d -> g p b d", b=GB)
        c_t = ctxt.rearrange("(g b) p d -> g p b d", b=GB)
        rows_t = rows.rearrange("(g b p) w -> g p b w", b=GB, p=P)

        block = ctx.enter_context(nc.Block())

        @block.sync
        def _(sp):
            sp.sem_inc(row_out, 16)
            sp.dma_start(xg[:], x_t[0]).then_inc(xg_in, 16)
            sp.dma_start(w1f, w1a).then_inc(w1_in, 16)
            sp.dma_start(cst[:], consts).then_inc(const_in, 16)
            sp.dma_start(bias[:], xbias).then_inc(const_in, 16)
            sp.dma_start(cg[:], c_t[0]).then_inc(cg_in, 16)
            sp.dma_start(wkf, w2a[:, :, 0:1024]).then_inc(wk_in, 16)
            sp.dma_start(wvf, w2a[:, :, 1024:2048]).then_inc(wv_in, 16)
            sp.dma_start(wqf, w2a[:, :, 2048:3072]).then_inc(wq_in, 16)
            sp.dma_start(wc[:], wca).then_inc(wc_in, 16)
            sp.dma_start(r1f, rw1).then_inc(r_in, 16)
            sp.dma_start(rw2s[:], rw2).then_inc(r_in, 16)
            sp.dma_start(rb1s[:], rb1).then_inc(r_in, 16)
            sp.dma_start(rb2s[:], rb2.rearrange("(a n) -> a n", a=1).broadcast_to([P, E])).then_inc(r_in, 16)
            sp.dma_start(bcs[:], bcd.rearrange("(a n) -> a n", a=1).broadcast_to([P, D])).then_inc(r_in, 16)

            with sp.Fori(1, G) as g:
                sp.wait_ge(c_lo, g)
                sp.dma_start(cg[:], c_t[g]).then_inc(cg_in, 16)
                sp.wait_ge(ov_free, OV * (g - 1) + 4)
                sp.dma_start(xg[:], x_t[g]).then_inc(xg_in, 16)
                sp.wait_ge(wrow2, g)
                sp.dma_start(rows_t[g - 1], row[:].bitcast(U32)).then_inc(row_out, 16)
            sp.wait_ge(wrow2, G)
            sp.dma_start(rows_t[G - 1], row[:].bitcast(U32)).then_inc(row_out, 16)
            sp.wait_ge(row_out, 16 * G + 16)
            if debug_out is not None:
                sp.wait_ge(base_done, G)
                sp.dma_start(debug_out.rearrange("b p d -> p b d"), base[:]).then_inc(dbg, 16)
                sp.wait_ge(dbg, 16)

        @block.gpsimd
        def _(pool):
            pool.memset(nhalf[:], -0.5).then_inc(nhalf_set, 1)
            pool.wait_ge(nhalf_set, 1)

            def power(k, n):
                pool.wait_ge(ln[k]["var"], n + 1)
                pool.tensor_tensor(rstd[:], veps[:], nhalf[:], ALU.pow).then_inc(ln[k]["pow"], 1)

            def front(g, after=True):
                for i, dst in enumerate((qr, kr)):
                    pool.wait_ge(pj_free[0], PJ * g + i + 1)
                    pool.wait_ge(pj_free[1], PJ * g + i + 1)
                    if after:
                        pool.wait_ge(sc_full[0], SC[0] * (g - 1) + 1)
                    pool.tensor_tensor(dst[:, 0, :], rope[:, 0, :], rope[:, 2, :], ALU.add)
                    pool.tensor_tensor(dst[:, 1, :], rope[:, 3, :], rope[:, 1, :], ALU.subtract)\
                        .then_inc(rope_add, 1)

            def back(g, more):
                power(2, g)
                pool.wait_ge(ln[2]["xn"], g + 1)
                pool.tensor_tensor(x1[:], x1[:], bcs[:].unsqueeze(1).to_broadcast([P, GB, D]), ALU.add)\
                    .then_inc(x1_bias, 1)
                for n in range(8):
                    if n == 4 and more:
                        power(1, g + 1)
                    if n >= 2:
                        pool.wait_ge((tpA_full, tpB_full)[n % 2],
                                     (TPA * g + 4, TPB * g + 3)[n % 2] + (n - 2) // 2 + 1)
                    pool.wait_ge(inv2_done, 8 * g + n + 1)
                    pool.tensor_tensor(pn2[:, n % 2], p2[:, n % 2],
                                       inv2[:, n % 2, :].unsqueeze(2).to_broadcast([P, 4, P]), ALU.mult)\
                        .then_inc(norm2, 1)
                power(3, g)

            power(1, 0)
            front(0, after=False)
            with pool.Fori(0, G - 1) as g:
                back(g, True)
                front(g + 1)
            back(G - 1, False)

        @block.scalar
        def _(act):
            copy = lambda out, in_, scale=1.0: act.activation(out, in_, ACT.Copy, scale=scale)

            def high(k, n, dst):
                act.wait_ge(ln[k]["xn"], n + 1)
                copy(dst, xn[:]).then_inc(ln[k]["hi"], 1)

            def early(g):
                act.wait_ge(tpA_full, TPA * (g - 1) + 4)
                high(1, g, nh[:])
                act.wait_ge(cg_in, 16 * (g + 1))
                copy(ch[:], cg[:], UP).then_inc(c_hi, 1)

            def front(g, after=True):
                act.wait_ge(tpA_full, TPA * g + 1)
                if after:
                    act.wait_ge(pj_full[1], PJ * g)
                copy(xTh[:], tpA[:].bitcast(F16)).then_inc(tpA_free, 1)
                for i in range(2):
                    act.wait_ge(ov_full, OV * g + i + 1)
                    copy(v1[:, 2 * i:2 * i + 2, :], ov[:], DOWN).then_inc(ov_free, 1)
                act.wait_ge(tpA_full, TPA * g + 2)
                copy(cTh[:], tpA[:].bitcast(F16)).then_inc(tpA_free, 1)

            def project(g, kind):
                for j in range(0, 8, 2):
                    if kind == 1 and j == 4:
                        high(2, g, nh[:])
                    use = PJ * g + 2 + 4 * kind + j // 2
                    act.wait_ge(pj_full[0], use + 1)
                    if kind == 0:
                        out, b = kT[:, j, :], bias[:, H + j:H + j + 1]
                    elif kind == 2:
                        out, b = qT[:, j, :], bias[:, j:j + 1]
                    if kind == 1:
                        copy(v2[:, j // 2, 0:512], pj0[:], DOWN).then_inc(pj_free[0], 1)
                    else:
                        act.activation(out, pj0[:], ACT.Identity, bias=b, scale=DOWN).then_inc(pj_free[0], 1)

            def back(g, more):
                act.wait_ge(neg1, g + 1)
                for b in range(GB):
                    last = act.activation(p1[:, b, :], sc0[:, b * P:(b + 1) * P], ACT.Exp,
                                          bias=nm1[:, b:b + 1], scale=ATTN_SCALE, accum_out=sum1[:, b:b + 1])
                last.then_inc(sc_free[0], 1)
                project(g, 0)
                act.wait_ge(tpA_full, TPA * g + 3)
                copy(pT1[:], tpA[:]).then_inc(tpA_free, 1)
                project(g, 1)
                act.wait_ge(tpA_full, TPA * g + 4)
                copy(xTh[:], tpA[:].bitcast(F16)).then_inc(tpA_free, 1)
                project(g, 2)
                for n in range(8):
                    if n == 5 and more:
                        early(g + 1)
                    s = n % 2
                    if n >= 2:
                        act.wait_ge(norm2, 8 * g + n - 1)
                    act.wait_ge(neg2, 8 * g + n + 1)
                    for i in range(4):
                        last = act.activation(p2[:, s, i, :], sc[s][:, i * P:(i + 1) * P], ACT.Exp,
                                              bias=nm2[:, s, i:i + 1], scale=1.0,
                                              accum_out=sum2[:, s, i:i + 1])
                    last.then_inc(sc_free[s], 1)
                act.wait_ge(row_out, 16 * g + 16)
                high(3, g, row[:, :, 0:D])

            def router(g, fronts):
                act.wait_ge(rope_add, 2 * fronts)
                act.wait_ge(sc_full[0], SC[0] * g + 6)
                copy(rTh[:], sc0[:].bitcast(F16)).then_inc(sc_free[0], 1)
                for m in range(KC):
                    act.wait_ge(sc_full[m], SC[m] * g + (7, 6)[m])
                    act.activation(th[:, m, :], sc[m][:], ACT.Tanh, bias=rb1half[:, m:m + 1],
                                   scale=0.5 * DOWN).then_inc(r_tanh, 1)
                act.wait_ge(gdiff, g + 1)
                act.activation(ge[:], gd[:], ACT.Exp).then_inc(gexp, 1)

            act.wait_ge(w1_in, 16)
            copy(w1h[:], w1f, UP).then_inc(w1_hi, 1)
            high(1, 0, nh[:])
            act.wait_ge(cg_in, 16)
            copy(ch[:], cg[:], UP).then_inc(c_hi, 1)
            front(0, after=False)
            for i, (q, src) in enumerate(((wk_in, wkf), (wv_in, wvf), (wq_in, wqf))):
                act.wait_ge(q, 16)
                copy(w2h[:, :, 1024 * i:1024 * i + 1024], src, UP).then_inc(w2_hi, 1)
            act.wait_ge(r_in, 80)
            copy(r1h[:], r1f, UP).then_inc(r1_hi, 1)
            copy(rb1half[:], rb1s[:], 0.5).then_inc(r1_hi, 1)
            act.wait_ge(r1_hi, 2)
            with act.Fori(0, G - 1) as g:
                back(g, True)
                front(g + 1)
                router(g, g + 2)
            back(G - 1, False)
            router(G - 1, G)

        @block.vector
        def _(dve):
            def norm(k, n, src):
                for b in range(GB):
                    last = dve.bn_stats(stats[:, b, :], src[:, b, :])
                last.then_inc(ln[k]["stats"], 1)
                dve.wait_ge(ln[k]["stats"], n + 1)
                dve.sem_inc(waited, 1)
                for b in range(GB):
                    last = dve.bn_aggr(mv[:, b, :], stats[:, b, :])
                last.then_inc(ln[k]["aggr"], 1)
                dve.wait_ge(ln[k]["aggr"], n + 1)
                dve.tensor_scalar(veps[:], mv[:, :, 1], EPS, None, ALU.add).then_inc(ln[k]["var"], 1)

            def normed(k, n, src):
                dve.wait_ge(ln[k]["pow"], n + 1)
                dve.tensor_scalar(rstd_up[:], rstd[:], UP, None, ALU.mult).then_inc(ln[k]["rstd"], 1)
                dve.wait_ge(ln[k]["rstd"], n + 1)
                for b in range(GB):
                    last = dve.tensor_scalar(xn[:, b, :], src[:, b, :], mv[:, b, 0:1], rstd_up[:, b:b + 1],
                                             ALU.subtract, ALU.mult)
                last.then_inc(ln[k]["xn"], 1)

            def low(k, n, hi, dst):
                dve.wait_ge(ln[k]["xn"], n + 1)
                dve.wait_ge(ln[k]["hi"], n + 1)
                dve.tensor_tensor(dst, xn[:], hi, ALU.subtract).then_inc(ln[k]["lo"], 1)

            def early(g, part, after=True):
                if part == 0:
                    dve.wait_ge(xg_in, 16 * (g + 1))
                    norm(1, g, xg)
                elif part == 1:
                    normed(1, g, xg)
                else:
                    if after:
                        dve.wait_ge(tpB_full, TPB * (g - 1) + 3)
                    low(1, g, nh[:], nl[:])
                    dve.wait_ge(c_hi, g + 1)
                    dve.scalar_tensor_tensor(out=cl[:], in0=cg[:], scalar=UP, in1=ch[:], op0=ALU.mult,
                                             op1=ALU.subtract).then_inc(c_lo, 1)

            def front(g, after=True):
                dve.wait_ge(tpB_full, TPB * g + 1)
                if after:
                    dve.wait_ge(pj_full[1], PJ * g)
                dve.tensor_copy(xTl[:], tpB[:].bitcast(F16)).then_inc(tpB_free, 1)
                cosb = cosT.unsqueeze(1).to_broadcast([P, GB, P])
                sinb = sinT.unsqueeze(1).to_broadcast([P, GB, P])
                for i in range(2):
                    if after or i:
                        dve.wait_ge(rope_add, 2 * g + i)
                    for half in range(2):
                        dve.wait_ge(pj_full[half], PJ * g + i + 1)
                        src = pj[half][:].rearrange("p (b t) -> p b t", b=GB)
                        dve.tensor_tensor(rope[:, 3 * half].rearrange("p (b t) -> p b t", b=GB), src, cosb, ALU.mult)
                        last = dve.tensor_tensor(rope[:, 1 + half].rearrange("p (b t) -> p b t", b=GB),
                                                 src, sinb, ALU.mult)
                        last.then_inc(pj_free[half], 1)
                dve.wait_ge(tpB_full, TPB * g + 2)
                dve.tensor_copy(cTl[:], tpB[:].bitcast(F16)).then_inc(tpB_free, 1)

            def project(g, kind, between):
                for j in range(1, 8, 2):
                    use = PJ * g + 2 + 4 * kind + j // 2
                    dve.wait_ge(pj_full[1], use + 1)
                    if kind == 0:
                        dve.tensor_scalar(kT[:, j, :], pj1[:], DOWN, bias[:, H + j:H + j + 1],
                                          ALU.mult, ALU.add).then_inc(pj_free[1], 1)
                    elif kind == 2:
                        dve.tensor_scalar(qT[:, j, :], pj1[:], DOWN, bias[:, j:j + 1],
                                          ALU.mult, ALU.add).then_inc(pj_free[1], 1)
                    else:
                        dve.tensor_scalar(v2[:, j // 2, 512:1024], pj1[:], DOWN, None,
                                          ALU.mult).then_inc(pj_free[1], 1)
                    between(j // 2)

            def back(g, more):
                dve.wait_ge(sc_full[0], SC[0] * g + 1)
                dve.tensor_reduce(mx1[:], sc0[:].rearrange("p (b t) -> p b t", b=GB), AX, ALU.max).then_inc(max1, 1)
                dve.wait_ge(max1, g + 1)
                dve.tensor_scalar(nm1[:], mx1[:], -ATTN_SCALE, None, ALU.mult).then_inc(neg1, 1)

                def sums(i):
                    if i == 1:
                        dve.wait_ge(sc_free[0], SC[0] * g + 1)
                        dve.reciprocal(inv1[:], sum1[:]).then_inc(inv1_done, 1)

                project(g, 0, sums)
                dve.wait_ge(inv1_done, g + 1)
                for i in range(2):
                    dve.wait_ge(ov_full, OV * g + 2 + i + 1)
                    for b in (2 * i, 2 * i + 1):
                        last = dve.scalar_tensor_tensor(out=x1[:, b, :], in0=ov[:, (b % 2) * D:(b % 2 + 1) * D],
                                                        scalar=inv1[:, b:b + 1], in1=xg[:, b, :],
                                                        op0=ALU.mult, op1=ALU.add)
                    last.then_inc(ov_free, 1)
                dve.wait_ge(ov_free, OV * g + 4)

                def second_norm(i):
                    if i == 0:
                        norm(2, g, x1)
                    elif i == 1:
                        normed(2, g, x1)
                    elif i == 3:
                        low(2, g, nh[:], nl[:])

                project(g, 1, second_norm)
                dve.wait_ge(tpB_full, TPB * g + 3)
                dve.tensor_copy(xTl[:], tpB[:].bitcast(F16)).then_inc(tpB_free, 1)
                project(g, 2, lambda i: None)

                for n in range(8 + 5):
                    if n < 8:
                        s = n % 2
                        dve.wait_ge(sc_full[s], SC[s] * g + (1 - s) + n // 2 + 1)
                        dve.tensor_reduce(mx2[:, s, :], sc[s][:].rearrange("p (b t) -> p b t", b=4), AX, ALU.max)\
                            .then_inc(max2, 1)
                        dve.wait_ge(max2, 8 * g + n + 1)
                        dve.tensor_scalar(nm2[:, s, :], mx2[:, s, :], -1.0, None, ALU.mult).then_inc(neg2, 1)
                    if 1 <= n <= 8:
                        s = (n - 1) % 2
                        dve.wait_ge(sc_free[s], SC[s] * g + (1 - s) + (n - 1) // 2 + 1)
                        if n >= 3:
                            dve.wait_ge(norm2, 8 * g + n - 2)
                        dve.reciprocal(inv2[:, s, :], sum2[:, s, :]).then_inc(inv2_done, 1)
                    if 2 <= n < 10:
                        m = n - 2
                        full, free, src = ((tpA_full, tpA_free, tpA), (tpB_full, tpB_free, tpB))[m % 2]
                        dve.wait_ge(full, ((TPA * g + 4), (TPB * g + 3))[m % 2] + m // 2 + 1)
                        if m >= 2:
                            dve.wait_ge(ov_full, OV * g + 4 + m - 1)
                        dve.tensor_copy(pT2[:, m % 2].rearrange("p a b -> p (a b)"), src[:]).then_inc(free, 1)
                    if 3 <= n < 11:
                        m = n - 3
                        hh = 4 * (m % 2)
                        if m >= 4:
                            dve.wait_ge(op_full, OP * g + m // 2 - 1)
                        dve.wait_ge(ov_full, OV * g + 4 + m + 1)
                        dve.tensor_tensor(oT[:, (m // 2) % 2, hh:hh + 4, :],
                                          ov[:].rearrange("p (b t) -> p b t", b=4),
                                          bias[:, 2 * H + hh:2 * H + hh + 4].unsqueeze(2).to_broadcast([P, 4, P]),
                                          ALU.add).then_inc(ov_free, 1)
                    if n >= 6 and n % 2 == 0:
                        b = (n - 6) // 2
                        if b == 0:
                            dve.wait_ge(x1_bias, g + 1)
                        dve.wait_ge(op_full, OP * g + b + 1)
                        dve.tensor_tensor(x2[:, b, :], op[:, 0:D], x1[:, b, :], ALU.add).then_inc(op_free, 1)
                    if more and n in (3, 5, 8):
                        early(g + 1, (3, 5, 8).index(n))
                dve.wait_ge(op_free, OP * g + 4)
                norm(3, g, x2)
                normed(3, g, x2)
                dve.wait_ge(ln[3]["xn"], g + 1)
                dve.scalar_tensor_tensor(out=base[:, bass.ds(g * GB, GB), :], in0=xn[:], scalar=1.0 / UP, in1=x2[:],
                                         op0=ALU.mult, op1=ALU.add).then_inc(base_done, 1)
                low(3, g, row[:, :, 0:D], row[:, :, D:2 * D])

            def router(g):
                dve.wait_ge(sc_full[1], SC[1] * g + 5)
                dve.tensor_copy(rTl[:], sc1[:].bitcast(F16)).then_inc(sc_free[1], 1)
                for m in range(KC):
                    dve.wait_ge(r_tanh, KC * g + m + 1)
                    dve.tensor_scalar(xb[:, m, :], sc[m][:], DOWN, rb1s[:, m:m + 1], ALU.mult, ALU.add)\
                        .then_inc(sc_free[m], 1)
                    dve.wait_ge(sc_free[m], SC[m] * g + (7, 6)[m])
                    dve.scalar_tensor_tensor(out=xb[:, m, :], in0=th[:, m, :], scalar=1.0, in1=xb[:, m, :],
                                             op0=ALU.add, op1=ALU.mult).then_inc(r_hid, 1)
                dve.wait_ge(op_full, OP * g + 5)
                dve.scalar_tensor_tensor(out=lg[:], in0=op[:, 0:GB * E].rearrange("p (b e) -> p b e", b=GB),
                                         scalar=0.5, in1=rb2s[:].unsqueeze(1).to_broadcast([P, GB, E]),
                                         op0=ALU.mult, op1=ALU.add).then_inc(op_free, 1)
                dve.wait_ge(op_free, OP * g + 5)
                dve.sem_inc(waited, 1)
                for b in range(GB):
                    last = dve.max(mx8[:, b, :], lg[:, b, :])
                last.then_inc(top8, 1)
                dve.wait_ge(top8, g + 1)
                dve.sem_inc(waited, 1)
                for b in range(GB):
                    last = dve.max_index(ix8[:, b, :], mx8[:, b, :], lg[:, b, :])
                last.then_inc(top8i, 1)
                dve.tensor_tensor(gd[:], mx8[:, :, 1], mx8[:, :, 0], ALU.subtract).then_inc(gdiff, 1)
                dve.wait_ge(gexp, g + 1)
                dve.tensor_scalar(gs[:], ge[:], 1.0, None, ALU.add).then_inc(gsum, 1)
                dve.wait_ge(gsum, g + 1)
                dve.reciprocal(g1[:], gs[:]).then_inc(gate1, 1)
                dve.wait_ge(gate1, g + 1)
                dve.tensor_tensor(g2[:], ge[:], g1[:], ALU.mult).then_inc(gate2, 1)
                dve.wait_ge(top8i, g + 1)
                dve.tensor_copy(ixf[:], ix8[:, :, 0:2]).then_inc(ixf_done, 1)
                dve.wait_ge(ixf_done, g + 1)
                dve.tensor_copy(eidx[:, bass.ds(g * GB, GB), :], ixf[:]).then_inc(kept, 1)
                iob = iota8.unsqueeze(1).to_broadcast([P, GB, E])
                dve.tensor_tensor(m1[:], iob, ixf[:, :, 0:1].to_broadcast([P, GB, E]), ALU.is_equal)
                dve.tensor_tensor(m2[:], iob, ixf[:, :, 1:2].to_broadcast([P, GB, E]), ALU.is_equal).then_inc(hot, 1)
                dve.wait_ge(hot, g + 1)
                dve.wait_ge(gate2, g + 1)
                wcols = row[:, :, 2 * D:ROW].bitcast(F32)
                dve.tensor_tensor(m1[:], m1[:], g1[:].unsqueeze(2).to_broadcast([P, GB, E]), ALU.mult)
                dve.tensor_tensor(m2[:], m2[:], g2[:].unsqueeze(2).to_broadcast([P, GB, E]), ALU.mult)\
                    .then_inc(wrow, 1)
                dve.wait_ge(wrow, g + 1)
                dve.tensor_tensor(wcols, m1[:], m2[:], ALU.add).then_inc(wrow2, 1)

            dve.wait_ge(const_in, 32)
            dve.wait_ge(xg_in, 16)
            norm(1, 0, xg)
            dve.tensor_copy(identh[:], ident).then_inc(ready, 1)
            normed(1, 0, xg)
            dve.wait_ge(w1_hi, 1)
            dve.scalar_tensor_tensor(out=w1l[:], in0=w1f, scalar=UP, in1=w1h[:], op0=ALU.mult,
                                     op1=ALU.subtract).then_inc(w1_lo, 1)
            early(0, 2, after=False)
            front(0, after=False)
            dve.tensor_copy(identb[:], ident)
            dve.tensor_copy(masks[:], cst[:, 2 * P:7 * P].rearrange("p (m k) -> p m k", m=5)).then_inc(ready, 1)
            for i, src in enumerate((wkf, wvf, wqf)):
                dve.wait_ge(w2_hi, i + 1)
                dve.scalar_tensor_tensor(out=w2l[:, :, 1024 * i:1024 * i + 1024], in0=src, scalar=UP,
                                         in1=w2h[:, :, 1024 * i:1024 * i + 1024], op0=ALU.mult,
                                         op1=ALU.subtract).then_inc(w2_lo, 1)
            dve.wait_ge(r1_hi, 1)
            dve.scalar_tensor_tensor(out=r1l[:], in0=r1f, scalar=UP, in1=r1h[:], op0=ALU.mult,
                                     op1=ALU.subtract).then_inc(r1_lo, 1)
            with dve.Fori(0, G - 1) as g:
                back(g, True)
                front(g + 1)
                router(g)
            back(G - 1, False)
            router(G - 1)

        @block.tensor
        def _(pe):
            def transposes(bankA, bankB, hi, lo, fullA, fullB):
                for dst, src, full in ((bankA, hi, fullA), (bankB, lo, fullB)):
                    view = dst[:].bitcast(F16)
                    for c in range(KC):
                        for b in range(GB):
                            last = pe.transpose(view[:, c * TOK + b * P:c * TOK + (b + 1) * P],
                                                src(b, c), identh[:])
                    last.then_inc(full, 1)

            def three(out, whi, wlo, xhi, xlo):
                terms = [(c, w, v) for c in range(KC) for w, v in ((whi, xhi), (whi, xlo), (wlo, xhi))]
                for i, (c, w, v) in enumerate(terms):
                    last = pe.matmul(out, w(c), v(c), start=(i == 0), stop=(i == len(terms) - 1))
                return last

            def front(g, after=True):
                pe.wait_ge(ln[1]["hi"], g + 1)
                pe.wait_ge(ln[1]["lo"], g + 1)
                if after:
                    pe.wait_ge(tpA_free, TPA * g)
                    pe.wait_ge(tpB_free, TPB * g)
                transposes(tpA, tpB, lambda b, c: nh[:, b, c * P:(c + 1) * P],
                           lambda b, c: nl[:, b, c * P:(c + 1) * P], tpA_full, tpB_full)
                pe.wait_ge(tpA_free, TPA * g + 1)
                pe.wait_ge(tpB_free, TPB * g + 1)
                for i in range(4):
                    if after or i >= 2:
                        pe.wait_ge(pj_free[i % 2], PJ * g + i // 2)
                    three(pj[i % 2][:], lambda c: w1h[:, c, i * P:(i + 1) * P], lambda c: w1l[:, c, i * P:(i + 1) * P],
                          lambda c: xTh[:, c, :], lambda c: xTl[:, c, :]).then_inc(pj_full[i % 2], 1)
                for i in range(2):
                    if after or i:
                        pe.wait_ge(ov_free, OV * g + i)
                    for b in (2 * i, 2 * i + 1):
                        last = three(ov[:, (b % 2) * D:(b % 2 + 1) * D],
                                     lambda c: xTh[:, c, b * P:(b + 1) * P], lambda c: xTl[:, c, b * P:(b + 1) * P],
                                     lambda c: w1h[:, c, 512:768], lambda c: w1l[:, c, 512:768])
                    last.then_inc(ov_full, 1)
                pe.wait_ge(c_hi, g + 1)
                pe.wait_ge(c_lo, g + 1)
                transposes(tpA, tpB, lambda b, c: ch[:, b, c * P:(c + 1) * P],
                           lambda b, c: cl[:, b, c * P:(c + 1) * P], tpA_full, tpB_full)

            def project(g, kind):
                for j in range(8):
                    pe.wait_ge(pj_free[j % 2], PJ * g + 2 + 4 * kind + j // 2)
                    if kind == 1:
                        b, n0 = j // 2, 1024 + 512 * (j % 2)
                        last = three(pj[j % 2][:],
                                     lambda c: cTh[:, c, b * P:(b + 1) * P], lambda c: cTl[:, c, b * P:(b + 1) * P],
                                     lambda c: w2h[:, c, n0:n0 + 512], lambda c: w2l[:, c, n0:n0 + 512])
                    else:
                        n0 = 1024 * kind + P * j
                        src = (cTh, cTl) if kind == 0 else (xTh, xTl)
                        last = three(pj[j % 2][:],
                                     lambda c: w2h[:, c, n0:n0 + P], lambda c: w2l[:, c, n0:n0 + P],
                                     lambda c: src[0][:, c, :], lambda c: src[1][:, c, :])
                    last.then_inc(pj_full[j % 2], 1)

            def back(g):
                pe.wait_ge(rope_add, 2 * g + 2)
                pe.matmul(sc0[:], identb[:], masks[:, 0:1, :].to_broadcast([P, 4, P]), start=True, stop=True,
                          skip_group_check=True)
                for b in range(GB):
                    s = slice(b * P, (b + 1) * P)
                    for c in range(KC):
                        last = pe.matmul(sc0[:, s], qr[:, c, s], kr[:, c, s], start=False,
                                         stop=(c == KC - 1), skip_group_check=True)
                last.then_inc(sc_full[0], 1)
                pe.wait_ge(tpA_free, TPA * g + 2)
                pe.wait_ge(tpB_free, TPB * g + 2)
                project(g, 0)
                pe.wait_ge(sc_free[0], SC[0] * g + 1)
                for b in range(GB):
                    last = pe.transpose(tpA[:, b * P:(b + 1) * P], p1[:, b, :], ident)
                last.then_inc(tpA_full, 1)
                pe.wait_ge(tpA_free, TPA * g + 3)
                for i in range(2):
                    pe.wait_ge(ov_free, OV * g + 2 + i)
                    for b in (2 * i, 2 * i + 1):
                        last = pe.matmul(ov[:, (b % 2) * D:(b % 2 + 1) * D], pT1[:, b, :], v1[:, b, :],
                                         start=True, stop=True)
                    last.then_inc(ov_full, 1)
                project(g, 1)
                pe.wait_ge(ln[2]["hi"], g + 1)
                pe.wait_ge(ln[2]["lo"], g + 1)
                transposes(tpA, tpB, lambda b, c: nh[:, b, c * P:(c + 1) * P],
                           lambda b, c: nl[:, b, c * P:(c + 1) * P], tpA_full, tpB_full)
                pe.wait_ge(tpA_free, TPA * g + 4)
                pe.wait_ge(tpB_free, TPB * g + 3)
                project(g, 2)
                pe.wait_ge(pj_free[0], PJ * (g + 1))
                pe.wait_ge(pj_free[1], PJ * (g + 1))
                for n in range(8 + 4):
                    if n < 8:
                        s, b, h0 = n % 2, n // 2, 4 * (n % 2)
                        t = slice(b * P, (b + 1) * P)
                        if n != 1:
                            pe.wait_ge(sc_free[s], SC[s] * g + (1 - s) + n // 2)
                        pe.matmul(sc[s][:], identb[:],
                                  masks[:, 1 + 2 * (n % 2):3 + 2 * (n % 2), :].unsqueeze(2).to_broadcast([P, 2, 2, P]),
                                  start=True, stop=True, skip_group_check=True)
                        for i in range(4):
                            last = pe.matmul(sc[s][:, i * P:(i + 1) * P], qT[:, h0 + i, t], kT[:, h0 + i, t],
                                             start=False, stop=True, skip_group_check=True)
                        last.then_inc(sc_full[s], 1)
                    if 2 <= n < 10:
                        m = n - 2
                        dst, full, free, use = ((tpA, tpA_full, tpA_free, TPA * g + 4),
                                                (tpB, tpB_full, tpB_free, TPB * g + 3))[m % 2]
                        pe.wait_ge(norm2, 8 * g + m + 1)
                        pe.wait_ge(free, use + m // 2)
                        for i in range(4):
                            last = pe.transpose(dst[:, i * P:(i + 1) * P], pn2[:, m % 2, i, :], ident)
                        last.then_inc(full, 1)
                    if 3 <= n < 11:
                        m = n - 3
                        b, h0 = m // 2, 4 * (m % 2)
                        free, use = ((tpA_free, TPA * g + 4), (tpB_free, TPB * g + 3))[m % 2]
                        pe.wait_ge(free, use + m // 2 + 1)
                        pe.wait_ge(ov_free, OV * g + 4 + m)
                        for i in range(4):
                            h = h0 + i
                            last = pe.matmul(ov[:, i * P:(i + 1) * P], v2[:, b, h * DH:(h + 1) * DH],
                                             pT2[:, m % 2, i, :], start=True, stop=True)
                        last.then_inc(ov_full, 1)
                    if n >= 5 and n % 2 == 1:
                        b = (n - 5) // 2
                        pe.wait_ge(ov_free, OV * g + 4 + 2 * b + 2)
                        if b > 0:
                            pe.wait_ge(op_free, OP * g + b)
                        for h in range(H):
                            last = pe.matmul(op[:, 0:D], oT[:, b % 2, h, :], wc[:, h, :],
                                             start=(h == 0), stop=(h == H - 1))
                        last.then_inc(op_full, 1)

            def router(g):
                pe.wait_ge(ln[3]["hi"], g + 1)
                pe.wait_ge(ln[3]["lo"], g + 1)
                pe.wait_ge(sc_free[0], SC[0] * g + 5)
                pe.wait_ge(sc_free[1], SC[1] * g + 4)
                transposes(sc0, sc1, lambda b, c: row[:, b, c * P:(c + 1) * P],
                           lambda b, c: row[:, b, D + c * P:D + (c + 1) * P], sc_full[0], sc_full[1])
                pe.wait_ge(sc_free[0], SC[0] * g + 6)
                pe.wait_ge(sc_free[1], SC[1] * g + 5)
                for m in range(KC):
                    three(sc[m][:], lambda c: r1h[:, c, m * P:(m + 1) * P], lambda c: r1l[:, c, m * P:(m + 1) * P],
                          lambda c: rTh[:, c, :], lambda c: rTl[:, c, :]).then_inc(sc_full[m], 1)
                pe.wait_ge(r_hid, KC * (g + 1))
                pe.wait_ge(op_free, OP * g + 4)
                for b in range(GB):
                    for m in range(KC):
                        last = pe.matmul(op[:, b * E:(b + 1) * E], xb[:, m, b * P:(b + 1) * P], rw2s[:, m, :],
                                         start=(m == 0), stop=(m == KC - 1))
                last.then_inc(op_full, 1)

            pe.wait_ge(ready, 1)
            pe.wait_ge(w1_hi, 1)
            pe.wait_ge(w1_lo, 1)
            front(0, after=False)
            pe.wait_ge(ready, 2)
            pe.wait_ge(w2_hi, 3)
            pe.wait_ge(w2_lo, 3)
            pe.wait_ge(wc_in, 16)
            pe.wait_ge(r_in, 80)
            pe.wait_ge(r1_hi, 2)
            pe.wait_ge(r1_lo, 1)
            with pe.Fori(0, G - 1) as g:
                back(g)
                front(g + 1)
                router(g)
            back(G - 1)
            router(G - 1)


SLOTS = 3
TILES = (B * L * 2 + E * (P - 1)) // P
SKIP = 8192
MC = HID // P
RW = ROW // 2


def expert_phase(nc, keep, dram, out):
    (ew1, eb1, ew2, eb2, disp) = dram
    base, eidx, rows, picked = keep
    with ExitStack() as ctx:
        def sb(name, shape, dt=F32):
            return ctx.enter_context(nc.sbuf_tensor(name, shape, dt))

        def bank(name):
            return ctx.enter_context(nc.psum_tensor(name, [P, 512], F32))

        def sem(name):
            return ctx.enter_context(nc.semaphore(name))

        up_f = sb("up_f", [P, E, KC * HID])
        up_h, up_l = sb("up_h", [P, E, KC, HID], F16), sb("up_l", [P, E, KC, HID], F16)
        down = sb("down", [P, E, MC, D])
        b1 = sb("b1", [P, E * MC])
        b2f, b2h, b2l = sb("b2f", [2, E * D]), sb("b2h", [2, E * D], F16), sb("b2l", [2, E * D], F16)
        ones2 = sb("ones2", [2, P], F16)
        dc = sb("dc", [P, P + P + TILES + B + E * E + B + E + P])
        c0 = 0
        cols = []
        for n in (P, P, TILES, B, E * E, B, E, P):
            cols.append(dc[:, c0:c0 + n])
            c0 += n
        before, iota_p, iota_t, steps, less, token, iota8, ident = cols
        hot = sb("hot", [P, 2, B, E])
        both = sb("both", [P, B, E], F16)
        beforeh, onesh, identh = sb("beforeh", [P, P], F16), sb("onesh", [P, P], F16), sb("identh2", [P, P], F16)
        over = sb("over", [P, E, B])
        ntiles, mixed, first, last_t, first_s = (sb("ntiles", [P, E]), sb("mixed", [P, E, E]), sb("first", [P, E]),
                                                 sb("last_t", [P, E]), sb("first_s", [P, E]))
        count = sb("count", [P, E])
        place, placed = sb("place", [P, B, E]), sb("placed", [P, 2, B, E])
        slot, sloti = sb("slot", [P, 2 * B]), sb("sloti", [P, 2 * B], mybir.dt.int32)
        ti, ri = sb("ti", [P, 2 * B], mybir.dt.int32), sb("ri", [P, 2 * B], mybir.dt.int32)
        tf, rf = sb("tf", [P, 2 * B]), sb("rf", [P, 2 * B])
        hot_r = sb("hot_r", [P, 2 * B, P], F16)
        hot_t, pay = sb("hot_t", [P, 2 * B, TILES]), sb("pay", [P, 2 * B, TILES], F16)
        signed = sb("signed", [P, 2, B])
        inv, mag, size, isneg, iszero, dsum = (sb(n, [P, TILES]) for n in ("inv", "mag", "size", "isneg", "iszero", "dsum"))
        src_row, dst_row = sb("src_row", [P, TILES], U32), sb("dst_row", [P, TILES], U32)
        below, texp = sb("below", [P, TILES, E]), sb("texp", [P, TILES])
        texp_i = sb("texp_i", [P, TILES], mybir.dt.int32)
        got = [sb(f"got{s}", [P, RW], U32) for s in range(SLOTS)]
        xt = [sb(f"xt{s}", [P, 4, P], F16) for s in range(SLOTS)]
        gate = [sb(f"gate{s}", [P, 1]) for s in range(SLOTS)]
        hT = [sb(f"hT{s}", [P, MC, P]) for s in range(SLOTS)]
        ys = [sb(f"ys{s}", [P, D]) for s in range(SLOTS)]
        z0 = sb("z0", [P, 2, GB, D])
        z1 = sb("z1", [P, 2, GB, D])
        fin = sb("fin", [P, 2, GB, D])

        rank = bank("rank")
        table = bank("table")
        tp = rank
        hb = [bank(f"h{s}") for s in range(SLOTS)]
        yb = [table, bank("y1"), bank("y2")]

        upl_in = [sem(f"up_in{i}") for i in range(4)]
        (down_in, small_in, disp_in, b2_lo_in) = (sem(n) for n in ("down_in", "small_in", "disp_in", "b2_lo_in"))
        up_hi, up_lo, b2_hi, b2_lo = (sem(n) for n in ("up_hi", "up_lo", "b2_hi", "b2_lo"))
        chain = sem("chain")
        rank_full, table_full, idx_done, texp_done = (sem(n) for n in ("rank_full", "table_full", "idx_done", "texp_done"))
        gathered = [sem(f"gathered{s}") for s in range(SLOTS)]
        scattered = [sem(f"scattered{s}") for s in range(SLOTS)]
        tp_full, tp_free = sem("tp_full"), sem("tp_free")
        h_full, silu_done = sem("h_full"), sem("silu_done")
        y_full, y_free = sem("y_full"), sem("y_free")
        z_in, out_done = [sem("z_in0"), sem("z_in1")], [sem("out_done0"), sem("out_done1")]
        summed, fin_done = sem("summed"), sem("fin_done")
        hot_pool = sem("hot_pool")

        rows_w = rows
        picked_t = picked.rearrange("(k g b p) d -> k g p b d", k=2, b=GB, p=P)
        out_t = out.rearrange("(g b) p d -> g p b d", b=GB)

        block = ctx.enter_context(nc.Block())

        @block.sync
        def _(sp):
            sp.dma_start(dc[:], disp).then_inc(disp_in, 16)
            for i in range(4):
                sp.dma_start(up_f[:, 2 * i:2 * i + 2, :], ew1[:, 2 * i:2 * i + 2, :]).then_inc(upl_in[i], 16)
            sp.dma_start(b1[:], eb1).then_inc(small_in, 16)
            sp.dma_start(b2f[:], eb2.rearrange("(a e) d -> a (e d)", a=1).broadcast_to([2, E * D])).then_inc(small_in, 16)
            sp.dma_start(down[:].rearrange("p e m d -> p (e m d)"), ew2).then_inc(down_in, 16)
            sp.wait_ge(b2_lo, 1)
            sp.dma_start(b2h[1:2, :], b2l[1:2, :]).then_inc(b2_lo_in, 16)
            for s in range(SLOTS):
                sp.wait_ge(scattered[s], 16 * (TILES // SLOTS))
            for g in range(G):
                if g >= 2:
                    sp.wait_ge(fin_done, g - 1)
                sp.dma_start(z0[:, g % 2], picked_t[0, g]).then_inc(z_in[g % 2], 16)
                sp.dma_start(z1[:, g % 2], picked_t[1, g]).then_inc(z_in[g % 2], 16)
                if g >= 1:
                    sp.wait_ge(fin_done, g)
                    sp.dma_start(out_t[g - 1], fin[:, (g - 1) % 2]).then_inc(out_done[(g - 1) % 2], 16)
            sp.wait_ge(fin_done, G)
            sp.dma_start(out_t[G - 1], fin[:, (G - 1) % 2]).then_inc(out_done[(G - 1) % 2], 16)
            for half in range(2):
                sp.wait_ge(out_done[half], 16 * (G // 2))

        @block.gpsimd
        def _(pool):
            def gather(t):
                s = t % SLOTS
                if t >= SLOTS:
                    pool.wait_ge(tp_free, t - SLOTS + 1)
                pool.indirect_dma_start(got[s][:], None, rows_w,
                                        bass.IndirectOffsetOnAxis(src_row[:, t:t + 1], 0),
                                        bounds_check=B * L - 1, oob_is_err=False).then_inc(gathered[s], 16)

            def scatter(t):
                s = t % SLOTS
                pool.wait_ge(y_free, t + 2)
                pool.indirect_dma_start(picked, bass.IndirectOffsetOnAxis(dst_row[:, t:t + 1], 0), ys[s][:], None,
                                        bounds_check=2 * B * L - 1, oob_is_err=False).then_inc(scattered[s], 16)

            pool.wait_ge(idx_done, 1)
            for t in range(TILES):
                gather(t)
                if t >= SLOTS:
                    scatter(t - SLOTS)
            for t in range(TILES - SLOTS, TILES):
                scatter(t)

        @block.scalar
        def _(act):
            for i in range(4):
                act.wait_ge(upl_in[i], 16)
                act.activation(up_h[:, 2 * i:2 * i + 2].rearrange("p e c n -> p e (c n)"), up_f[:, 2 * i:2 * i + 2, :],
                               ACT.Copy, scale=UP).then_inc(up_hi, 1)
            act.wait_ge(small_in, 32)
            act.activation(b2h[:], b2f[:], ACT.Copy, scale=UP).then_inc(b2_hi, 1)
            act.preload_act_table(ACT.Silu)
            act.wait_ge(texp_done, 1)
            with act.Fori(0, TILES // SLOTS) as i:
                for s in range(SLOTS):
                    e = act.value_load(texp_i[0:1, bass.ds(i * SLOTS + s, 1)], min_val=0, max_val=E - 1)
                    act.wait_ge(h_full, i * SLOTS + s + 1)
                    for m in range(MC):
                        last = act.activation(hT[s][:, m, :], hb[s][:, m * P:(m + 1) * P], ACT.Silu,
                                              bias=b1[:, bass.ds(e * MC + m, 1)], scale=DOWN)
                    last.then_inc(silu_done, 1)

        @block.vector
        def _(dve):
            step = [0]

            def done(ins):
                step[0] += 1
                ins.then_inc(chain, 1)
                dve.wait_ge(chain, step[0])

            dve.sem_inc(y_free, 1)
            dve.wait_ge(disp_in, 16)
            dve.tensor_copy(beforeh[:], before)
            dve.tensor_copy(identh[:], ident)
            dve.memset(onesh[:], 1.0)
            dve.memset(ones2[:], 1.0 / UP)
            for k in range(2):
                ins = dve.tensor_tensor(hot[:, k], iota8.unsqueeze(1).to_broadcast([P, B, E]),
                                        eidx[:, :, k:k + 1].to_broadcast([P, B, E]), ALU.is_equal)
            done(ins)
            done(dve.tensor_tensor(both[:], hot[:, 0], hot[:, 1], ALU.add))
            for k in range(2):
                ins = dve.tensor_scalar(signed[:, k, :], token, 1.0 - 2.0 * k, None, ALU.mult)
            done(ins)
            dve.wait_ge(rank_full, 1)
            done(dve.tensor_copy(count[:], rank[:, B * E:(B + 1) * E]))
            done(dve.tensor_tensor(over[:], count[:].unsqueeze(2).to_broadcast([P, E, B]),
                                   steps.unsqueeze(1).to_broadcast([P, E, B]), ALU.is_gt))
            done(dve.tensor_reduce(ntiles[:], over[:], AX, ALU.add))
            done(dve.tensor_tensor(mixed[:], ntiles[:].unsqueeze(1).to_broadcast([P, E, E]),
                                   less.rearrange("p (a b) -> p a b", a=E), ALU.mult))
            done(dve.tensor_reduce(first[:], mixed[:], AX, ALU.add))
            done(dve.tensor_scalar(first_s[:], first[:], float(P), None, ALU.mult))
            done(dve.tensor_tensor(place[:], rank[:, 0:B * E].rearrange("p (b e) -> p b e", b=B),
                                   first_s[:].unsqueeze(1).to_broadcast([P, B, E]), ALU.add))
            done(dve.tensor_tensor(placed[:].rearrange("p k b e -> p k (b e)"),
                                   hot[:].rearrange("p k b e -> p k (b e)"),
                                   place[:].rearrange("p b e -> p (b e)").unsqueeze(1).to_broadcast([P, 2, B * E]),
                                   ALU.mult))
            done(dve.tensor_reduce(slot[:], placed[:].rearrange("p k b e -> p (k b) e"), AX, ALU.add))
            done(dve.tensor_copy(sloti[:], slot[:]))
            dve.tensor_scalar(ti[:], sloti[:], 7, None, ALU.arith_shift_right)
            done(dve.tensor_scalar(ri[:], sloti[:], P - 1, None, ALU.bitwise_and))
            dve.tensor_copy(tf[:], ti[:])
            done(dve.tensor_copy(rf[:], ri[:]))
            for q in range(2 * B):
                ins = dve.tensor_scalar(hot_r[:, q, :], iota_p, rf[:, q:q + 1], None, ALU.is_equal)
            dve.tensor_tensor(hot_t[:], iota_t.unsqueeze(1).to_broadcast([P, 2 * B, TILES]),
                              tf[:].unsqueeze(2).to_broadcast([P, 2 * B, TILES]), ALU.is_equal).then_inc(chain, 1)
            step[0] += 1
            dve.wait_ge(chain, step[0])
            done(dve.tensor_tensor(pay[:], hot_t[:], signed[:].rearrange("p k b -> p (k b)").unsqueeze(2)
                                   .to_broadcast([P, 2 * B, TILES]), ALU.mult))
            global TABLE_STEP
            TABLE_STEP = step[0]
            done(dve.tensor_tensor(last_t[:], first[:], ntiles[:], ALU.add))
            done(dve.tensor_tensor(below[:], last_t[:].unsqueeze(1).to_broadcast([P, TILES, E]),
                                   iota_t.unsqueeze(2).to_broadcast([P, TILES, E]), ALU.is_le))
            done(dve.tensor_reduce(texp[:], below[:], AX, ALU.add))
            done(dve.tensor_scalar(texp[:], texp[:], float(E - 1), None, ALU.min))
            dve.tensor_copy(texp_i[:], texp[:]).then_inc(texp_done, 1)
            dve.wait_ge(table_full, 1)
            done(dve.tensor_copy(inv[:], table[:, 0:TILES]))
            done(dve.scalar_tensor_tensor(out=mag[:], in0=inv[:], scalar=-1.0, in1=inv[:], op0=ALU.mult, op1=ALU.max))
            dve.tensor_scalar(size[:], mag[:], -1.0, None, ALU.add)
            dve.tensor_scalar(isneg[:], inv[:], 0.0, float(B * L), ALU.is_lt, ALU.mult)
            done(dve.tensor_scalar(iszero[:], inv[:], 0.0, float(SKIP), ALU.is_equal, ALU.mult))
            dve.tensor_scalar(src_row[:], size[:], 0.0, None, ALU.max)
            done(dve.tensor_tensor(dsum[:], size[:], isneg[:], ALU.add))
            dve.tensor_tensor(dst_row[:], dsum[:], iszero[:], ALU.add).then_inc(idx_done, 1)
            for i in range(4):
                dve.wait_ge(up_hi, i + 1)
                dve.scalar_tensor_tensor(out=up_l[:, 2 * i:2 * i + 2].rearrange("p e c n -> p e (c n)"),
                                         in0=up_f[:, 2 * i:2 * i + 2, :], scalar=UP,
                                         in1=up_h[:, 2 * i:2 * i + 2].rearrange("p e c n -> p e (c n)"),
                                         op0=ALU.mult, op1=ALU.subtract).then_inc(up_lo, 1)
            dve.wait_ge(b2_hi, 1)
            dve.scalar_tensor_tensor(out=b2l[:], in0=b2f[:], scalar=UP, in1=b2h[:], op0=ALU.mult,
                                     op1=ALU.subtract).then_inc(b2_lo, 1)

            def take(t, s):
                e = dve.value_load(texp_i[0:1, bass.ds(t, 1)], min_val=0, max_val=E - 1)
                dve.wait_ge(tp_full, t + 1)
                dve.tensor_copy(xt[s][:].rearrange("p a b -> p (a b)"), tp[:].bitcast(F16)[:, 0:4 * P])
                dve.tensor_copy(gate[s][:], got[s][:].bitcast(F32)[:, bass.ds(e + D, 1)]).then_inc(tp_free, 1)

            def weigh(t, s, n, after=True):
                if after:
                    dve.wait_ge(scattered[s], 16 * n)
                dve.wait_ge(y_full, t + 1)
                dve.tensor_scalar(ys[s][:], yb[s][:, 0:D], gate[s][:], None, ALU.mult).then_inc(y_free, 1)

            take(0, 0)
            take(1, 1)
            for s in range(SLOTS):
                weigh(s, s, 0, after=False)
                take(s + 2, (s + 2) % SLOTS)
            with dve.Fori(1, TILES // SLOTS - 1) as i:
                for s in range(SLOTS):
                    t = i * SLOTS + s
                    weigh(t, s, i)
                    take(t + 2, (s + 2) % SLOTS)
            t = TILES - SLOTS
            weigh(t, 0, TILES // SLOTS - 1)
            take(t + 2, 2)
            weigh(t + 1, 1, TILES // SLOTS - 1)
            weigh(t + 2, 2, TILES // SLOTS - 1)

            for g in range(G):
                dve.wait_ge(z_in[g % 2], 32 * (g // 2 + 1))
                dve.tensor_tensor(z0[:, g % 2], z0[:, g % 2], z1[:, g % 2], ALU.add).then_inc(summed, 1)
                dve.wait_ge(summed, g + 1)
                if g >= 2:
                    dve.wait_ge(out_done[g % 2], 16 * (g // 2))
                dve.tensor_tensor(fin[:, g % 2], z0[:, g % 2], base[:, g * GB:(g + 1) * GB, :], ALU.add)\
                    .then_inc(fin_done, 1)

        @block.tensor
        def _(pe):
            pe.wait_ge(chain, 2)
            flat = both[:].rearrange("p b e -> p (b e)")
            pe.matmul(rank[:, 0:B * E], beforeh[:], flat, start=True, stop=True, skip_group_check=True)
            for b in range(B):
                n = B - b
                ins = pe.matmul(rank[:, (b + 1) * E:(B + 1) * E].rearrange("p (n e) -> p n e", n=n), onesh[:],
                                both[:, b:b + 1, :].to_broadcast([P, n, E]), start=False, stop=True,
                                skip_group_check=True)
            ins.then_inc(rank_full, 1)
            pe.wait_ge(chain, TABLE_STEP)
            for q in range(2 * B):
                ins = pe.matmul(table[:, 0:TILES], hot_r[:, q, :], pay[:, q, :], start=(q == 0), stop=(q == 2 * B - 1))
            ins.then_inc(table_full, 1)

            def turn(t, s, n):
                pe.wait_ge(gathered[s], 16 * n)
                pe.wait_ge(tp_free, t)
                g = got[s][:].bitcast(F16)
                v = tp[:].bitcast(F16)
                for j in range(4):
                    ins = pe.transpose(v[:, j * P:(j + 1) * P], g[:, j * P:(j + 1) * P], identh[:])
                ins.then_inc(tp_full, 1)

            def hidden(t, s):
                e = pe.value_load(texp_i[0:1, bass.ds(t, 1)], min_val=0, max_val=E - 1)
                pe.wait_ge(tp_free, t + 1)
                for m in range(MC):
                    k = 0
                    for c in range(KC):
                        for w, x in ((up_h, c), (up_h, KC + c), (up_l, c)):
                            lhs = w[:, bass.ds(e, 1), c, m * P:(m + 1) * P].rearrange("p a n -> p (a n)")
                            ins = pe.matmul(hb[s][:, m * P:(m + 1) * P], lhs, xt[s][:, x, :],
                                            start=(k == 0), stop=(k == 3 * KC - 1))
                            k += 1
                ins.then_inc(h_full, 1)
                return e

            def outer(t, s, e, first):
                pe.wait_ge(silu_done, t + 1)
                if not first:
                    pe.wait_ge(y_free, t - SLOTS + 2)
                for m in range(MC):
                    pe.matmul(yb[s][:, 0:D], hT[s][:, m, :],
                              down[:, bass.ds(e, 1), m, :].rearrange("p a n -> p (a n)"), start=(m == 0), stop=False)
                ins = pe.matmul(yb[s][:, 0:D], ones2[:], b2h[:, bass.ds(e * D, D)], start=False, stop=True)
                ins.then_inc(y_full, 1)

            turn(0, 0, 1)
            pe.wait_ge(up_hi, 4)
            pe.wait_ge(up_lo, 4)
            pe.wait_ge(down_in, 16)
            pe.wait_ge(b2_lo_in, 16)

            e0 = hidden(0, 0)
            turn(1, 1, 1)
            e1 = hidden(1, 1)
            outer(0, 0, e0, True)
            turn(2, 2, 1)
            e2 = hidden(2, 2)
            outer(1, 1, e1, True)
            turn(3, 0, 2)
            with pe.Fori(1, TILES // SLOTS - 1) as i:
                t = i * SLOTS
                ep = pe.value_load(texp_i[0:1, bass.ds(t - 1, 1)], min_val=0, max_val=E - 1)
                for s in range(SLOTS):
                    e = hidden(t + s, s)
                    outer(t + s - 1, (s + 2) % SLOTS, ep, False)
                    turn(t + s + 1, (s + 1) % SLOTS, i + 1 if s < 2 else i + 2)
                    ep = e
            t = TILES - SLOTS
            n = TILES // SLOTS
            ep = pe.value_load(texp_i[0:1, t - 1:t], min_val=0, max_val=E - 1)
            for s in range(SLOTS):
                e = hidden(t + s, s)
                outer(t + s - 1, (s + 2) % SLOTS, ep, False)
                if s < 2:
                    turn(t + s + 1, s + 1, n)
                ep = e
            outer(t + 2, 2, ep, False)


def extra_data(np, n, data):
    f = np.float32
    p = np.arange(P)
    row = lambda v: np.tile(np.asarray(v, f), (P, 1))
    data["ew1"] = n["L0_ffn_ew1"].reshape(E, KC, P, HID).transpose(2, 0, 1, 3).reshape(P, E, KC * HID)
    data["eb1"] = n["L0_ffn_eb1"].reshape(E, MC, P).transpose(2, 0, 1).reshape(P, E * MC)
    data["ew2"] = n["L0_ffn_ew2"].reshape(E, MC, P, D).transpose(2, 0, 1, 3).reshape(P, E * MC * D)
    data["eb2"] = n["L0_ffn_eb2"]
    data["disp"] = np.concatenate([
        (p[:, None] < p[None, :]).astype(f), row(p), row(np.arange(TILES)), row(P * np.arange(B)),
        row((np.arange(E)[None, :] < np.arange(E)[:, None]).reshape(-1)),
        (np.arange(B)[None, :] * P + p[:, None] + 1).astype(f), row(np.arange(E)), np.eye(P, dtype=f)], axis=1)


def build(nc, a, out):
    rows = nc.dram_tensor("rows", [B * L, ROW // 2], U32, kind="Internal").ap()
    picked = nc.dram_tensor("picked", [2 * B * L, D], F32, kind="Internal").ap()
    with ExitStack() as ctx:
        base = ctx.enter_context(nc.sbuf_tensor("base", [P, B, D], F32))
        eidx = ctx.enter_context(nc.sbuf_tensor("eidx", [P, B, 2], F32))
        attention_phase(nc, (base, eidx, None, rows),
                        tuple(a[k] for k in ("x", "ctx", "w1", "w2", "wc", "xbias", "bc", "rw1", "rb1", "rw2", "rb2",
                                             "consts")))
        expert_phase(nc, (base, eidx, rows, picked), tuple(a[k] for k in ("ew1", "eb1", "ew2", "eb2", "disp")), out)


def shape_constants(np):
    f = np.float32
    i = np.arange(D // 2, dtype=f)
    theta = np.power(f(10000.0), (f(-2.0) * (i - f(1.0)) / f(D)).astype(f)).astype(f)
    ang = (np.arange(L, dtype=f)[:, None] * theta[None, :]).astype(f)
    q = np.arange(L)[:, None]
    k = np.arange(L)[None, :]
    masks = [np.where(k <= q, 0.0, NEG)]
    for d in (1, 2, 4, 8):
        off = k - q
        ok = (off % d == 0) & (off // d >= -((WIN - 1) // 2)) & (off // d <= WIN - 1 - (WIN - 1) // 2)
        masks.append(np.where(ok, 0.0, NEG))
    return np.concatenate([np.cos(ang).T, np.sin(ang).T] + masks + [np.eye(P), np.tile(np.arange(E), (P, 1))],
                          axis=1).astype(f)


def kernel(**inputs):
    import numpy as np
    import concourse.bacc as bacc
    from concourse.bass_utils import run_bass_kernel_spmd

    def chunks(a):
        return a.reshape(KC, P, -1).transpose(1, 0, 2)

    n = {k: np.asarray(v) for k, v in inputs.items()}
    wq, wk, wv = n["L0_attn_w_q"], n["L0_attn_w_k"], n["L0_attn_w_v"]
    data = {
        "x": n["x"],
        "ctx": n["ctx_1024"],
        "w1": chunks(np.concatenate([wq[0::2], wq[1::2], wk[0::2], wk[1::2], wv], axis=0).T),
        "w2": chunks(np.concatenate([n["L0_xattn_" + w].reshape(H * DH, D) for w in ("Wk", "Wv", "Wq")], axis=0).T),
        "wc": n["L0_xattn_Wc"].T.reshape(H, DH, D).transpose(1, 0, 2),
        "xbias": np.concatenate([n["L0_xattn_" + w].T for w in ("bq", "bk", "bv")], axis=1),
        "bc": n["L0_xattn_bc"],
        "rw1": chunks(n["L0_ffn_rw1"]),
        "rb1": n["L0_ffn_rb1"].reshape(KC, P).T,
        "rw2": chunks(n["L0_ffn_rw2"]),
        "rb2": n["L0_ffn_rb2"],
        "consts": shape_constants(np),
    }
    extra_data(np, n, data)
    nc = bacc.Bacc("TRN2", target_bir_lowering=False, num_devices=1)
    arrays, aps = {}, {}
    for name, a in data.items():
        arrays["in_" + name] = np.ascontiguousarray(a)
        aps[name] = nc.dram_tensor("in_" + name, a.shape, mybir.dt.from_np(a.dtype), kind="ExternalInput").ap()
    out = nc.dram_tensor("out", [B, L, D], F32, kind="ExternalOutput").ap()
    build(nc, aps, out)
    r = run_bass_kernel_spmd(nc, [arrays], core_ids=[0])
    return r.results[0]["out"]
```

```python
from contextlib import ExitStack

import numpy as np

import concourse.bass as bass
from concourse import mybir

F32 = mybir.dt.float32
F16 = mybir.dt.float16
BF16 = mybir.dt.bfloat16
U32 = mybir.dt.uint32
ALU = mybir.AluOpType
ACT = mybir.ActivationFunctionType
AX = mybir.AxisListType.X

P = 128
B, L, D = 16, 128, 256
GB = 4
G = B // GB
TOK = GB * L
KC = D // P
H, DH = 8, 128
DILATIONS = (1, 1, 2, 2, 4, 4, 8, 8)
WIN = 64
E, HID = 8, 512
EPS = 1e-5
NEG = -1e30
UP = 256.0
DOWN = 1.0 / (UP * UP)
ATTN_SCALE = DOWN * DOWN / float(D) ** 0.5
ROW = 2 * D + 2 * E


def bc(ap, shape):
    return ap.to_broadcast(shape)


class Room:

    def __init__(self, ap):
        self.ap, self.at = ap, 0

    def take(self, a, b):
        view = self.ap[:, self.at:self.at + a * b].rearrange("p (a b) -> p a b", a=a)
        self.at += a * b
        assert self.at <= self.ap.shape[1]
        return view


def attention_phase(nc, shared, dram, debug_out=None):
    (x, ctxt, w1a, w2a, wca, xbias, bcd, rw1, rb1, rw2, rb2, consts, disp, ew1) = dram
    base, eidx, rows, cols, dc, identh = (shared[k] for k in ("base", "eidx", "rows", "cols", "dc", "identh"))
    up_f, up_h, up_l, up_in, up_hi, up_lo, row_out = (
        shared[k] for k in ("up_f", "up_h", "up_l", "up_in", "up_hi", "up_lo", "row_out"))
    ident, iota8 = cols["ident"], cols["iota8"]
    with ExitStack() as ctx:
        def sb(name, shape, dt=F32):
            return ctx.enter_context(nc.sbuf_tensor(name, shape, dt))

        def bank(name):
            return ctx.enter_context(nc.psum_tensor(name, [P, 512], F32))

        def sem(name):
            return ctx.enter_context(nc.semaphore(name))

        room = Room(up_f[:].rearrange("p e n -> p (e n)").bitcast(F16))
        w2h, w2l = room.take(KC, 3072), room.take(KC, 3072)
        w1h, w1l = room.take(KC, 768), room.take(KC, 768)
        ch = room.take(GB, D)
        r1h, r1l = sb("r1h", [P, KC, D], F16), sb("r1l", [P, KC, D], F16)
        wc = sb("wc", [P, H, D])
        rw2s = sb("rw2s", [P, KC, E])
        rb1s, rb1half = sb("rb1s", [P, KC]), sb("rb1half", [P, KC])
        rb2s = sb("rb2s", [P, E])
        bias = sb("bias", [P, 3 * H])
        bcs = sb("bcs", [P, D])
        cst = sb("cst", [P, 2 * P + 5 * P])
        cosT = cst[:, 0:P]
        sinT = cst[:, P:2 * P]
        masks = sb("masks", [P, 5, P], BF16)
        identb = sb("identb", [P, P], BF16)
        nhalf = sb("nhalf", [P, GB])
        room = Room(up_l[:].rearrange("p e c n -> p (e c n)").bitcast(F32))
        xg, cg = sb("xg", [P, GB, D]), room.take(GB, D)
        qr, kr, v1 = room.take(KC, TOK), room.take(KC, TOK), room.take(GB, D)
        xn = sb("xn", [P, GB, D])
        room = Room(up_h[:].rearrange("p e c n -> p (e c n)"))
        xTh, xTl, cTh, cTl = (room.take(KC, TOK) for _ in range(4))
        nh, nl, cl = (room.take(GB, D) for _ in range(3))
        stats, mv = sb("stats", [P, GB, 6]), sb("mv", [P, GB, 2])
        veps, rstd, rstd_up = sb("veps", [P, GB]), sb("rstd", [P, GB]), sb("rstd_up", [P, GB])
        rope = sb("rope", [P, 4, TOK])
        p1, pT1 = sb("p1", [P, GB, P]), sb("pT1", [P, GB, P])
        mx1, nm1, sum1, inv1 = (sb(n, [P, GB]) for n in ("mx1", "nm1", "sum1", "inv1"))
        kT, qT = sb("kT", [P, H, TOK]), sb("qT", [P, H, TOK])
        v2 = sb("v2", [P, GB, H * DH])
        p2, pn2, pT2 = (sb(n, [P, 2, 4, P]) for n in ("p2", "pn2", "pT2"))
        mx2, nm2, sum2, inv2 = (sb(n, [P, 2, 4]) for n in ("mx2", "nm2", "sum2", "inv2"))
        oT = sb("oT", [P, 2, H, P])
        x1, x2 = sb("x1", [P, GB, D]), sb("x2", [P, GB, D])
        row = sb("row", [P, GB, ROW], F16)
        rTh, rTl = sb("rTh", [P, KC, TOK], F16), sb("rTl", [P, KC, TOK], F16)
        xb, th = rope[:, 0:2, :], rope[:, 2:4, :]
        lg, mx8 = sb("lg", [P, GB, E]), sb("mx8", [P, GB, E])
        ix8 = sb("ix8", [P, GB, E], U32)
        gd, ge, gs = sb("gd", [P, GB]), sb("ge", [P, GB]), sb("gs", [P, GB])
        g1, g2 = sb("g1", [P, GB]), sb("g2", [P, GB])
        ixf = sb("ixf", [P, GB, 2])
        m1, m2 = sb("m1", [P, GB, E]), sb("m2", [P, GB, E])

        w1f = kT[:, 0:3, :].rearrange("p a b -> p (a b)").rearrange("p (c n) -> p c n", c=KC)
        wkf = v2[:, 0:2, :]
        wvf = v2[:, 2:4, :]
        r1f = x2[:, 0:2, :]
        wqf = qT[:, 0:4, :].rearrange("p a b -> p (a b)").rearrange("p (c n) -> p c n", c=KC)

        tpA, tpB, pj0, pj1, sc0, sc1, ov, op = (
            bank(n) for n in ("tpA", "tpB", "pj0", "pj1", "sc0", "sc1", "ov", "op"))
        pj, sc = (pj0, pj1), (sc0, sc1)
        tpA_full, tpA_free = sem("tpA_full"), sem("tpA_free")
        tpB_full, tpB_free = sem("tpB_full"), sem("tpB_free")
        pj_full, pj_free = (sem("pj0_full"), sem("pj1_full")), (sem("pj0_free"), sem("pj1_free"))
        sc_full, sc_free = (sem("sc0_full"), sem("sc1_full")), (sem("sc0_free"), sem("sc1_free"))
        ov_full, ov_free = sem("ov_full"), sem("ov_free")
        op_full, op_free = sem("op_full"), sem("op_free")
        TPA, TPB, PJ, SC, OV, OP = 8, 7, 14, (8, 6), 10, 6
        LAST = (SC[0] * G - 3, SC[1] * G - 2)

        const_in, w1_in, wk_in, wv_in, wq_in = (sem(n) for n in ("const_in", "w1_in", "wk_in", "wv_in", "wq_in"))
        wc_in, r_in, xg_in, cg_in, table_in, bc_in = (
            sem(n) for n in ("wc_in", "r_in", "xg_in", "cg_in", "table_in", "bc_in"))
        ready, nhalf_set = sem("ready"), sem("nhalf_set")
        w1_hi, w1_lo, w2_hi, w2_lo, r1_hi, r1_lo = (
            sem(n) for n in ("w1_hi", "w1_lo", "w2_hi", "w2_lo", "r1_hi", "r1_lo"))
        ln = {k: {s: sem(f"ln{k}_{s}") for s in ("stats", "aggr", "var", "pow", "rstd", "xn", "hi", "lo")}
              for k in (1, 2, 3)}
        c_hi, c_lo = sem("c_hi"), sem("c_lo")
        rope_add = sem("rope_add")
        max1, neg1, inv1_done, x1_bias = (
            sem(n) for n in ("max1", "neg1", "inv1_done", "x1_bias"))
        max2, neg2, inv2_done, norm2, x2_done = (
            sem(n) for n in ("max2", "neg2", "inv2_done", "norm2", "x2_done"))
        base_done, r_tanh, r_xb, r_hid = (sem(n) for n in ("base_done", "r_tanh", "r_xb", "r_hid"))
        lg_done, top8, top8i, gdiff, gexp, gsum, gate1, gate2, ixf_done, hot, wrow, wrow2 = (
            sem(n) for n in ("lg_done", "top8", "top8i", "gdiff", "gexp", "gsum", "gate1", "gate2",
                             "ixf_done", "hot", "wrow", "wrow2"))
        kept, dbg, waited = sem("kept"), sem("dbg"), sem("waited")

        x_t = x.rearrange("(g b) p d -> g p b d", b=GB)
        c_t = ctxt.rearrange("(g b) p d -> g p b d", b=GB)
        rows_t = rows.rearrange("(p g b) w -> g p b w", b=GB, g=G)

        block = ctx.enter_context(nc.Block())


        @block.sync
        def _(sp):
            sp.sem_inc(row_out, 16)
            sp.dma_start(xg[:], x_t[0]).then_inc(xg_in, 16)
            sp.dma_start(w1f, w1a).then_inc(w1_in, 16)
            sp.dma_start(dc[:], disp).then_inc(const_in, 16)
            sp.dma_start(cg[:], c_t[0]).then_inc(cg_in, 16)
            sp.dma_start(wkf, w2a[:, :, 0:1024]).then_inc(wk_in, 16)
            sp.dma_start(cst[:], consts).then_inc(table_in, 16)
            sp.dma_start(bias[:], xbias).then_inc(table_in, 16)
            sp.dma_start(wvf, w2a[:, :, 1024:2048]).then_inc(wv_in, 16)
            sp.dma_start(wqf, w2a[:, :, 2048:3072]).then_inc(wq_in, 16)
            sp.dma_start(bcs[:], bcd.rearrange("(a n) -> a n", a=1).broadcast_to([P, D])).then_inc(bc_in, 16)
            sp.dma_start(wc[:], wca).then_inc(wc_in, 16)
            sp.dma_start(r1f, rw1).then_inc(r_in, 16)
            sp.dma_start(rw2s[:], rw2).then_inc(r_in, 16)
            sp.dma_start(rb1s[:], rb1).then_inc(r_in, 16)
            sp.dma_start(rb2s[:], rb2.rearrange("(a n) -> a n", a=1).broadcast_to([P, E])).then_inc(r_in, 16)

            with sp.Fori(1, G) as g:
                sp.wait_ge(c_lo, g)
                sp.dma_start(cg[:], c_t[g]).then_inc(cg_in, 16)
                sp.wait_ge(ov_free, OV * (g - 1) + 2)
                sp.wait_ge(op_free, OP * (g - 1) + 2)
                sp.dma_start(xg[:], x_t[g]).then_inc(xg_in, 16)
                sp.wait_ge(wrow2, g)
                sp.dma_start(rows_t[g - 1], row[:].bitcast(U32)).then_inc(row_out, 16)
            sp.wait_ge(pj_full[0], PJ * G)
            sp.wait_ge(pj_full[1], PJ * G)
            for i in range(4):
                sp.dma_start(up_f[:, 2 * i:2 * i + 2, :], ew1[:, 2 * i:2 * i + 2, :]).then_inc(up_in[i], 16)
            sp.wait_ge(wrow2, G)
            sp.dma_start(rows_t[G - 1], row[:].bitcast(U32)).then_inc(row_out, 16)
            if debug_out is not None:
                sp.wait_ge(base_done, G)
                sp.dma_start(debug_out.rearrange("b p d -> p b d"), base[:]).then_inc(dbg, 16)
                sp.wait_ge(dbg, 16)

        @block.gpsimd
        def _(pool):
            pool.memset(nhalf[:], -0.5).then_inc(nhalf_set, 1)
            pool.wait_ge(nhalf_set, 1)

            def power(k, n):
                pool.wait_ge(ln[k]["var"], n + 1)
                pool.tensor_tensor(rstd[:], veps[:], nhalf[:], ALU.pow).then_inc(ln[k]["pow"], 1)

            def front(g, r=None):
                for i, dst in enumerate((qr, kr)):
                    pool.wait_ge(pj_free[0], PJ * g + i + 1)
                    pool.wait_ge(pj_free[1], PJ * g + i + 1)
                    if r is not None:
                        pool.wait_ge(max1, g)
                    pool.tensor_tensor(dst[:, 0, :], rope[:, 0, :], rope[:, 2, :], ALU.add)
                    pool.tensor_tensor(dst[:, 1, :], rope[:, 3, :], rope[:, 1, :], ALU.subtract)\
                        .then_inc(rope_add, 1)
                if r is not None:
                    power(3, r)
                power(2, g)
                pool.wait_ge(ln[2]["xn"], g + 1)
                pool.tensor_tensor(x1[:], x1[:], bcs[:].unsqueeze(1).to_broadcast([P, GB, D]), ALU.add)\
                    .then_inc(x1_bias, 1)

            def back(g, more):
                for n in range(8):
                    if n == 4 and more:
                        power(1, g + 1)
                    if n >= 2:
                        pool.wait_ge((tpA_full, tpB_full)[n % 2],
                                     (TPA * g + 4, TPB * g + 3)[n % 2] + (n - 2) // 2 + 1)
                    pool.wait_ge(inv2_done, 8 * g + n + 1)
                    pool.tensor_tensor(pn2[:, n % 2], p2[:, n % 2],
                                       inv2[:, n % 2, :].unsqueeze(2).to_broadcast([P, 4, P]), ALU.mult)\
                        .then_inc(norm2, 1)

            power(1, 0)
            pool.wait_ge(bc_in, 16)
            front(0)
            with pool.Fori(0, G - 1) as g:
                back(g, True)
                front(g + 1, g)
            back(G - 1, False)
            power(3, G - 1)

        @block.scalar
        def _(act):
            copy = lambda out, in_, scale=1.0: act.activation(out, in_, ACT.Copy, scale=scale)

            def high(k, n, dst):
                act.wait_ge(ln[k]["xn"], n + 1)
                copy(dst, xn[:]).then_inc(ln[k]["hi"], 1)

            def early(g):
                act.wait_ge(tpA_full, TPA * (g - 1) + 4)
                high(1, g, nh[:])
                act.wait_ge(cg_in, 16 * (g + 1))
                copy(ch[:], cg[:], UP).then_inc(c_hi, 1)

            def turned(g):
                act.wait_ge(tpA_full, TPA * g + 1)
                copy(xTh[:], tpA[:].bitcast(F16)).then_inc(tpA_free, 1)
                act.wait_ge(tpA_full, TPA * g + 2)
                copy(cTh[:], tpA[:].bitcast(F16)).then_inc(tpA_free, 1)

            def project(g, kind, js):
                for j in js:
                    s = j % 2
                    act.wait_ge(pj_full[s], PJ * g + 2 + 4 * kind + j // 2 + 1)
                    if kind == 1:
                        h0 = 512 * (j % 2)
                        copy(v2[:, j // 2, h0:h0 + 512], pj[s][:], DOWN).then_inc(pj_free[s], 1)
                    else:
                        out, b = ((kT, H + j), None, (qT, j))[kind]
                        act.activation(out[:, j, :], pj[s][:], ACT.Identity, bias=bias[:, b:b + 1],
                                       scale=DOWN).then_inc(pj_free[s], 1)

            def rows_high(r):
                act.wait_ge(row_out, 16 * r + 16)
                high(3, r, row[:, :, 0:D])

            def router(r, u0, u1):
                for m in range(KC):
                    act.wait_ge(sc_full[m], (u0, u1)[m] + 2)
                    act.activation(th[:, m, :], sc[m][:], ACT.Tanh, bias=rb1half[:, m:m + 1],
                                   scale=0.5 * DOWN).then_inc(r_tanh, 1)

            def gate_exp(r):
                act.wait_ge(gdiff, r + 1)
                act.activation(ge[:], gd[:], ACT.Exp).then_inc(gexp, 1)

            def weights_high(i, q, src):
                act.wait_ge(q, 16)
                copy(w2h[:, :, 1024 * i:1024 * i + 1024], src, UP).then_inc(w2_hi, 1)

            def front(g, r=None):
                for i, (bank_, full, free, use) in enumerate(((ov, ov_full, ov_free, OV * g), (op, op_full, op_free, OP * g))):
                    act.wait_ge(full, use + 1)
                    copy(v1[:, 2 * i:2 * i + 2, :], bank_[:], DOWN).then_inc(free, 1)
                if r is None:
                    weights_high(1, wv_in, wvf)
                project(g, 0, range(3))
                if r is not None:
                    rows_high(r)
                project(g, 0, range(3, 4))
                act.wait_ge(neg1, g + 1)
                for b in range(GB):
                    last = act.activation(p1[:, b, :], sc0[:, b * P:(b + 1) * P], ACT.Exp,
                                          bias=nm1[:, b:b + 1], scale=ATTN_SCALE, accum_out=sum1[:, b:b + 1])
                last.then_inc(sc_free[0], 1)
                project(g, 0, range(4, 8))
                if r is None:
                    weights_high(2, wq_in, wqf)
                act.wait_ge(tpA_full, TPA * g + 3)
                copy(pT1[:], tpA[:]).then_inc(tpA_free, 1)
                if r is not None:
                    act.wait_ge(sc_full[0], SC[0] * r + 7)
                    copy(rTh[:], sc0[:].bitcast(F16)).then_inc(sc_free[0], 1)
                project(g, 1, range(4))
                if r is not None:
                    act.wait_ge(rope_add, 2 * g + 2)
                    router(r, SC[0] * r + 6, SC[1] * r + 4)
                else:
                    act.wait_ge(r_in, 64)
                    copy(r1h[:], r1f, UP).then_inc(r1_hi, 1)
                    copy(rb1half[:], rb1s[:], 0.5).then_inc(r1_hi, 1)
                high(2, g, nh[:])
                project(g, 1, range(4, 8))
                act.wait_ge(tpA_full, TPA * g + 4)
                copy(xTh[:], tpA[:].bitcast(F16)).then_inc(tpA_free, 1)
                if r is not None:
                    gate_exp(r)

            def back(g, more):
                project(g, 2, range(6))
                for n in range(8):
                    if n == 5 and more:
                        early(g + 1)
                    s = n % 2
                    if n >= 2:
                        act.wait_ge(norm2, 8 * g + n - 1)
                    act.wait_ge(neg2, 8 * g + n + 1)
                    for i in range(4):
                        last = act.activation(p2[:, s, i, :], sc[s][:, i * P:(i + 1) * P], ACT.Exp,
                                              bias=nm2[:, s, i:i + 1], scale=1.0,
                                              accum_out=sum2[:, s, i:i + 1])
                    last.then_inc(sc_free[s], 1)
                if more:
                    turned(g + 1)

            act.wait_ge(w1_in, 16)
            copy(w1h, w1f, UP).then_inc(w1_hi, 1)
            high(1, 0, nh[:])
            act.wait_ge(cg_in, 16)
            copy(ch[:], cg[:], UP).then_inc(c_hi, 1)
            weights_high(0, wk_in, wkf)
            turned(0)
            front(0)
            act.wait_ge(r1_hi, 2)
            with act.Fori(0, G - 1) as g:
                back(g, True)
                front(g + 1, g)
            back(G - 1, False)
            for i in range(4):
                act.wait_ge(up_in[i], 16)
                copy(up_h[:, 2 * i:2 * i + 2].rearrange("p e c n -> p e (c n)"), up_f[:, 2 * i:2 * i + 2, :],
                     UP).then_inc(up_hi, 1)
            rows_high(G - 1)
            act.wait_ge(sc_full[0], LAST[0] + 1)
            copy(rTh[:], sc0[:].bitcast(F16)).then_inc(sc_free[0], 1)
            router(G - 1, *LAST)
            gate_exp(G - 1)

        @block.vector
        def _(dve):
            def norm(k, n, src):
                for b in range(GB):
                    last = dve.bn_stats(stats[:, b, :], src[:, b, :])
                last.then_inc(ln[k]["stats"], 1)
                dve.wait_ge(ln[k]["stats"], n + 1)
                dve.sem_inc(waited, 1)
                for b in range(GB):
                    last = dve.bn_aggr(mv[:, b, :], stats[:, b, :])
                last.then_inc(ln[k]["aggr"], 1)
                dve.wait_ge(ln[k]["aggr"], n + 1)
                dve.tensor_scalar(veps[:], mv[:, :, 1], EPS, None, ALU.add).then_inc(ln[k]["var"], 1)

            def normed(k, n, src):
                dve.wait_ge(ln[k]["pow"], n + 1)
                dve.tensor_scalar(rstd_up[:], rstd[:], UP, None, ALU.mult).then_inc(ln[k]["rstd"], 1)
                dve.wait_ge(ln[k]["rstd"], n + 1)
                for b in range(GB):
                    last = dve.tensor_scalar(xn[:, b, :], src[:, b, :], mv[:, b, 0:1], rstd_up[:, b:b + 1],
                                             ALU.subtract, ALU.mult)
                last.then_inc(ln[k]["xn"], 1)

            def low(k, n, hi, dst):
                dve.wait_ge(ln[k]["xn"], n + 1)
                dve.wait_ge(ln[k]["hi"], n + 1)
                dve.tensor_tensor(dst, xn[:], hi, ALU.subtract).then_inc(ln[k]["lo"], 1)

            def context_low(g):
                dve.wait_ge(c_hi, g + 1)
                dve.scalar_tensor_tensor(out=cl[:], in0=cg[:], scalar=UP, in1=ch[:], op0=ALU.mult,
                                         op1=ALU.subtract).then_inc(c_lo, 1)

            def early(g, part):
                if part == 0:
                    dve.wait_ge(xg_in, 16 * (g + 1))
                    norm(1, g, xg)
                elif part == 1:
                    normed(1, g, xg)
                else:
                    dve.wait_ge(tpB_full, TPB * (g - 1) + 3)
                    low(1, g, nh[:], nl[:])
                    context_low(g)

            def turned(g, part):
                dve.wait_ge(tpB_full, TPB * g + 1 + part)
                dve.tensor_copy((xTl, cTl)[part][:], tpB[:].bitcast(F16)).then_inc(tpB_free, 1)

            def weights_low2(i, src):
                dve.wait_ge(w2_hi, i + 1)
                dve.scalar_tensor_tensor(out=w2l[:, :, 1024 * i:1024 * i + 1024], in0=src, scalar=UP,
                                         in1=w2h[:, :, 1024 * i:1024 * i + 1024], op0=ALU.mult,
                                         op1=ALU.subtract).then_inc(w2_lo, 1)

            def weights_low(i):
                dve.wait_ge(up_hi, i + 1)
                dve.scalar_tensor_tensor(out=up_l[:, 2 * i:2 * i + 2].rearrange("p e c n -> p e (c n)"),
                                         in0=up_f[:, 2 * i:2 * i + 2, :], scalar=UP,
                                         in1=up_h[:, 2 * i:2 * i + 2].rearrange("p e c n -> p e (c n)"),
                                         op0=ALU.mult, op1=ALU.subtract).then_inc(up_lo, 1)

            def rows_low(r):
                normed(3, r, x2)
                dve.wait_ge(ln[3]["xn"], r + 1)
                dve.scalar_tensor_tensor(out=base[:, bass.ds(r * GB, GB), :], in0=xn[:], scalar=1.0 / UP, in1=x2[:],
                                         op0=ALU.mult, op1=ALU.add).then_inc(base_done, 1)
                low(3, r, row[:, :, 0:D], row[:, :, D:2 * D])

            def router_turned(r, u1):
                dve.wait_ge(sc_full[1], u1 + 1)
                dve.tensor_copy(rTl[:], sc1[:].bitcast(F16)).then_inc(sc_free[1], 1)

            def router(r, u0, u1):
                for m in range(KC):
                    dve.wait_ge(r_tanh, KC * r + m + 1)
                    dve.tensor_scalar(xb[:, m, :], sc[m][:], DOWN, rb1s[:, m:m + 1], ALU.mult, ALU.add)\
                        .then_inc(sc_free[m], 1)
                    dve.wait_ge(sc_free[m], (u0, u1)[m] + 2)
                    dve.scalar_tensor_tensor(out=xb[:, m, :], in0=th[:, m, :], scalar=1.0, in1=xb[:, m, :],
                                             op0=ALU.add, op1=ALU.mult).then_inc(r_hid, 1)

            def choose(r, u0):
                dve.wait_ge(sc_full[0], u0 + 3)
                dve.scalar_tensor_tensor(out=lg[:], in0=sc0[:, 0:GB * E].rearrange("p (b e) -> p b e", b=GB),
                                         scalar=0.5, in1=rb2s[:].unsqueeze(1).to_broadcast([P, GB, E]),
                                         op0=ALU.mult, op1=ALU.add).then_inc(sc_free[0], 1)
                dve.wait_ge(sc_free[0], u0 + 3)
                dve.sem_inc(waited, 1)
                for b in range(GB):
                    last = dve.max(mx8[:, b, :], lg[:, b, :])
                last.then_inc(top8, 1)
                dve.wait_ge(top8, r + 1)
                dve.sem_inc(waited, 1)
                for b in range(GB):
                    last = dve.max_index(ix8[:, b, :], mx8[:, b, :], lg[:, b, :])
                last.then_inc(top8i, 1)
                dve.tensor_tensor(gd[:], mx8[:, :, 1], mx8[:, :, 0], ALU.subtract).then_inc(gdiff, 1)
                iob = iota8.unsqueeze(1).to_broadcast([P, GB, E])
                dve.wait_ge(top8i, r + 1)
                dve.tensor_copy(ixf[:], ix8[:, :, 0:2]).then_inc(ixf_done, 1)
                dve.wait_ge(ixf_done, r + 1)
                dve.tensor_copy(eidx[:, bass.ds(r * GB, GB), :], ixf[:]).then_inc(kept, 1)
                dve.tensor_tensor(m1[:], iob, ixf[:, :, 0:1].to_broadcast([P, GB, E]), ALU.is_equal)
                dve.tensor_tensor(m2[:], iob, ixf[:, :, 1:2].to_broadcast([P, GB, E]), ALU.is_equal).then_inc(hot, 1)
                dve.wait_ge(gexp, r + 1)
                dve.tensor_scalar(gs[:], ge[:], 1.0, None, ALU.add).then_inc(gsum, 1)
                dve.wait_ge(gsum, r + 1)
                dve.reciprocal(g1[:], gs[:]).then_inc(gate1, 1)
                dve.wait_ge(gate1, r + 1)
                dve.tensor_tensor(g2[:], ge[:], g1[:], ALU.mult).then_inc(gate2, 1)
                dve.wait_ge(hot, r + 1)
                dve.wait_ge(gate2, r + 1)
                wcols = row[:, :, 2 * D:ROW].bitcast(F32)
                dve.tensor_tensor(m1[:], m1[:], g1[:].unsqueeze(2).to_broadcast([P, GB, E]), ALU.mult)
                dve.tensor_tensor(m2[:], m2[:], g2[:].unsqueeze(2).to_broadcast([P, GB, E]), ALU.mult)\
                    .then_inc(wrow, 1)
                dve.wait_ge(wrow, r + 1)
                dve.tensor_tensor(wcols, m1[:], m2[:], ALU.add).then_inc(wrow2, 1)

            def front(g, r=None):
                cosb = cosT.unsqueeze(1).to_broadcast([P, GB, P])
                sinb = sinT.unsqueeze(1).to_broadcast([P, GB, P])
                for i in range(2):
                    if r is not None or i:
                        dve.wait_ge(rope_add, 2 * g + i)
                    for half in range(2):
                        dve.wait_ge(pj_full[half], PJ * g + i + 1)
                        src = pj[half][:].rearrange("p (b t) -> p b t", b=GB)
                        dve.tensor_tensor(rope[:, 3 * half].rearrange("p (b t) -> p b t", b=GB), src, cosb, ALU.mult)
                        last = dve.tensor_tensor(rope[:, 1 + half].rearrange("p (b t) -> p b t", b=GB),
                                                 src, sinb, ALU.mult)
                        last.then_inc(pj_free[half], 1)
                if r is not None:
                    norm(3, r, x2)
                    rows_low(r)
                else:
                    weights_low2(1, wvf)
                s1 = 1 if r is None else SC[0] * r + 6
                dve.wait_ge(sc_full[0], s1)
                dve.tensor_reduce(mx1[:], sc0[:].rearrange("p (b t) -> p b t", b=GB), AX, ALU.max).then_inc(max1, 1)
                dve.wait_ge(max1, g + 1)
                dve.tensor_scalar(nm1[:], mx1[:], -ATTN_SCALE, None, ALU.mult).then_inc(neg1, 1)
                dve.wait_ge(sc_free[0], s1)
                dve.reciprocal(inv1[:], sum1[:]).then_inc(inv1_done, 1)
                if r is not None:
                    router_turned(r, SC[1] * r + 4)
                else:
                    weights_low2(2, wqf)
                dve.wait_ge(inv1_done, g + 1)
                for i, (bank_, full, free, use) in enumerate(((ov, ov_full, ov_free, OV * g), (op, op_full, op_free, OP * g))):
                    dve.wait_ge(full, use + 2)
                    for b in (2 * i, 2 * i + 1):
                        last = dve.scalar_tensor_tensor(out=x1[:, b, :], in0=bank_[:, (b % 2) * D:(b % 2 + 1) * D],
                                                        scalar=inv1[:, b:b + 1], in1=xg[:, b, :],
                                                        op0=ALU.mult, op1=ALU.add)
                    last.then_inc(free, 1)
                dve.wait_ge(ov_free, OV * g + 2)
                dve.wait_ge(op_free, OP * g + 2)
                norm(2, g, x1)
                normed(2, g, x1)
                if r is not None:
                    router(r, SC[0] * r + 6, SC[1] * r + 4)
                else:
                    dve.wait_ge(r1_hi, 1)
                    dve.scalar_tensor_tensor(out=r1l[:], in0=r1f, scalar=UP, in1=r1h[:], op0=ALU.mult,
                                             op1=ALU.subtract).then_inc(r1_lo, 1)
                low(2, g, nh[:], nl[:])
                dve.wait_ge(tpB_full, TPB * g + 3)
                dve.tensor_copy(xTl[:], tpB[:].bitcast(F16)).then_inc(tpB_free, 1)
                if r is not None:
                    choose(r, SC[0] * r + 6)

            def back(g, more):
                for n in range(8 + 5):
                    if n < 8:
                        s = n % 2
                        dve.wait_ge(sc_full[s], (SC[0] * g + 1, SC[1] * g)[s] + n // 2 + 1)
                        dve.tensor_reduce(mx2[:, s, :], sc[s][:].rearrange("p (b t) -> p b t", b=4), AX, ALU.max)\
                            .then_inc(max2, 1)
                        dve.wait_ge(max2, 8 * g + n + 1)
                        dve.tensor_scalar(nm2[:, s, :], mx2[:, s, :], -1.0, None, ALU.mult).then_inc(neg2, 1)
                    if n == 0:
                        for j in (6, 7):
                            dve.wait_ge(pj_full[j % 2], PJ * (g + 1))
                            dve.tensor_scalar(qT[:, j, :], pj[j % 2][:], DOWN, bias[:, j:j + 1],
                                              ALU.mult, ALU.add).then_inc(pj_free[j % 2], 1)
                    if 1 <= n <= 8:
                        s = (n - 1) % 2
                        dve.wait_ge(sc_free[s], (SC[0] * g + 1, SC[1] * g)[s] + (n - 1) // 2 + 1)
                        if n >= 3:
                            dve.wait_ge(norm2, 8 * g + n - 2)
                        dve.reciprocal(inv2[:, s, :], sum2[:, s, :]).then_inc(inv2_done, 1)
                    if 2 <= n < 10:
                        m = n - 2
                        full, free, src = ((tpA_full, tpA_free, tpA), (tpB_full, tpB_free, tpB))[m % 2]
                        dve.wait_ge(full, ((TPA * g + 4), (TPB * g + 3))[m % 2] + m // 2 + 1)
                        if m >= 2:
                            dve.wait_ge(ov_full, OV * g + 2 + m - 1)
                        dve.tensor_copy(pT2[:, m % 2].rearrange("p a b -> p (a b)"), src[:]).then_inc(free, 1)
                    if 3 <= n < 11:
                        m = n - 3
                        hh = 4 * (m % 2)
                        if m >= 4:
                            dve.wait_ge(op_full, OP * g + 2 + m // 2 - 1)
                        dve.wait_ge(ov_full, OV * g + 2 + m + 1)
                        dve.tensor_tensor(oT[:, (m // 2) % 2, hh:hh + 4, :],
                                          ov[:].rearrange("p (b t) -> p b t", b=4),
                                          bias[:, 2 * H + hh:2 * H + hh + 4].unsqueeze(2).to_broadcast([P, 4, P]),
                                          ALU.add).then_inc(ov_free, 1)
                    if n >= 6 and n % 2 == 0:
                        b = (n - 6) // 2
                        if b == 0:
                            dve.wait_ge(x1_bias, g + 1)
                        dve.wait_ge(op_full, OP * g + 2 + b + 1)
                        dve.tensor_tensor(x2[:, b, :], op[:, 0:D], x1[:, b, :], ALU.add).then_inc(op_free, 1)
                    if more and n in (3, 5, 8):
                        early(g + 1, (3, 5, 8).index(n))
                    if more and n in (10, 12):
                        turned(g + 1, (n - 10) // 2)
                    if n == 10 and not more:
                        weights_low(0)
                dve.wait_ge(op_free, OP * (g + 1))

            dve.wait_ge(xg_in, 16)
            norm(1, 0, xg)
            dve.wait_ge(const_in, 16)
            dve.tensor_copy(identh[:], ident).then_inc(ready, 1)
            normed(1, 0, xg)
            dve.wait_ge(w1_hi, 1)
            dve.scalar_tensor_tensor(out=w1l[:], in0=w1f, scalar=UP, in1=w1h[:], op0=ALU.mult,
                                     op1=ALU.subtract).then_inc(w1_lo, 1)
            low(1, 0, nh[:], nl[:])
            context_low(0)
            turned(0, 0)
            weights_low2(0, wkf)
            turned(0, 1)
            dve.wait_ge(table_in, 32)
            dve.tensor_copy(identb[:], ident)
            dve.tensor_copy(masks[:], cst[:, 2 * P:7 * P].rearrange("p (m k) -> p m k", m=5)).then_inc(ready, 1)
            front(0)
            with dve.Fori(0, G - 1) as g:
                back(g, True)
                front(g + 1, g)
            back(G - 1, False)
            norm(3, G - 1, x2)
            rows_low(G - 1)
            weights_low(1)
            router_turned(G - 1, LAST[1])
            weights_low(2)
            router(G - 1, *LAST)
            weights_low(3)
            choose(G - 1, LAST[0])

        @block.tensor
        def _(pe):
            def transposes(bankA, bankB, hi, lo, fullA, fullB):
                for dst, src, full in ((bankA, hi, fullA), (bankB, lo, fullB)):
                    view = dst[:].bitcast(F16)
                    for c in range(KC):
                        for b in range(GB):
                            last = pe.transpose(view[:, c * TOK + b * P:c * TOK + (b + 1) * P],
                                                src(b, c), identh[:])
                    last.then_inc(full, 1)

            def three(out, whi, wlo, xhi, xlo):
                terms = [(c, w, v) for c in range(KC) for w, v in ((whi, xhi), (whi, xlo), (wlo, xhi))]
                for i, (c, w, v) in enumerate(terms):
                    last = pe.matmul(out, w(c), v(c), start=(i == 0), stop=(i == len(terms) - 1))
                return last

            def turn_tokens(g, after=True):
                pe.wait_ge(ln[1]["hi"], g + 1)
                pe.wait_ge(ln[1]["lo"], g + 1)
                if after:
                    pe.wait_ge(tpA_free, TPA * g)
                    pe.wait_ge(tpB_free, TPB * g)
                transposes(tpA, tpB, lambda b, c: nh[:, b, c * P:(c + 1) * P],
                           lambda b, c: nl[:, b, c * P:(c + 1) * P], tpA_full, tpB_full)

            def turn_context(g):
                pe.wait_ge(tpA_free, TPA * g + 1)
                pe.wait_ge(tpB_free, TPB * g + 1)
                pe.wait_ge(c_hi, g + 1)
                pe.wait_ge(c_lo, g + 1)
                transposes(tpA, tpB, lambda b, c: ch[:, b, c * P:(c + 1) * P],
                           lambda b, c: cl[:, b, c * P:(c + 1) * P], tpA_full, tpB_full)

            def project(g, kind, js):
                for j in js:
                    pe.wait_ge(pj_free[j % 2], PJ * g + 2 + 4 * kind + j // 2)
                    if kind == 1:
                        b, n0 = j // 2, 1024 + 512 * (j % 2)
                        last = three(pj[j % 2][:],
                                     lambda c: cTh[:, c, b * P:(b + 1) * P], lambda c: cTl[:, c, b * P:(b + 1) * P],
                                     lambda c: w2h[:, c, n0:n0 + 512], lambda c: w2l[:, c, n0:n0 + 512])
                    else:
                        n0 = 1024 * kind + P * j
                        src = (cTh, cTl) if kind == 0 else (xTh, xTl)
                        last = three(pj[j % 2][:],
                                     lambda c: w2h[:, c, n0:n0 + P], lambda c: w2l[:, c, n0:n0 + P],
                                     lambda c: src[0][:, c, :], lambda c: src[1][:, c, :])
                    last.then_inc(pj_full[j % 2], 1)

            def turn_rows(r, u0, u1):
                pe.wait_ge(ln[3]["hi"], r + 1)
                pe.wait_ge(ln[3]["lo"], r + 1)
                pe.wait_ge(sc_free[0], u0)
                pe.wait_ge(sc_free[1], u1)
                transposes(sc0, sc1, lambda b, c: row[:, b, c * P:(c + 1) * P],
                           lambda b, c: row[:, b, D + c * P:D + (c + 1) * P], sc_full[0], sc_full[1])

            def router_hidden(r, u0, u1):
                pe.wait_ge(sc_free[0], u0 + 1)
                pe.wait_ge(sc_free[1], u1 + 1)
                for m in range(KC):
                    three(sc[m][:], lambda c: r1h[:, c, m * P:(m + 1) * P], lambda c: r1l[:, c, m * P:(m + 1) * P],
                          lambda c: rTh[:, c, :], lambda c: rTl[:, c, :]).then_inc(sc_full[m], 1)

            def logits(r, u0):
                pe.wait_ge(r_hid, KC * (r + 1))
                pe.wait_ge(sc_free[0], u0 + 2)
                for b in range(GB):
                    for m in range(KC):
                        last = pe.matmul(sc0[:, b * E:(b + 1) * E], xb[:, m, b * P:(b + 1) * P], rw2s[:, m, :],
                                         start=(m == 0), stop=(m == KC - 1))
                last.then_inc(sc_full[0], 1)

            def front(g, r=None):
                pe.wait_ge(tpA_free, TPA * g + 1)
                pe.wait_ge(tpB_free, TPB * g + 1)
                for i in range(4):
                    if r is None and i == 2:
                        turn_context(0)
                    if r is not None or i >= 2:
                        pe.wait_ge(pj_free[i % 2], PJ * g + i // 2)
                    three(pj[i % 2][:], lambda c: w1h[:, c, i * P:(i + 1) * P], lambda c: w1l[:, c, i * P:(i + 1) * P],
                          lambda c: xTh[:, c, :], lambda c: xTl[:, c, :]).then_inc(pj_full[i % 2], 1)
                first = ((ov, ov_full, ov_free, OV * g), (op, op_full, op_free, OP * g))
                for i, (bank_, full, free, use) in enumerate(first):
                    if r is not None:
                        pe.wait_ge(free, use)
                    for b in (2 * i, 2 * i + 1):
                        last = three(bank_[:, (b % 2) * D:(b % 2 + 1) * D],
                                     lambda c: xTh[:, c, b * P:(b + 1) * P], lambda c: xTl[:, c, b * P:(b + 1) * P],
                                     lambda c: w1h[:, c, 512:768], lambda c: w1l[:, c, 512:768])
                    last.then_inc(full, 1)
                if r is None:
                    pe.wait_ge(w2_hi, 1)
                    pe.wait_ge(w2_lo, 1)
                pe.wait_ge(tpA_free, TPA * g + 2)
                pe.wait_ge(tpB_free, TPB * g + 2)
                project(g, 0, range(4))
                pe.wait_ge(rope_add, 2 * g + 2)
                if r is None:
                    pe.wait_ge(ready, 2)
                else:
                    pe.wait_ge(sc_free[0], SC[0] * r + 5)
                pe.matmul(sc0[:], identb[:], masks[:, 0:1, :].to_broadcast([P, 4, P]), start=True, stop=True,
                          skip_group_check=True)
                for b in range(GB):
                    s = slice(b * P, (b + 1) * P)
                    for c in range(KC):
                        last = pe.matmul(sc0[:, s], qr[:, c, s], kr[:, c, s], start=False,
                                         stop=(c == KC - 1), skip_group_check=True)
                last.then_inc(sc_full[0], 1)
                project(g, 0, range(4, 8))
                if r is not None:
                    turn_rows(r, SC[0] * r + 6, SC[1] * r + 4)
                else:
                    pe.wait_ge(sc_free[0], 1)
                for b in range(GB):
                    last = pe.transpose(tpA[:, b * P:(b + 1) * P], p1[:, b, :], ident)
                last.then_inc(tpA_full, 1)
                if r is None:
                    pe.wait_ge(w2_hi, 2)
                    pe.wait_ge(w2_lo, 2)
                project(g, 1, range(1))
                pe.wait_ge(tpA_free, TPA * g + 3)
                for i, (bank_, full, free, use) in enumerate(first):
                    pe.wait_ge(free, use + 1)
                    for b in (2 * i, 2 * i + 1):
                        last = pe.matmul(bank_[:, (b % 2) * D:(b % 2 + 1) * D], pT1[:, b, :], v1[:, b, :],
                                         start=True, stop=True)
                    last.then_inc(full, 1)
                project(g, 1, range(1, 4))
                if r is not None:
                    router_hidden(r, SC[0] * r + 6, SC[1] * r + 4)
                project(g, 1, range(4, 8))
                pe.wait_ge(ln[2]["hi"], g + 1)
                pe.wait_ge(ln[2]["lo"], g + 1)
                transposes(tpA, tpB, lambda b, c: nh[:, b, c * P:(c + 1) * P],
                           lambda b, c: nl[:, b, c * P:(c + 1) * P], tpA_full, tpB_full)
                if r is not None:
                    logits(r, SC[0] * r + 6)

            def back(g, more):
                pe.wait_ge(tpA_free, TPA * g + 4)
                pe.wait_ge(tpB_free, TPB * g + 3)
                project(g, 2, range(6))
                for n in range(8 + 4):
                    if n < 8:
                        s, b, h0 = n % 2, n // 2, 4 * (n % 2)
                        t = slice(b * P, (b + 1) * P)
                        if n != 1:
                            pe.wait_ge(sc_free[s], (SC[0] * g + 1, SC[1] * g)[s] + n // 2)
                        pe.matmul(sc[s][:], identb[:],
                                  masks[:, 1 + 2 * (n % 2):3 + 2 * (n % 2), :].unsqueeze(2).to_broadcast([P, 2, 2, P]),
                                  start=True, stop=True, skip_group_check=True)
                        for i in range(4):
                            last = pe.matmul(sc[s][:, i * P:(i + 1) * P], qT[:, h0 + i, t], kT[:, h0 + i, t],
                                             start=False, stop=True, skip_group_check=True)
                        last.then_inc(sc_full[s], 1)
                    if n == 0:
                        project(g, 2, range(6, 8))
                        pe.wait_ge(pj_free[0], PJ * (g + 1))
                        pe.wait_ge(pj_free[1], PJ * (g + 1))
                    if 2 <= n < 10:
                        m = n - 2
                        dst, full, free, use = ((tpA, tpA_full, tpA_free, TPA * g + 4),
                                                (tpB, tpB_full, tpB_free, TPB * g + 3))[m % 2]
                        pe.wait_ge(norm2, 8 * g + m + 1)
                        pe.wait_ge(free, use + m // 2)
                        for i in range(4):
                            last = pe.transpose(dst[:, i * P:(i + 1) * P], pn2[:, m % 2, i, :], ident)
                        last.then_inc(full, 1)
                    if 3 <= n < 11:
                        m = n - 3
                        b, h0 = m // 2, 4 * (m % 2)
                        free, use = ((tpA_free, TPA * g + 4), (tpB_free, TPB * g + 3))[m % 2]
                        pe.wait_ge(free, use + m // 2 + 1)
                        pe.wait_ge(ov_free, OV * g + 2 + m)
                        for i in range(4):
                            h = h0 + i
                            last = pe.matmul(ov[:, i * P:(i + 1) * P], v2[:, b, h * DH:(h + 1) * DH],
                                             pT2[:, m % 2, i, :], start=True, stop=True)
                        last.then_inc(ov_full, 1)
                    if n == 10 and more:
                        turn_tokens(g + 1)
                    if n >= 5 and n % 2 == 1:
                        b = (n - 5) // 2
                        pe.wait_ge(ov_free, OV * g + 2 + 2 * b + 2)
                        pe.wait_ge(op_free, OP * g + 2 + b)
                        for h in range(H):
                            last = pe.matmul(op[:, 0:D], oT[:, b % 2, h, :], wc[:, h, :],
                                             start=(h == 0), stop=(h == H - 1))
                        last.then_inc(op_full, 1)
                if more:
                    turn_context(g + 1)

            pe.wait_ge(ready, 1)
            turn_tokens(0, after=False)
            pe.wait_ge(w1_hi, 1)
            pe.wait_ge(w1_lo, 1)
            front(0)
            pe.wait_ge(w2_hi, 3)
            pe.wait_ge(w2_lo, 3)
            pe.wait_ge(wc_in, 16)
            pe.wait_ge(r_in, 64)
            pe.wait_ge(r1_hi, 2)
            pe.wait_ge(r1_lo, 1)
            with pe.Fori(0, G - 1) as g:
                back(g, True)
                front(g + 1, g)
            back(G - 1, False)
            turn_rows(G - 1, *LAST)
            router_hidden(G - 1, *LAST)
            logits(G - 1, LAST[0])


SLOTS = 3
TILES = (B * L * 2 + E * (P - 1)) // P
SKIP = 8192
MC = HID // P
RW = ROW // 2


CONSTS = (("before", P), ("iota_p", P), ("iota_t", TILES), ("steps", B), ("less", E * E), ("token", B), ("iota8", E),
          ("ident", P))


def expert_phase(nc, shared, dram, out):
    (eb1, ew2, eb2) = dram
    base, eidx, rows, cols, identh, picked = (shared[k] for k in ("base", "eidx", "rows", "cols", "identh", "picked"))
    up_f, up_h, up_l, up_hi, up_lo, row_out = (shared[k] for k in ("up_f", "up_h", "up_l", "up_hi", "up_lo", "row_out"))
    before, iota_p, iota_t, steps, less, token, iota8 = (cols[k] for k, _ in CONSTS[:7])
    with ExitStack() as ctx:
        def sb(name, shape, dt=F32):
            return ctx.enter_context(nc.sbuf_tensor(name, shape, dt))

        def bank(name):
            return ctx.enter_context(nc.psum_tensor(name, [P, 512], F32))

        def sem(name):
            return ctx.enter_context(nc.semaphore(name))

        down = sb("down", [P, E, MC, D])
        b1 = sb("b1", [P, E * MC])
        b2f, b2h, b2l = sb("b2f", [2, E * D]), sb("b2h", [2, E * D], F16), sb("b2l", [2, E * D], F16)
        ones2 = sb("ones2", [2, P], F16)
        hot = sb("hot", [P, 2, B, E])
        both = sb("both", [P, B, E], F16)
        beforeh, onesh = sb("beforeh", [P, P], F16), sb("onesh", [P, P], F16)
        iotah = sb("iotah", [P, P], F16)
        over = sb("over", [P, E, B])
        ntiles, mixed, first, last_t, first_s = (sb("ntiles", [P, E]), sb("mixed", [P, E, E]), sb("first", [P, E]),
                                                 sb("last_t", [P, E]), sb("first_s", [P, E]))
        count = sb("count", [P, E])
        place, placed = sb("place", [P, B, E]), sb("placed", [P, 2, B, E])
        slot, sloti = sb("slot", [P, 2 * B]), sb("sloti", [P, 2 * B], mybir.dt.int32)
        ti, ri = sb("ti", [P, 2 * B], mybir.dt.int32), sb("ri", [P, 2 * B], mybir.dt.int32)
        tf, rf = sb("tf", [P, 2 * B], F16), sb("rf", [P, 2 * B])
        hot_r = sb("hot_r", [P, 2 * B, P], F16)
        hot_t = sb("hot_t", [P, 2 * B, TILES], F16)
        signed = sb("signed", [P, 2, B])
        inv, mag, size, isneg, iszero, dsum = (sb(n, [P, TILES]) for n in ("inv", "mag", "size", "isneg", "iszero", "dsum"))
        src_row, dst_row = sb("src_row", [P, TILES], U32), sb("dst_row", [P, TILES], U32)
        below, texp = sb("below", [P, TILES, E]), sb("texp", [P, TILES])
        texp_i = sb("texp_i", [P, TILES], mybir.dt.int32)
        got = [sb(f"got{s}", [P, RW], U32) for s in range(SLOTS)]
        xt = [sb(f"xt{s}", [P, 4, P], F16) for s in range(SLOTS)]
        gate = [sb(f"gate{s}", [P, 1]) for s in range(SLOTS)]
        hT = [sb(f"hT{s}", [P, MC, P]) for s in range(SLOTS)]
        ys = [sb(f"ys{s}", [P, D]) for s in range(SLOTS)]
        z = up_f[:].rearrange("p e n -> p (e n)").rearrange("p (k b d) -> p k b d", k=2, b=B)

        rank = bank("rank")
        table = bank("table")
        tp = rank
        hb = [bank(f"h{s}") for s in range(SLOTS)]
        yb = [table, bank("y1"), bank("y2")]

        (down_in, small_in, b2_lo_in) = (sem(n) for n in ("down_in", "small_in", "b2_lo_in"))
        b2_up, b2_hi, b2_lo, hot_t_done = (sem(n) for n in ("b2_up", "b2_hi", "b2_lo", "hot_t_done"))
        row_ones = sem("row_ones")
        chain = sem("chain")
        rank_full, table_full, idx_done, texp_done = (sem(n) for n in ("rank_full", "table_full", "idx_done", "texp_done"))
        gathered = [sem(f"gathered{s}") for s in range(SLOTS)]
        scattered = [sem(f"scattered{s}") for s in range(SLOTS)]
        tp_full, tp_free = sem("tp_full"), sem("tp_free")
        h_full, silu_done = sem("h_full"), sem("silu_done")
        y_full, y_free = sem("y_full"), sem("y_free")
        z_in, out_done = [sem(f"z_in{g}") for g in range(G)], sem("out_done")
        summed, fin_done = sem("summed"), sem("fin_done")

        picked_t = picked.rearrange("(k p g b) d -> k g p b d", k=2, b=GB, g=G)
        out_t = out.rearrange("(g b) p d -> g p b d", b=GB)

        block = ctx.enter_context(nc.Block())

        @block.sync
        def _(sp):
            sp.dma_start(b1[:], eb1).then_inc(small_in, 16)
            sp.dma_start(b2f[:], eb2.rearrange("(a e) d -> a (e d)", a=1).broadcast_to([2, E * D])).then_inc(small_in, 16)
            sp.dma_start(down[:].rearrange("p e m d -> p (e m d)"), ew2).then_inc(down_in, 16)
            sp.wait_ge(b2_lo, 1)
            sp.dma_start(b2h[1:2, :], b2l[1:2, :]).then_inc(b2_lo_in, 16)
            for s in range(SLOTS):
                sp.wait_ge(scattered[s], 16 * (TILES // SLOTS))
            for g in range(G):
                sp.dma_start(z[:, 0, g * GB:(g + 1) * GB], picked_t[0, g]).then_inc(z_in[g], 16)
            for g in range(0, G, 2):
                sp.wait_ge(fin_done, g + 1)
                sp.dma_start(out_t[g], z[:, 0, g * GB:(g + 1) * GB]).then_inc(out_done, 16)
            sp.wait_ge(out_done, 16 * G)

        @block.gpsimd
        def _(pool):
            def gather(t):
                s = t % SLOTS
                if t >= SLOTS:
                    pool.wait_ge(tp_free, t - SLOTS + 1)
                pool.indirect_dma_start(got[s][:], None, rows,
                                        bass.IndirectOffsetOnAxis(src_row[:, t:t + 1], 0),
                                        bounds_check=B * L - 1, oob_is_err=False).then_inc(gathered[s], 16)

            def scatter(t):
                s = t % SLOTS
                pool.wait_ge(y_free, t + 2)
                pool.indirect_dma_start(picked, bass.IndirectOffsetOnAxis(dst_row[:, t:t + 1], 0), ys[s][:], None,
                                        bounds_check=2 * B * L - 1, oob_is_err=False).then_inc(scattered[s], 16)

            pool.wait_ge(b2_hi, 1)
            pool.tensor_tensor(b2l[:], b2f[:], b2h[:], ALU.subtract).then_inc(b2_lo, 1)
            pool.wait_ge(row_out, 16 * G + 16)
            pool.wait_ge(idx_done, 1)
            for t in range(TILES):
                gather(t)
                if t >= SLOTS:
                    scatter(t - SLOTS)
            for t in range(TILES - SLOTS, TILES):
                scatter(t)

        @block.scalar
        def _(act):
            act.wait_ge(small_in, 32)
            act.activation(b2f[:], b2f[:], ACT.Copy, scale=UP).then_inc(b2_up, 1)
            act.wait_ge(b2_up, 1)
            act.activation(b2h[:], b2f[:], ACT.Copy).then_inc(b2_hi, 1)
            act.preload_act_table(ACT.Silu)
            act.wait_ge(texp_done, 1)
            with act.Fori(0, TILES // SLOTS) as i:
                for s in range(SLOTS):
                    e = act.value_load(texp_i[0:1, bass.ds(i * SLOTS + s, 1)], min_val=0, max_val=E - 1)
                    act.wait_ge(h_full, i * SLOTS + s + 1)
                    for m in range(MC):
                        last = act.activation(hT[s][:, m, :], hb[s][:, m * P:(m + 1) * P], ACT.Silu,
                                              bias=b1[:, bass.ds(e * MC + m, 1)], scale=DOWN)
                    last.then_inc(silu_done, 1)
            for s in range(SLOTS):
                act.wait_ge(scattered[s], 16 * (TILES // SLOTS))
            for g in range(G):
                act.dma_start(z[:, 1, g * GB:(g + 1) * GB], picked_t[1, g]).then_inc(z_in[g], 16)
            for g in range(1, G, 2):
                act.wait_ge(fin_done, g + 1)
                act.dma_start(out_t[g], z[:, 0, g * GB:(g + 1) * GB]).then_inc(out_done, 16)

        @block.vector
        def _(dve):
            step = [0]

            def done(ins):
                step[0] += 1
                ins.then_inc(chain, 1)
                dve.wait_ge(chain, step[0])

            dve.sem_inc(y_free, 1)
            dve.tensor_copy(beforeh[:], before)
            dve.memset(onesh[:], 1.0)
            for k in range(2):
                ins = dve.tensor_tensor(hot[:, k], iota8.unsqueeze(1).to_broadcast([P, B, E]),
                                        eidx[:, :, k:k + 1].to_broadcast([P, B, E]), ALU.is_equal)
            done(ins)
            done(dve.tensor_tensor(both[:], hot[:, 0], hot[:, 1], ALU.add))
            dve.memset(ones2[:], 1.0 / UP)
            dve.tensor_copy(iotah[:], iota_p)
            for k in range(2):
                ins = dve.tensor_scalar(signed[:, k, :], token, 1.0 - 2.0 * k, None, ALU.mult)
            done(ins)
            dve.wait_ge(rank_full, 1)
            done(dve.tensor_copy(count[:], rank[:, B * E:(B + 1) * E]))
            done(dve.tensor_tensor(over[:], count[:].unsqueeze(2).to_broadcast([P, E, B]),
                                   steps.unsqueeze(1).to_broadcast([P, E, B]), ALU.is_gt))
            done(dve.tensor_reduce(ntiles[:], over[:], AX, ALU.add))
            done(dve.tensor_tensor(mixed[:], ntiles[:].unsqueeze(1).to_broadcast([P, E, E]),
                                   less.rearrange("p (a b) -> p a b", a=E), ALU.mult))
            done(dve.tensor_reduce(first[:], mixed[:], AX, ALU.add))
            done(dve.tensor_scalar(first_s[:], first[:], float(P), None, ALU.mult))
            done(dve.tensor_tensor(place[:], rank[:, 0:B * E].rearrange("p (b e) -> p b e", b=B),
                                   first_s[:].unsqueeze(1).to_broadcast([P, B, E]), ALU.add))
            done(dve.tensor_tensor(placed[:].rearrange("p k b e -> p k (b e)"),
                                   hot[:].rearrange("p k b e -> p k (b e)"),
                                   place[:].rearrange("p b e -> p (b e)").unsqueeze(1).to_broadcast([P, 2, B * E]),
                                   ALU.mult))
            done(dve.tensor_reduce(slot[:], placed[:].rearrange("p k b e -> p (k b) e"), AX, ALU.add))
            done(dve.tensor_copy(sloti[:], slot[:]))
            dve.tensor_scalar(ti[:], sloti[:], 7, None, ALU.arith_shift_right)
            done(dve.tensor_scalar(ri[:], sloti[:], P - 1, None, ALU.bitwise_and))
            dve.tensor_copy(tf[:], ti[:])
            done(dve.tensor_copy(rf[:], ri[:]))
            dve.tensor_tensor(hot_t[:], iotah[:, 0:TILES].unsqueeze(1).to_broadcast([P, 2 * B, TILES]),
                              tf[:].unsqueeze(2).to_broadcast([P, 2 * B, TILES]), ALU.is_equal).then_inc(hot_t_done, 1)
            for q in range(2 * B):
                ins = dve.tensor_scalar(hot_r[:, q, :], iotah[:], rf[:, q:q + 1],
                                        signed[:].rearrange("p k b -> p (k b)")[:, q:q + 1], ALU.is_equal, ALU.mult)
                if q % 8 == 7:
                    ins.then_inc(row_ones, 1)
            done(dve.tensor_tensor(last_t[:], first[:], ntiles[:], ALU.add))
            done(dve.tensor_tensor(below[:], last_t[:].unsqueeze(1).to_broadcast([P, TILES, E]),
                                   iota_t.unsqueeze(2).to_broadcast([P, TILES, E]), ALU.is_le))
            done(dve.tensor_reduce(texp[:], below[:], AX, ALU.add))
            done(dve.tensor_scalar(texp[:], texp[:], float(E - 1), None, ALU.min))
            done(dve.tensor_copy(texp_i[:], texp[:]))
            dve.sem_inc(texp_done, 1)
            dve.wait_ge(table_full, 1)
            done(dve.tensor_copy(inv[:], table[:, 0:TILES]))
            done(dve.scalar_tensor_tensor(out=mag[:], in0=inv[:], scalar=-1.0, in1=inv[:], op0=ALU.mult, op1=ALU.max))
            dve.tensor_scalar(size[:], mag[:], -1.0, None, ALU.add)
            dve.tensor_scalar(isneg[:], inv[:], 0.0, float(B * L), ALU.is_lt, ALU.mult)
            done(dve.tensor_scalar(iszero[:], inv[:], 0.0, float(SKIP), ALU.is_equal, ALU.mult))
            dve.tensor_scalar(src_row[:], size[:], 0.0, None, ALU.max)
            done(dve.tensor_tensor(dsum[:], size[:], isneg[:], ALU.add))
            dve.tensor_tensor(dst_row[:], dsum[:], iszero[:], ALU.add).then_inc(idx_done, 1)
            def take(t, s, after=True):
                e = dve.value_load(texp_i[0:1, bass.ds(t, 1)], min_val=0, max_val=E - 1)
                dve.wait_ge(tp_full, t + 1)
                dve.tensor_copy(xt[s][:].rearrange("p a b -> p (a b)"), tp[:].bitcast(F16)[:, 0:4 * P])
                if after:
                    dve.wait_ge(y_free, t - SLOTS + 2)
                dve.tensor_copy(gate[s][:], got[s][:].bitcast(F32)[:, bass.ds(e + D, 1)]).then_inc(tp_free, 1)

            def weigh(t, s, n, after=True):
                if after:
                    dve.wait_ge(scattered[s], 16 * n)
                dve.wait_ge(y_full, t + 1)
                dve.tensor_scalar(ys[s][:], yb[s][:, 0:D], gate[s][:], None, ALU.mult).then_inc(y_free, 1)

            take(0, 0, after=False)
            take(1, 1, after=False)
            for s in range(SLOTS):
                take(s + 2, (s + 2) % SLOTS, after=s > 0)
                weigh(s, s, 0, after=False)
            with dve.Fori(1, TILES // SLOTS - 1) as i:
                for s in range(SLOTS):
                    t = i * SLOTS + s
                    take(t + 2, (s + 2) % SLOTS)
                    weigh(t, s, i)
            t = TILES - SLOTS
            take(t + 2, 2)
            for s in range(SLOTS):
                weigh(t + s, s, TILES // SLOTS - 1)

            for g in range(G):
                b = slice(g * GB, (g + 1) * GB)
                dve.wait_ge(z_in[g], 32)
                dve.tensor_tensor(z[:, 0, b], z[:, 0, b], z[:, 1, b], ALU.add).then_inc(summed, 1)
                dve.wait_ge(summed, g + 1)
                dve.tensor_tensor(z[:, 0, b], z[:, 0, b], base[:, b, :], ALU.add).then_inc(fin_done, 1)

        @block.tensor
        def _(pe):
            pe.wait_ge(chain, 2)
            flat = both[:].rearrange("p b e -> p (b e)")
            pe.matmul(rank[:, 0:B * E], beforeh[:], flat, start=True, stop=True, skip_group_check=True)
            for b in range(B):
                n = B - b
                ins = pe.matmul(rank[:, (b + 1) * E:(B + 1) * E].rearrange("p (n e) -> p n e", n=n), onesh[:],
                                both[:, b:b + 1, :].to_broadcast([P, n, E]), start=False, stop=True,
                                skip_group_check=True)
            ins.then_inc(rank_full, 1)
            pe.wait_ge(hot_t_done, 1)
            for q in range(2 * B):
                if q % 8 == 0:
                    pe.wait_ge(row_ones, q // 8 + 1)
                ins = pe.matmul(table[:, 0:TILES], hot_r[:, q, :], hot_t[:, q, :], start=(q == 0), stop=(q == 2 * B - 1))
            ins.then_inc(table_full, 1)

            def turn(t, s, n):
                pe.wait_ge(gathered[s], 16 * n)
                pe.wait_ge(tp_free, t)
                g = got[s][:].bitcast(F16)
                v = tp[:].bitcast(F16)
                for j in range(4):
                    ins = pe.transpose(v[:, j * P:(j + 1) * P], g[:, j * P:(j + 1) * P], identh[:])
                ins.then_inc(tp_full, 1)

            def hidden(t, s):
                e = pe.value_load(texp_i[0:1, bass.ds(t, 1)], min_val=0, max_val=E - 1)
                pe.wait_ge(tp_free, t + 1)
                for m in range(MC):
                    k = 0
                    for c in range(KC):
                        for w, x in ((up_h, c), (up_h, KC + c), (up_l, c)):
                            lhs = w[:, bass.ds(e, 1), c, m * P:(m + 1) * P].rearrange("p a n -> p (a n)")
                            ins = pe.matmul(hb[s][:, m * P:(m + 1) * P], lhs, xt[s][:, x, :],
                                            start=(k == 0), stop=(k == 3 * KC - 1))
                            k += 1
                ins.then_inc(h_full, 1)
                return e

            def outer(t, s, e, first):
                pe.wait_ge(silu_done, t + 1)
                if not first:
                    pe.wait_ge(y_free, t - SLOTS + 2)
                for m in range(MC):
                    pe.matmul(yb[s][:, 0:D], hT[s][:, m, :],
                              down[:, bass.ds(e, 1), m, :].rearrange("p a n -> p (a n)"), start=(m == 0), stop=False)
                ins = pe.matmul(yb[s][:, 0:D], ones2[:], b2h[:, bass.ds(e * D, D)], start=False, stop=True)
                ins.then_inc(y_full, 1)

            turn(0, 0, 1)
            pe.wait_ge(up_hi, 4)
            pe.wait_ge(up_lo, 4)
            pe.wait_ge(down_in, 16)
            pe.wait_ge(b2_lo_in, 16)

            e0 = hidden(0, 0)
            turn(1, 1, 1)
            e1 = hidden(1, 1)
            turn(2, 2, 1)
            outer(0, 0, e0, True)
            e2 = hidden(2, 2)
            turn(3, 0, 2)
            outer(1, 1, e1, True)
            with pe.Fori(1, TILES // SLOTS - 1) as i:
                t = i * SLOTS
                ep = pe.value_load(texp_i[0:1, bass.ds(t - 1, 1)], min_val=0, max_val=E - 1)
                for s in range(SLOTS):
                    e = hidden(t + s, s)
                    turn(t + s + 1, (s + 1) % SLOTS, i + 1 if s < 2 else i + 2)
                    outer(t + s - 1, (s + 2) % SLOTS, ep, False)
                    ep = e
            t = TILES - SLOTS
            n = TILES // SLOTS
            ep = pe.value_load(texp_i[0:1, t - 1:t], min_val=0, max_val=E - 1)
            for s in range(SLOTS):
                e = hidden(t + s, s)
                if s < 2:
                    turn(t + s + 1, s + 1, n)
                outer(t + s - 1, (s + 2) % SLOTS, ep, False)
                ep = e
            outer(t + 2, 2, ep, False)


def extra_data(np, n, data):
    f = np.float32
    p = np.arange(P)
    row = lambda v: np.tile(np.asarray(v, f), (P, 1))
    data["ew1"] = n["L0_ffn_ew1"].reshape(E, KC, P, HID).transpose(2, 0, 1, 3).reshape(P, E, KC * HID)
    data["eb1"] = n["L0_ffn_eb1"].reshape(E, MC, P).transpose(2, 0, 1).reshape(P, E * MC)
    data["ew2"] = n["L0_ffn_ew2"].reshape(E, MC, P, D).transpose(2, 0, 1, 3).reshape(P, E * MC * D)
    data["eb2"] = n["L0_ffn_eb2"]
    data["disp"] = np.concatenate([
        (p[:, None] < p[None, :]).astype(f), row(p), row(np.arange(TILES)), row(P * np.arange(B)),
        row((np.arange(E)[None, :] < np.arange(E)[:, None]).reshape(-1)),
        (np.arange(B)[None, :] + B * p[:, None] + 1).astype(f), row(np.arange(E)), np.eye(P, dtype=f)], axis=1)


def build(nc, a, out):
    shared = {"rows": nc.dram_tensor("rows", [B * L, ROW // 2], U32, kind="Internal").ap(),
              "picked": nc.dram_tensor("picked", [2 * B * L, D], F32, kind="Internal").ap()}
    with ExitStack() as ctx:
        for name, shape, dt in (("base", [P, B, D], F32), ("eidx", [P, B, 2], F32),
                                ("dc", [P, sum(n for _, n in CONSTS)], F32), ("identh", [P, P], F16),
                                ("up_f", [P, E, KC * HID], F32), ("up_h", [P, E, KC, HID], F16),
                                ("up_l", [P, E, KC, HID], F16)):
            shared[name] = ctx.enter_context(nc.sbuf_tensor(name, shape, dt))
        for name in ("up_hi", "up_lo", "row_out"):
            shared[name] = ctx.enter_context(nc.semaphore(name))
        shared["up_in"] = [ctx.enter_context(nc.semaphore(f"up_in{i}")) for i in range(4)]
        at, shared["cols"] = 0, {}
        for name, n in CONSTS:
            shared["cols"][name] = shared["dc"][:, at:at + n]
            at += n
        attention_phase(nc, shared, tuple(a[k] for k in ("x", "ctx", "w1", "w2", "wc", "xbias", "bc", "rw1", "rb1", "rw2",
                                                         "rb2", "consts", "disp", "ew1")))
        expert_phase(nc, shared, tuple(a[k] for k in ("eb1", "ew2", "eb2")), out)


def shape_constants(np):
    f = np.float32
    i = np.arange(D // 2, dtype=f)
    theta = np.power(f(10000.0), (f(-2.0) * (i - f(1.0)) / f(D)).astype(f)).astype(f)
    ang = (np.arange(L, dtype=f)[:, None] * theta[None, :]).astype(f)
    q = np.arange(L)[:, None]
    k = np.arange(L)[None, :]
    masks = [np.where(k <= q, 0.0, NEG)]
    for d in (1, 2, 4, 8):
        off = k - q
        ok = (off % d == 0) & (off // d >= -((WIN - 1) // 2)) & (off // d <= WIN - 1 - (WIN - 1) // 2)
        masks.append(np.where(ok, 0.0, NEG))
    return np.concatenate([np.cos(ang).T, np.sin(ang).T] + masks, axis=1).astype(f)


def kernel(**inputs):
    import numpy as np
    import concourse.bacc as bacc
    from concourse.bass_utils import run_bass_kernel_spmd

    def chunks(a):
        return a.reshape(KC, P, -1).transpose(1, 0, 2)

    n = {k: np.asarray(v) for k, v in inputs.items()}
    wq, wk, wv = n["L0_attn_w_q"], n["L0_attn_w_k"], n["L0_attn_w_v"]
    data = {
        "x": n["x"],
        "ctx": n["ctx_1024"],
        "w1": chunks(np.concatenate([wq[0::2], wq[1::2], wk[0::2], wk[1::2], wv], axis=0).T),
        "w2": chunks(np.concatenate([n["L0_xattn_" + w].reshape(H * DH, D) for w in ("Wk", "Wv", "Wq")], axis=0).T),
        "wc": n["L0_xattn_Wc"].T.reshape(H, DH, D).transpose(1, 0, 2),
        "xbias": np.concatenate([n["L0_xattn_" + w].T for w in ("bq", "bk", "bv")], axis=1),
        "bc": n["L0_xattn_bc"],
        "rw1": chunks(n["L0_ffn_rw1"]),
        "rb1": n["L0_ffn_rb1"].reshape(KC, P).T,
        "rw2": chunks(n["L0_ffn_rw2"]),
        "rb2": n["L0_ffn_rb2"],
        "consts": shape_constants(np),
    }
    extra_data(np, n, data)
    nc = bacc.Bacc("TRN2", target_bir_lowering=False, num_devices=1)
    arrays, aps = {}, {}
    for name, a in data.items():
        arrays["in_" + name] = np.ascontiguousarray(a)
        aps[name] = nc.dram_tensor("in_" + name, a.shape, mybir.dt.from_np(a.dtype), kind="ExternalInput").ap()
    out = nc.dram_tensor("out", [B, L, D], F32, kind="ExternalOutput").ap()
    build(nc, aps, out)
    r = run_bass_kernel_spmd(nc, [arrays], core_ids=[0])
    return r.results[0]["out"]
```

```python
from contextlib import ExitStack

import numpy as np

import concourse.bass as bass
from concourse import mybir

F32 = mybir.dt.float32
F16 = mybir.dt.float16
BF16 = mybir.dt.bfloat16
U32 = mybir.dt.uint32
ALU = mybir.AluOpType
ACT = mybir.ActivationFunctionType
AX = mybir.AxisListType.X

P = 128
B, L, D = 16, 128, 256
GB = 4
G = B // GB
TOK = GB * L
KC = D // P
H, DH = 8, 128
DILATIONS = (1, 1, 2, 2, 4, 4, 8, 8)
WIN = 64
E, HID = 8, 512
MC = HID // P
EPS = 1e-5
NEG = -1e30
UP = 256.0
DOWN = 1.0 / (UP * UP)
MID = 16.0
MID_DOWN = 1.0 / (MID * UP)
ATTN_SCALE = DOWN * DOWN / float(D) ** 0.5
ROW = 2 * D + 2 * E


def bc(ap, shape):
    return ap.to_broadcast(shape)


class Room:

    def __init__(self, ap):
        self.ap, self.at = ap, 0

    def take(self, a, b):
        view = self.ap[:, self.at:self.at + a * b].rearrange("p (a b) -> p a b", a=a)
        self.at += a * b
        assert self.at <= self.ap.shape[1]
        return view


def attention_phase(nc, shared, dram, debug_out=None):
    (x, ctxt, w1a, w2a, wca, xbias, bcd, rw1, rb1, rw2, rb2, consts, disp, ew1, ew2) = dram
    base, eidx, rows, cols, dc, identh = (shared[k] for k in ("base", "eidx", "rows", "cols", "dc", "identh"))
    up_f, up_h, up_l, up_in, up_hi, up_lo, row_out = (
        shared[k] for k in ("up_f", "up_h", "up_l", "up_in", "up_hi", "up_lo", "row_out"))
    down, down_in, down_up, down_hi, down_lo = (
        shared[k] for k in ("down", "down_in", "down_up", "down_hi", "down_lo"))
    row, ge, gs, g1, g2, m1, m2 = (shared[k] for k in ("row", "ge", "gs", "g1", "g2", "m1", "m2"))
    ident, iota8 = cols["ident"], cols["iota8"]
    with ExitStack() as ctx:
        def sb(name, shape, dt=F32):
            return ctx.enter_context(nc.sbuf_tensor(name, shape, dt))

        def bank(name):
            return ctx.enter_context(nc.psum_tensor(name, [P, 512], F32))

        def sem(name):
            return ctx.enter_context(nc.semaphore(name))

        room = Room(up_f[:].rearrange("p e n -> p (e n)").bitcast(F16))
        w2h, w2l = room.take(KC, 3072), room.take(KC, 3072)
        w1h, w1l = room.take(KC, 768), room.take(KC, 768)
        ch = room.take(GB, D)
        r1h, r1l = sb("r1h", [P, KC, D], F16), sb("r1l", [P, KC, D], F16)
        wch, wcl = sb("wch", [P, H, D], F16), sb("wcl", [P, H, D], F16)
        rw2s = sb("rw2s", [P, KC, E])
        rb1s, rb1half = sb("rb1s", [P, KC]), sb("rb1half", [P, KC])
        rb2s = sb("rb2s", [P, E])
        bias = sb("bias", [P, 3 * H])
        bcs = sb("bcs", [P, D])
        cst = sb("cst", [P, 2 * P + 5 * P])
        cosT = cst[:, 0:P]
        sinT = cst[:, P:2 * P]
        masks = sb("masks", [P, 5, P], BF16)
        identb = sb("identb", [P, P], BF16)
        nhalf = sb("nhalf", [P, GB])
        room = Room(up_l[:].rearrange("p e c n -> p (e c n)").bitcast(F32))
        xg, cg = sb("xg", [P, GB, D]), room.take(GB, D)
        qr, kr, v1 = room.take(KC, TOK), room.take(KC, TOK), room.take(GB, D)
        xn = sb("xn", [P, GB, D])
        room = Room(up_h[:].rearrange("p e c n -> p (e c n)"))
        xTh, xTl, cTh, cTl = (room.take(KC, TOK) for _ in range(4))
        nh, nl, cl = (room.take(GB, D) for _ in range(3))
        stats, mv = sb("stats", [P, GB, 6]), sb("mv", [P, GB, 2])
        veps, rstd, rstd_up = sb("veps", [P, GB]), sb("rstd", [P, GB]), sb("rstd_up", [P, GB])
        rope = sb("rope", [P, 4, TOK])
        p1, pT1 = sb("p1", [P, GB, P]), sb("pT1", [P, GB, P])
        mx1, nm1, sum1, inv1 = (sb(n, [P, GB]) for n in ("mx1", "nm1", "sum1", "inv1"))
        room = Room(down[:].rearrange("p e m k d -> p (e m k d)").bitcast(F32))
        kT, qT = room.take(H, TOK), room.take(H, TOK)
        v2 = sb("v2", [P, GB, H * DH])
        p2, pn2, pT2 = (sb(n, [P, 2, 4, P]) for n in ("p2", "pn2", "pT2"))
        mx2, nm2, sum2, inv2 = (sb(n, [P, 2, 4]) for n in ("mx2", "nm2", "sum2", "inv2"))
        oTh, oTl = sb("oTh", [P, 2, H, P], F16), sb("oTl", [P, 2, H, P], F16)
        x1, x2 = sb("x1", [P, GB, D]), sb("x2", [P, GB, D])
        rTh, rTl = sb("rTh", [P, KC, TOK], F16), sb("rTl", [P, KC, TOK], F16)
        xb, th = rope[:, 0:2, :], rope[:, 2:4, :]
        lg, mx8 = sb("lg", [P, GB, E]), sb("mx8", [P, GB, E])
        ix8 = sb("ix8", [P, GB, E], U32)
        gd = sb("gd", [P, GB])
        ixf = sb("ixf", [P, GB, 2])

        wcf = qT[:, 4:8, :].rearrange("p a b -> p (a b)").rearrange("p (h d) -> p h d", h=H)
        w1f = kT[:, 0:3, :].rearrange("p a b -> p (a b)").rearrange("p (c n) -> p c n", c=KC)
        wkf = v2[:, 0:2, :]
        wvf = v2[:, 2:4, :]
        r1f = x2[:, 0:2, :]
        wqf = qT[:, 0:4, :].rearrange("p a b -> p (a b)").rearrange("p (c n) -> p c n", c=KC)

        tpA, tpB, pj0, pj1, sc0, sc1, ov, op = (
            bank(n) for n in ("tpA", "tpB", "pj0", "pj1", "sc0", "sc1", "ov", "op"))
        pj, sc = (pj0, pj1), (sc0, sc1)
        tpA_full, tpA_free = sem("tpA_full"), sem("tpA_free")
        tpB_full, tpB_free = sem("tpB_full"), sem("tpB_free")
        pj_full, pj_free = (sem("pj0_full"), sem("pj1_full")), (sem("pj0_free"), sem("pj1_free"))
        sc_full, sc_free = (sem("sc0_full"), sem("sc1_full")), (sem("sc0_free"), sem("sc1_free"))
        ov_full, ov_free = sem("ov_full"), sem("ov_free")
        op_full, op_free = sem("op_full"), sem("op_free")
        TPA, TPB, PJ, SC, OV, OP = 8, 7, 18, (8, 6), 2, 6
        PROJ = 14
        HALVES = (slice(0, GB // 2), slice(GB // 2, GB))
        LAST = ((("sc", SC[0] * G - 3), ("sc", SC[1] * G - 2)), (("pj", PJ * G), ("pj", PJ * G)))

        const_in, w1_in, wk_in, wv_in, wq_in = (sem(n) for n in ("const_in", "w1_in", "wk_in", "wv_in", "wq_in"))
        wc_in, r_in, xg_in, cg_in, table_in, bc_in = (
            sem(n) for n in ("wc_in", "r_in", "xg_in", "cg_in", "table_in", "bc_in"))
        ready, nhalf_set = sem("ready"), sem("nhalf_set")
        last_tanh, last_hid = sem("last_tanh"), sem("last_hid")
        banks = {"sc": (sc, sc_full, sc_free), "pj": (pj, pj_full, pj_free)}
        w1_hi, w1_lo, w2_hi, w2_lo, r1_hi, r1_lo = (
            sem(n) for n in ("w1_hi", "w1_lo", "w2_hi", "w2_lo", "r1_hi", "r1_lo"))
        ln = {k: {s: sem(f"ln{k}_{s}") for s in ("stats", "aggr", "var", "pow", "rstd", "xn", "hi", "lo")}
              for k in (1, 2, 3)}
        c_hi, c_lo = sem("c_hi"), sem("c_lo")
        rope_add = sem("rope_add")
        max1, neg1, inv1_done, x1_bias = (
            sem(n) for n in ("max1", "neg1", "inv1_done", "x1_bias"))
        max2, neg2, inv2_done, norm2, x2_done = (
            sem(n) for n in ("max2", "neg2", "inv2_done", "norm2", "x2_done"))
        base_done, r_tanh, r_xb, r_hid = (sem(n) for n in ("base_done", "r_tanh", "r_xb", "r_hid"))
        lg_done, top8, top8i, gdiff, gexp, gsum, gate1, gate2, ixf_done, hot, wrow, wrow2 = (
            sem(n) for n in ("lg_done", "top8", "top8i", "gdiff", "gexp", "gsum", "gate1", "gate2",
                             "ixf_done", "hot", "wrow", "wrow2"))
        wc_hi, wc_lo, bv_full, bc_done, o_hi = (sem(n) for n in ("wc_hi", "wc_lo", "bv_full", "bc_done", "o_hi"))
        kept, dbg, waited = sem("kept"), sem("dbg"), sem("waited")

        x_t = x.rearrange("(g b) p d -> g p b d", b=GB)
        c_t = ctxt.rearrange("(g b) p d -> g p b d", b=GB)
        rows_t = rows.rearrange("(p g b) w -> g p b w", b=GB, g=G)

        block = ctx.enter_context(nc.Block())


        @block.sync
        def _(sp):
            sp.sem_inc(row_out, 16)
            sp.dma_start(xg[:], x_t[0]).then_inc(xg_in, 16)
            sp.dma_start(w1f, w1a).then_inc(w1_in, 16)
            sp.dma_start(dc[:], disp).then_inc(const_in, 16)
            sp.dma_start(cg[:], c_t[0]).then_inc(cg_in, 16)
            sp.dma_start(wkf, w2a[:, :, 0:1024]).then_inc(wk_in, 16)
            sp.dma_start(cst[:], consts).then_inc(table_in, 16)
            sp.dma_start(bias[:], xbias).then_inc(table_in, 16)
            sp.dma_start(wvf, w2a[:, :, 1024:2048]).then_inc(wv_in, 16)
            sp.dma_start(wqf, w2a[:, :, 2048:3072]).then_inc(wq_in, 16)
            sp.dma_start(bcs[:], bcd.rearrange("(a n) -> a n", a=1).broadcast_to([P, D])).then_inc(bc_in, 16)
            sp.dma_start(wcf, wca).then_inc(wc_in, 16)
            sp.dma_start(r1f, rw1).then_inc(r_in, 16)
            sp.dma_start(rw2s[:], rw2).then_inc(r_in, 16)
            sp.dma_start(rb1s[:], rb1).then_inc(r_in, 16)
            sp.dma_start(rb2s[:], rb2.rearrange("(a n) -> a n", a=1).broadcast_to([P, E])).then_inc(r_in, 16)

            def inputs(g):
                sp.wait_ge(c_lo, g)
                sp.dma_start(cg[:], c_t[g]).then_inc(cg_in, 16)
                sp.wait_ge(ov_free, OV * (g - 1) + 2)
                sp.wait_ge(op_free, OP * (g - 1) + 2)
                sp.dma_start(xg[:], x_t[g]).then_inc(xg_in, 16)

            def rows_of(g):
                sp.wait_ge(wrow2, g + 1)
                sp.dma_start(rows_t[g], row[:].bitcast(U32)).then_inc(row_out, 16)

            inputs(1)
            with sp.Fori(2, G) as g:
                inputs(g)
                rows_of(g - 2)
            rows_of(G - 2)
            sp.wait_ge(pj_full[0], PJ * (G - 1) + PROJ)
            sp.wait_ge(pj_full[1], PJ * (G - 1) + PROJ)
            for i in range(4):
                sp.dma_start(up_f[:, 2 * i:2 * i + 2, :], ew1[:, 2 * i:2 * i + 2, :]).then_inc(up_in[i], 16)
            for i in range(4):
                sp.wait_ge(up_lo, i + 1)
                sp.dma_start(up_f[:, 2 * i:2 * i + 2, :], ew2[:, 2 * i:2 * i + 2, :]).then_inc(down_in[i], 16)
            if debug_out is not None:
                sp.wait_ge(base_done, G)
                sp.dma_start(debug_out.rearrange("b p d -> p b d"), base[:]).then_inc(dbg, 16)
                sp.wait_ge(dbg, 16)

        @block.gpsimd
        def _(pool):
            pool.memset(nhalf[:], -0.5).then_inc(nhalf_set, 1)
            pool.wait_ge(nhalf_set, 1)

            def power(k, n, bs=slice(0, GB)):
                pool.wait_ge(ln[k]["var"], n + 1)
                pool.tensor_tensor(rstd[:, bs], veps[:, bs], nhalf[:, bs], ALU.pow).then_inc(ln[k]["pow"], 1)

            def front(g, r=None):
                for i, dst in enumerate((qr, kr)):
                    pool.wait_ge(pj_free[0], PJ * g + i + 1)
                    pool.wait_ge(pj_free[1], PJ * g + i + 1)
                    if r is not None:
                        pool.wait_ge(max1, g)
                    pool.tensor_tensor(dst[:, 0, :], rope[:, 0, :], rope[:, 2, :], ALU.add)
                    pool.tensor_tensor(dst[:, 1, :], rope[:, 3, :], rope[:, 1, :], ALU.subtract)\
                        .then_inc(rope_add, 1)
                    if i == 0 and r is not None:
                        power(3, r)
                power(2, g)
                if r is None:
                    pool.wait_ge(bc_done, 1)
                pool.wait_ge(ln[2]["xn"], g + 1)
                pool.tensor_tensor(x1[:], x1[:], bcs[:].unsqueeze(1).to_broadcast([P, GB, D]), ALU.add)\
                    .then_inc(x1_bias, 1)

            def back(g, more):
                for n in range(8):
                    if n == 0 and more:
                        power(1, g + 1)
                    if n >= 2:
                        pool.wait_ge((tpA_full, tpB_full)[n % 2],
                                     (TPA * g + 4, TPB * g + 3)[n % 2] + (n - 2) // 2 + 1)
                    pool.wait_ge(inv2_done, 8 * g + n + 1)
                    pool.tensor_tensor(pn2[:, n % 2], p2[:, n % 2],
                                       inv2[:, n % 2, :].unsqueeze(2).to_broadcast([P, 4, P]), ALU.mult)\
                        .then_inc(norm2, 1)

            power(1, 0)
            pool.wait_ge(bc_in, 16)
            front(0)
            with pool.Fori(0, G - 1) as g:
                back(g, True)
                front(g + 1, g)
            back(G - 1, False)
            for h in range(2):
                power(3, G - 1 + h, HALVES[h])
                pool.wait_ge(down_hi, h + 1)
                pool.tensor_tensor(down[:, 2 * h:2 * h + 2, :, 1, :].rearrange("p e m d -> p (e m) d"),
                                   up_f[:, 2 * h:2 * h + 2, :].rearrange("p e (m d) -> p (e m) d", m=MC),
                                   down[:, 2 * h:2 * h + 2, :, 0, :].rearrange("p e m d -> p (e m) d"), ALU.subtract)\
                    .then_inc(down_lo, 1)

        @block.scalar
        def _(act):
            copy = lambda out, in_, scale=1.0: act.activation(out, in_, ACT.Copy, scale=scale)

            def high(k, n, dst, bs=slice(0, GB)):
                act.wait_ge(ln[k]["xn"], n + 1)
                copy(dst, xn[:, bs]).then_inc(ln[k]["hi"], 1)

            def early(g, part):
                if part == 0:
                    act.wait_ge(cg_in, 16 * (g + 1))
                    copy(ch[:], cg[:], UP).then_inc(c_hi, 1)
                else:
                    act.wait_ge(tpA_full, TPA * (g - 1) + 4)
                    high(1, g, nh[:])

            def turned(g, part):
                act.wait_ge(tpA_full, TPA * g + 1 + part)
                copy((xTh, cTh)[part][:], tpA[:].bitcast(F16)).then_inc(tpA_free, 1)

            def project(g, kind, js):
                for j in js:
                    s = j % 2
                    if (kind, j) == (2, 4):
                        act.wait_ge(wc_lo, 1)
                    act.wait_ge(pj_full[s], PJ * g + 2 + 4 * kind + j // 2 + 1)
                    if kind == 1:
                        h0 = 512 * (j % 2)
                        copy(v2[:, j // 2, h0:h0 + 512], pj[s][:], DOWN).then_inc(pj_free[s], 1)
                    else:
                        out, b = ((kT, H + j), None, (qT, j))[kind]
                        act.activation(out[:, j, :], pj[s][:], ACT.Identity, bias=bias[:, b:b + 1],
                                       scale=DOWN).then_inc(pj_free[s], 1)

            def rows_high(r):
                act.wait_ge(row_out, 16 * r + 16)
                high(3, r, row[:, :, 0:D])

            def router(r, u0, u1):
                for m in range(KC):
                    act.wait_ge(sc_full[m], (u0, u1)[m] + 2)
                    act.activation(th[:, m, :], sc[m][:], ACT.Tanh, bias=rb1half[:, m:m + 1],
                                   scale=0.5 * DOWN).then_inc(r_tanh, 1)

            def gate_exp(r):
                act.wait_ge(gdiff, r + 1)
                act.activation(ge[:], gd[:], ACT.Exp).then_inc(gexp, 1)

            def weights_high(i, q, src):
                act.wait_ge(q, 16)
                copy(w2h[:, :, 1024 * i:1024 * i + 1024], src, UP).then_inc(w2_hi, 1)

            def front(g, r=None):
                for i, (bank_, full, free, use) in enumerate(((ov, ov_full, ov_free, OV * g), (op, op_full, op_free, OP * g))):
                    act.wait_ge(full, use + 1)
                    copy(v1[:, 2 * i:2 * i + 2, :], bank_[:], DOWN).then_inc(free, 1)
                if r is None:
                    weights_high(1, wv_in, wvf)
                project(g, 0, range(2))
                if r is not None:
                    rows_high(r)
                project(g, 0, range(2, 4))
                if r is None:
                    weights_high(2, wq_in, wqf)
                act.wait_ge(neg1, g + 1)
                for b in range(GB):
                    last = act.activation(p1[:, b, :], sc0[:, b * P:(b + 1) * P], ACT.Exp,
                                          bias=nm1[:, b:b + 1], scale=ATTN_SCALE, accum_out=sum1[:, b:b + 1])
                last.then_inc(sc_free[0], 1)
                project(g, 0, range(4, 8))
                act.wait_ge(tpA_full, TPA * g + 3)
                copy(pT1[:], tpA[:]).then_inc(tpA_free, 1)
                if r is not None:
                    act.wait_ge(sc_full[0], SC[0] * r + 7)
                    copy(rTh[:], sc0[:].bitcast(F16)).then_inc(sc_free[0], 1)
                project(g, 1, range(4))
                if r is not None:
                    act.wait_ge(rope_add, 2 * g + 2)
                    router(r, SC[0] * r + 6, SC[1] * r + 4)
                else:
                    act.wait_ge(r_in, 64)
                    copy(r1h[:], r1f, UP).then_inc(r1_hi, 1)
                    copy(rb1half[:], rb1s[:], 0.5).then_inc(r1_hi, 1)
                    project(g, 1, range(4, 6))
                high(2, g, nh[:])
                project(g, 1, range(4 if r is not None else 6, 8))
                act.wait_ge(tpA_full, TPA * g + 4)
                copy(xTh[:], tpA[:].bitcast(F16)).then_inc(tpA_free, 1)
                if r is None:
                    act.wait_ge(wc_in, 16)
                    copy(wch[:], wcf, UP).then_inc(wc_hi, 1)
                else:
                    gate_exp(r)

            def up_high(i):
                act.wait_ge(up_in[i], 16)
                copy(up_h[:, 2 * i:2 * i + 2].rearrange("p e c n -> p e (c n)"), up_f[:, 2 * i:2 * i + 2, :],
                     UP).then_inc(up_hi, 1)

            def back(g, more):
                project(g, 2, range(5))
                for n in range(8 + 4):
                    if n >= 4:
                        m = n - 4
                        hh = 4 * (m % 2)
                        if m >= 4:
                            act.wait_ge(op_full, OP * g + 2 + m // 2 - 1)
                        act.wait_ge(pj_full[m % 2], PJ * g + PROJ + m // 2 + 1)
                        copy(oTh[:, (m // 2) % 2, hh:hh + 4, :].rearrange("p a b -> p (a b)"), pj[m % 2][:], MID)\
                            .then_inc(o_hi, 1)
                    if more and n == 8:
                        early(g + 1, 0)
                    if more and n == 11:
                        turned(g + 1, 0)
                    if not more and n in (4, 6, 8, 9):
                        up_high((4, 6, 8, 9).index(n))
                    if n >= 8:
                        continue
                    s = n % 2
                    if n >= 2:
                        act.wait_ge(norm2, 8 * g + n - 1)
                    act.wait_ge(neg2, 8 * g + n + 1)
                    for i in range(4):
                        last = act.activation(p2[:, s, i, :], sc[s][:, i * P:(i + 1) * P], ACT.Exp,
                                              bias=nm2[:, s, i:i + 1], scale=1.0,
                                              accum_out=sum2[:, s, i:i + 1])
                    last.then_inc(sc_free[s], 1)
                    if more and n == 0:
                        early(g + 1, 1)
                if more:
                    turned(g + 1, 1)

            act.wait_ge(w1_in, 16)
            copy(w1h, w1f, UP).then_inc(w1_hi, 1)
            high(1, 0, nh[:])
            act.wait_ge(cg_in, 16)
            copy(ch[:], cg[:], UP).then_inc(c_hi, 1)
            turned(0, 0)
            weights_high(0, wk_in, wkf)
            turned(0, 1)
            front(0)
            act.wait_ge(r1_hi, 2)
            with act.Fori(0, G - 1) as g:
                back(g, True)
                front(g + 1, g)
            back(G - 1, False)

            def last_high(h):
                high(3, G - 1 + h, row[:, HALVES[h], 0:D], HALVES[h])

            def last_turned(h):
                act.wait_ge(tpA_full, TPA * G + h + 1)
                t = slice(h * 2 * P, (h + 1) * 2 * P)
                copy(rTh[:, :, t], tpA[:].bitcast(F16).rearrange("p (c t) -> p c t", c=KC)[:, :, t]).then_inc(tpA_free, 1)

            def last_hidden(h):
                for m in range(KC):
                    name, use = LAST[h][m]
                    act.wait_ge(banks[name][1][m], use + 1)
                    t = slice(h * 2 * P, (h + 1) * 2 * P)
                    act.activation(th[:, m, t], banks[name][0][m][:, 0:2 * P], ACT.Tanh, bias=rb1half[:, m:m + 1],
                                   scale=0.5 * DOWN).then_inc(last_tanh, 1)

            def down_scaled(i):
                act.wait_ge(down_in[i], 16)
                src = up_f[:, 2 * i:2 * i + 2, :]
                copy(src, src, UP).then_inc(down_up, 1)

            def down_high(i):
                act.wait_ge(down_up, i + 1)
                copy(down[:, 2 * i:2 * i + 2, :, 0, :].rearrange("p e m d -> p (e m) d"),
                     up_f[:, 2 * i:2 * i + 2, :].rearrange("p e (m d) -> p (e m) d", m=MC)).then_inc(down_hi, 1)

            down_scaled(0)
            down_high(0)
            act.wait_ge(row_out, 16 * (G - 1) + 16)
            last_high(0)
            down_scaled(1)
            last_turned(0)
            down_high(1)
            last_high(1)
            last_hidden(0)
            last_turned(1)
            last_hidden(1)
            down_scaled(2)
            down_high(2)
            gate_exp(G - 1)

        @block.vector
        def _(dve):
            def norm(k, n, src, bs=slice(0, GB)):
                for b in range(bs.start, bs.stop):
                    last = dve.bn_stats(stats[:, b, :], src[:, b, :])
                last.then_inc(ln[k]["stats"], 1)
                dve.wait_ge(ln[k]["stats"], n + 1)
                dve.sem_inc(waited, 1)
                for b in range(bs.start, bs.stop):
                    last = dve.bn_aggr(mv[:, b, :], stats[:, b, :])
                last.then_inc(ln[k]["aggr"], 1)
                dve.wait_ge(ln[k]["aggr"], n + 1)
                dve.tensor_scalar(veps[:, bs], mv[:, bs, 1], EPS, None, ALU.add).then_inc(ln[k]["var"], 1)

            def normed(k, n, src, bs=slice(0, GB)):
                dve.wait_ge(ln[k]["pow"], n + 1)
                dve.tensor_scalar(rstd_up[:, bs], rstd[:, bs], UP, None, ALU.mult).then_inc(ln[k]["rstd"], 1)
                dve.wait_ge(ln[k]["rstd"], n + 1)
                for b in range(bs.start, bs.stop):
                    last = dve.tensor_scalar(xn[:, b, :], src[:, b, :], mv[:, b, 0:1], rstd_up[:, b:b + 1],
                                             ALU.subtract, ALU.mult)
                last.then_inc(ln[k]["xn"], 1)

            def low(k, n, hi, dst, bs=slice(0, GB)):
                dve.wait_ge(ln[k]["xn"], n + 1)
                dve.wait_ge(ln[k]["hi"], n + 1)
                dve.tensor_tensor(dst, xn[:, bs], hi, ALU.subtract).then_inc(ln[k]["lo"], 1)

            def context_low(g):
                dve.wait_ge(c_hi, g + 1)
                dve.scalar_tensor_tensor(out=cl[:], in0=cg[:], scalar=UP, in1=ch[:], op0=ALU.mult,
                                         op1=ALU.subtract).then_inc(c_lo, 1)

            def early(g, part):
                if part == 0:
                    dve.wait_ge(xg_in, 16 * (g + 1))
                    norm(1, g, xg)
                elif part == 1:
                    normed(1, g, xg)
                elif part == 2:
                    context_low(g)
                else:
                    dve.wait_ge(tpB_full, TPB * (g - 1) + 3)
                    low(1, g, nh[:], nl[:])

            def turned(g, part):
                dve.wait_ge(tpB_full, TPB * g + 1 + part)
                dve.tensor_copy((xTl, cTl)[part][:], tpB[:].bitcast(F16)).then_inc(tpB_free, 1)

            def weights_low2(i, src):
                dve.wait_ge(w2_hi, i + 1)
                dve.scalar_tensor_tensor(out=w2l[:, :, 1024 * i:1024 * i + 1024], in0=src, scalar=UP,
                                         in1=w2h[:, :, 1024 * i:1024 * i + 1024], op0=ALU.mult,
                                         op1=ALU.subtract).then_inc(w2_lo, 1)

            def weights_low(i):
                dve.wait_ge(up_hi, i + 1)
                dve.scalar_tensor_tensor(out=up_l[:, 2 * i:2 * i + 2].rearrange("p e c n -> p e (c n)"),
                                         in0=up_f[:, 2 * i:2 * i + 2, :], scalar=UP,
                                         in1=up_h[:, 2 * i:2 * i + 2].rearrange("p e c n -> p e (c n)"),
                                         op0=ALU.mult, op1=ALU.subtract).then_inc(up_lo, 1)

            def base_half(h):
                bs = HALVES[h]
                dve.wait_ge(ln[3]["xn"], G + h)
                dve.scalar_tensor_tensor(out=base[:, (G - 1) * GB + bs.start:(G - 1) * GB + bs.stop, :], in0=xn[:, bs],
                                         scalar=1.0 / UP, in1=x2[:, bs], op0=ALU.mult, op1=ALU.add).then_inc(base_done, 1)

            def rows_low_half(h):
                bs = HALVES[h]
                low(3, G - 1 + h, row[:, bs, 0:D], row[:, bs, D:2 * D], bs)

            def last_turned(h):
                dve.wait_ge(tpB_full, TPB * G + h + 1)
                t = slice(h * 2 * P, (h + 1) * 2 * P)
                dve.tensor_copy(rTl[:, :, t], tpB[:].bitcast(F16).rearrange("p (c t) -> p c t", c=KC)[:, :, t])\
                    .then_inc(tpB_free, 1)

            def last_hidden(h):
                t = slice(h * 2 * P, (h + 1) * 2 * P)
                for m in range(KC):
                    name, use = LAST[h][m]
                    free = banks[name][2][m]
                    dve.wait_ge(last_tanh, KC * h + m + 1)
                    dve.tensor_scalar(xb[:, m, t], banks[name][0][m][:, 0:2 * P], DOWN, rb1s[:, m:m + 1],
                                      ALU.mult, ALU.add).then_inc(free, 1)
                    dve.wait_ge(free, use + 1)
                    dve.scalar_tensor_tensor(out=xb[:, m, t], in0=th[:, m, t], scalar=1.0, in1=xb[:, m, t],
                                             op0=ALU.add, op1=ALU.mult).then_inc(last_hid, 1)

            def rows_low(r):
                normed(3, r, x2)
                dve.wait_ge(ln[3]["xn"], r + 1)
                dve.scalar_tensor_tensor(out=base[:, bass.ds(r * GB, GB), :], in0=xn[:], scalar=1.0 / UP, in1=x2[:],
                                         op0=ALU.mult, op1=ALU.add).then_inc(base_done, 1)
                low(3, r, row[:, :, 0:D], row[:, :, D:2 * D])

            def router_turned(r, u1):
                dve.wait_ge(sc_full[1], u1 + 1)
                dve.tensor_copy(rTl[:], sc1[:].bitcast(F16)).then_inc(sc_free[1], 1)

            def router(r, u0, u1):
                for m in range(KC):
                    dve.wait_ge(r_tanh, KC * r + m + 1)
                    dve.tensor_scalar(xb[:, m, :], sc[m][:], DOWN, rb1s[:, m:m + 1], ALU.mult, ALU.add)\
                        .then_inc(sc_free[m], 1)
                    dve.wait_ge(sc_free[m], (u0, u1)[m] + 2)
                    dve.scalar_tensor_tensor(out=xb[:, m, :], in0=th[:, m, :], scalar=1.0, in1=xb[:, m, :],
                                             op0=ALU.add, op1=ALU.mult).then_inc(r_hid, 1)

            def choose(r, bank_, full, free, use):
                dve.wait_ge(full, use + 1)
                dve.scalar_tensor_tensor(out=lg[:], in0=bank_[:, 0:GB * E].rearrange("p (b e) -> p b e", b=GB),
                                         scalar=0.5, in1=rb2s[:].unsqueeze(1).to_broadcast([P, GB, E]),
                                         op0=ALU.mult, op1=ALU.add).then_inc(free, 1)
                dve.wait_ge(free, use + 1)
                dve.sem_inc(waited, 1)
                for b in range(GB):
                    last = dve.max(mx8[:, b, :], lg[:, b, :])
                last.then_inc(top8, 1)
                dve.wait_ge(top8, r + 1)
                dve.sem_inc(waited, 1)
                for b in range(GB):
                    last = dve.max_index(ix8[:, b, :], mx8[:, b, :], lg[:, b, :])
                last.then_inc(top8i, 1)
                dve.tensor_tensor(gd[:], mx8[:, :, 1], mx8[:, :, 0], ALU.subtract).then_inc(gdiff, 1)
                iob = iota8.unsqueeze(1).to_broadcast([P, GB, E])
                dve.wait_ge(top8i, r + 1)
                dve.tensor_copy(ixf[:], ix8[:, :, 0:2]).then_inc(ixf_done, 1)
                dve.wait_ge(ixf_done, r + 1)
                dve.tensor_copy(eidx[:, bass.ds(r * GB, GB), :], ixf[:]).then_inc(kept, 1)
                dve.tensor_tensor(m1[:], iob, ixf[:, :, 0:1].to_broadcast([P, GB, E]), ALU.is_equal)
                dve.tensor_tensor(m2[:], iob, ixf[:, :, 1:2].to_broadcast([P, GB, E]), ALU.is_equal).then_inc(hot, 1)

            def weigh(r):
                dve.wait_ge(gexp, r + 1)
                dve.tensor_scalar(gs[:], ge[:], 1.0, None, ALU.add).then_inc(gsum, 1)
                dve.wait_ge(gsum, r + 1)
                dve.reciprocal(g1[:], gs[:]).then_inc(gate1, 1)
                dve.wait_ge(gate1, r + 1)
                dve.tensor_tensor(g2[:], ge[:], g1[:], ALU.mult).then_inc(gate2, 1)
                dve.wait_ge(hot, r + 1)
                dve.wait_ge(gate2, r + 1)
                wcols = row[:, :, 2 * D:ROW].bitcast(F32)
                dve.tensor_tensor(m1[:], m1[:], g1[:].unsqueeze(2).to_broadcast([P, GB, E]), ALU.mult)
                dve.tensor_tensor(m2[:], m2[:], g2[:].unsqueeze(2).to_broadcast([P, GB, E]), ALU.mult)\
                    .then_inc(wrow, 1)
                dve.wait_ge(wrow, r + 1)
                dve.tensor_tensor(wcols, m1[:], m2[:], ALU.add).then_inc(wrow2, 1)

            def front(g, r=None):
                cosb = cosT.unsqueeze(1).to_broadcast([P, GB, P])
                sinb = sinT.unsqueeze(1).to_broadcast([P, GB, P])
                for i in range(2):
                    if r is not None or i:
                        dve.wait_ge(rope_add, 2 * g + i)
                    for half in range(2):
                        dve.wait_ge(pj_full[half], PJ * g + i + 1)
                        src = pj[half][:].rearrange("p (b t) -> p b t", b=GB)
                        dve.tensor_tensor(rope[:, 3 * half].rearrange("p (b t) -> p b t", b=GB), src, cosb, ALU.mult)
                        last = dve.tensor_tensor(rope[:, 1 + half].rearrange("p (b t) -> p b t", b=GB),
                                                 src, sinb, ALU.mult)
                        last.then_inc(pj_free[half], 1)
                    if i == 0:
                        if r is None:
                            turned(0, 1)
                            dve.tensor_copy(identb[:], ident)
                            dve.tensor_copy(masks[:], cst[:, 2 * P:7 * P].rearrange("p (m k) -> p m k", m=5))\
                                .then_inc(ready, 1)
                        else:
                            norm(3, r, x2)
                if r is None:
                    weights_low2(1, wvf)
                else:
                    rows_low(r)
                s1 = 1 if r is None else SC[0] * r + 6
                dve.wait_ge(sc_full[0], s1)
                dve.tensor_reduce(mx1[:], sc0[:].rearrange("p (b t) -> p b t", b=GB), AX, ALU.max).then_inc(max1, 1)
                dve.wait_ge(max1, g + 1)
                dve.tensor_scalar(nm1[:], mx1[:], -ATTN_SCALE, None, ALU.mult).then_inc(neg1, 1)
                dve.wait_ge(sc_free[0], s1)
                dve.reciprocal(inv1[:], sum1[:]).then_inc(inv1_done, 1)
                if r is not None:
                    router_turned(r, SC[1] * r + 4)
                else:
                    weights_low2(2, wqf)
                dve.wait_ge(inv1_done, g + 1)
                for i, (bank_, full, free, use) in enumerate(((ov, ov_full, ov_free, OV * g), (op, op_full, op_free, OP * g))):
                    dve.wait_ge(full, use + 2)
                    for b in (2 * i, 2 * i + 1):
                        last = dve.scalar_tensor_tensor(out=x1[:, b, :], in0=bank_[:, (b % 2) * D:(b % 2 + 1) * D],
                                                        scalar=inv1[:, b:b + 1], in1=xg[:, b, :],
                                                        op0=ALU.mult, op1=ALU.add)
                    last.then_inc(free, 1)
                dve.wait_ge(ov_free, OV * g + 2)
                dve.wait_ge(op_free, OP * g + 2)
                norm(2, g, x1)
                normed(2, g, x1)
                if r is not None:
                    router(r, SC[0] * r + 6, SC[1] * r + 4)
                low(2, g, nh[:], nl[:])
                dve.wait_ge(tpB_full, TPB * g + 3)
                dve.tensor_copy(xTl[:], tpB[:].bitcast(F16)).then_inc(tpB_free, 1)
                if r is None:
                    dve.wait_ge(r1_hi, 1)
                    dve.scalar_tensor_tensor(out=r1l[:], in0=r1f, scalar=UP, in1=r1h[:], op0=ALU.mult,
                                             op1=ALU.subtract).then_inc(r1_lo, 1)
                    dve.wait_ge(bv_full, 1)
                    dve.wait_ge(bc_in, 16)
                    dve.tensor_tensor(bcs[:], bcs[:], sc1[:, 0:D], ALU.add).then_inc(bc_done, 1)
                    dve.wait_ge(wc_hi, 1)
                    dve.scalar_tensor_tensor(out=wcl[:], in0=wcf, scalar=UP, in1=wch[:], op0=ALU.mult,
                                             op1=ALU.subtract).then_inc(wc_lo, 1)
                else:
                    choose(r, sc0, sc_full[0], sc_free[0], SC[0] * r + 8)
                    weigh(r)

            def back(g, more):
                def sums(n):
                    s = n % 2
                    dve.wait_ge(sc_free[s], (SC[0] * g + 1, SC[1] * g)[s] + n // 2 + 1)
                    if n >= 2:
                        dve.wait_ge(norm2, 8 * g + n - 1)
                    dve.reciprocal(inv2[:, s, :], sum2[:, s, :]).then_inc(inv2_done, 1)

                def transposed(m):
                    full, free, src = ((tpA_full, tpA_free, tpA), (tpB_full, tpB_free, tpB))[m % 2]
                    dve.wait_ge(full, ((TPA * g + 4), (TPB * g + 3))[m % 2] + m // 2 + 1)
                    if m >= 2:
                        dve.wait_ge(pj_full[m % 2], PJ * g + PROJ + m // 2)
                    dve.tensor_copy(pT2[:, m % 2].rearrange("p a b -> p (a b)"), src[:]).then_inc(free, 1)

                def outputs_low(m):
                    hh = 4 * (m % 2)
                    dve.wait_ge(o_hi, 8 * g + m + 1)
                    dve.scalar_tensor_tensor(out=oTl[:, (m // 2) % 2, hh:hh + 4, :].rearrange("p a b -> p (a b)"),
                                             in0=pj[m % 2][:], scalar=MID,
                                             in1=oTh[:, (m // 2) % 2, hh:hh + 4, :].rearrange("p a b -> p (a b)"),
                                             op0=ALU.mult, op1=ALU.subtract).then_inc(pj_free[m % 2], 1)

                if more:
                    for part in (0, 1):
                        early(g + 1, part)
                for n in range(8 + 5):
                    if n == 7:
                        sums(6)
                    if n in (7, 9):
                        outputs_low(n - 4)
                    if not more and n == 7:
                        weights_low(0)
                    if n < 8:
                        s = n % 2
                        dve.wait_ge(sc_full[s], (SC[0] * g + 1, SC[1] * g)[s] + n // 2 + 1)
                        dve.tensor_reduce(mx2[:, s, :], sc[s][:].rearrange("p (b t) -> p b t", b=4), AX, ALU.max)\
                            .then_inc(max2, 1)
                        dve.wait_ge(max2, 8 * g + n + 1)
                        dve.tensor_scalar(nm2[:, s, :], mx2[:, s, :], -1.0, None, ALU.mult).then_inc(neg2, 1)
                    if n == 0:
                        for j in (5, 6, 7):
                            dve.wait_ge(pj_full[j % 2], PJ * g + 10 + j // 2 + 1)
                            dve.tensor_scalar(qT[:, j, :], pj[j % 2][:], DOWN, bias[:, j:j + 1],
                                              ALU.mult, ALU.add).then_inc(pj_free[j % 2], 1)
                            if j == 6:
                                sums(0)
                        transposed(0)
                    if n in (2, 3, 4, 5, 6, 8):
                        sums(n - 1)
                    if more and n == 2:
                        early(g + 1, 3)
                    if 3 <= n < 10:
                        transposed(n - 2)
                    if n in (4, 5, 6, 8, 10, 11):
                        outputs_low(n - 4)
                    if not more and n in (8, 9):
                        weights_low(n - 7)
                    if n in (7, 9, 11, 12):
                        b = (7, 9, 11, 12).index(n)
                        if b == 0:
                            dve.wait_ge(x1_bias, g + 1)
                        dve.wait_ge(op_full, OP * g + 2 + b + 1)
                        dve.scalar_tensor_tensor(out=x2[:, b, :], in0=op[:, 0:D], scalar=MID_DOWN, in1=x1[:, b, :],
                                                 op0=ALU.mult, op1=ALU.add).then_inc(op_free, 1)
                    if more and n == 10:
                        early(g + 1, 2)
                    if more and n in (11, 12):
                        turned(g + 1, n - 11)
                    if not more and n == 9:
                        dve.wait_ge(op_free, OP * g + 2 + 2)
                        norm(3, G - 1, x2, HALVES[0])
                    if not more and n == 10:
                        normed(3, G - 1, x2, HALVES[0])
                    if not more and n == 11:
                        rows_low_half(0)
                        weights_low(3)
                dve.wait_ge(op_free, OP * (g + 1))

            dve.wait_ge(xg_in, 16)
            norm(1, 0, xg)
            dve.wait_ge(const_in, 16)
            dve.tensor_copy(identh[:], ident).then_inc(ready, 1)
            normed(1, 0, xg)
            dve.wait_ge(w1_hi, 1)
            dve.scalar_tensor_tensor(out=w1l[:], in0=w1f, scalar=UP, in1=w1h[:], op0=ALU.mult,
                                     op1=ALU.subtract).then_inc(w1_lo, 1)
            low(1, 0, nh[:], nl[:])
            turned(0, 0)
            context_low(0)
            weights_low2(0, wkf)
            dve.wait_ge(table_in, 32)
            front(0)
            with dve.Fori(0, G - 1) as g:
                back(g, True)
                front(g + 1, g)
            back(G - 1, False)
            norm(3, G, x2, HALVES[1])
            last_turned(0)
            base_half(0)
            normed(3, G, x2, HALVES[1])
            base_half(1)
            rows_low_half(1)
            last_hidden(0)
            last_turned(1)
            last_hidden(1)
            choose(G - 1, ov, ov_full, ov_free, OV * G)

        @block.tensor
        def _(pe):
            def transposes(bankA, bankB, hi, lo, fullA, fullB, lows, n):
                for dst, src, full in ((bankA, hi, fullA), (bankB, lo, fullB)):
                    if full is fullB:
                        pe.wait_ge(lows, n)
                    view = dst[:].bitcast(F16)
                    for c in range(KC):
                        for b in range(GB):
                            last = pe.transpose(view[:, c * TOK + b * P:c * TOK + (b + 1) * P],
                                                src(b, c), identh[:])
                    last.then_inc(full, 1)

            def three(out, whi, wlo, xhi, xlo):
                terms = [(c, w, v) for c in range(KC) for w, v in ((whi, xhi), (whi, xlo), (wlo, xhi))]
                for i, (c, w, v) in enumerate(terms):
                    last = pe.matmul(out, w(c), v(c), start=(i == 0), stop=(i == len(terms) - 1))
                return last

            def turn_tokens(g, after=True):
                pe.wait_ge(ln[1]["hi"], g + 1)
                if after:
                    pe.wait_ge(tpA_free, TPA * g)
                    pe.wait_ge(tpB_free, TPB * g)
                transposes(tpA, tpB, lambda b, c: nh[:, b, c * P:(c + 1) * P],
                           lambda b, c: nl[:, b, c * P:(c + 1) * P], tpA_full, tpB_full, ln[1]["lo"], g + 1)

            def turn_context(g):
                pe.wait_ge(tpA_free, TPA * g + 1)
                pe.wait_ge(tpB_free, TPB * g + 1)
                pe.wait_ge(c_hi, g + 1)
                transposes(tpA, tpB, lambda b, c: ch[:, b, c * P:(c + 1) * P],
                           lambda b, c: cl[:, b, c * P:(c + 1) * P], tpA_full, tpB_full, c_lo, g + 1)

            def project(g, kind, js):
                for j in js:
                    pe.wait_ge(pj_free[j % 2], PJ * g + 2 + 4 * kind + j // 2)
                    if kind == 1:
                        b, n0 = j // 2, 1024 + 512 * (j % 2)
                        last = three(pj[j % 2][:],
                                     lambda c: cTh[:, c, b * P:(b + 1) * P], lambda c: cTl[:, c, b * P:(b + 1) * P],
                                     lambda c: w2h[:, c, n0:n0 + 512], lambda c: w2l[:, c, n0:n0 + 512])
                    else:
                        n0 = 1024 * kind + P * j
                        src = (cTh, cTl) if kind == 0 else (xTh, xTl)
                        last = three(pj[j % 2][:],
                                     lambda c: w2h[:, c, n0:n0 + P], lambda c: w2l[:, c, n0:n0 + P],
                                     lambda c: src[0][:, c, :], lambda c: src[1][:, c, :])
                    last.then_inc(pj_full[j % 2], 1)

            def turn_rows(r, u0, u1):
                pe.wait_ge(ln[3]["hi"], r + 1)
                pe.wait_ge(sc_free[0], u0)
                pe.wait_ge(sc_free[1], u1)
                transposes(sc0, sc1, lambda b, c: row[:, b, c * P:(c + 1) * P],
                           lambda b, c: row[:, b, D + c * P:D + (c + 1) * P], sc_full[0], sc_full[1],
                           ln[3]["lo"], r + 1)

            def router_hidden(r, u0, u1):
                pe.wait_ge(r1_hi, 2)
                pe.wait_ge(r1_lo, 1)
                pe.wait_ge(sc_free[0], u0 + 1)
                pe.wait_ge(sc_free[1], u1 + 1)
                for m in range(KC):
                    three(sc[m][:], lambda c: r1h[:, c, m * P:(m + 1) * P], lambda c: r1l[:, c, m * P:(m + 1) * P],
                          lambda c: rTh[:, c, :], lambda c: rTl[:, c, :]).then_inc(sc_full[m], 1)

            def logits(r, u0):
                pe.wait_ge(r_in, 64)
                pe.wait_ge(r_hid, KC * (r + 1))
                pe.wait_ge(sc_free[0], u0 + 2)
                for b in range(GB):
                    for m in range(KC):
                        last = pe.matmul(sc0[:, b * E:(b + 1) * E], xb[:, m, b * P:(b + 1) * P], rw2s[:, m, :],
                                         start=(m == 0), stop=(m == KC - 1))
                last.then_inc(sc_full[0], 1)

            def front(g, r=None):
                pe.wait_ge(tpA_free, TPA * g + 1)
                pe.wait_ge(tpB_free, TPB * g + 1)
                for i in range(4):
                    if r is None and i == 2:
                        turn_context(0)
                    if r is not None or i >= 2:
                        pe.wait_ge(pj_free[i % 2], PJ * g + i // 2)
                    three(pj[i % 2][:], lambda c: w1h[:, c, i * P:(i + 1) * P], lambda c: w1l[:, c, i * P:(i + 1) * P],
                          lambda c: xTh[:, c, :], lambda c: xTl[:, c, :]).then_inc(pj_full[i % 2], 1)
                first = ((ov, ov_full, ov_free, OV * g), (op, op_full, op_free, OP * g))
                for i, (bank_, full, free, use) in enumerate(first):
                    if r is not None:
                        pe.wait_ge(free, use)
                    for b in (2 * i, 2 * i + 1):
                        last = three(bank_[:, (b % 2) * D:(b % 2 + 1) * D],
                                     lambda c: xTh[:, c, b * P:(b + 1) * P], lambda c: xTl[:, c, b * P:(b + 1) * P],
                                     lambda c: w1h[:, c, 512:768], lambda c: w1l[:, c, 512:768])
                    last.then_inc(full, 1)
                if r is None:
                    pe.wait_ge(w2_hi, 1)
                    pe.wait_ge(w2_lo, 1)
                pe.wait_ge(tpA_free, TPA * g + 2)
                pe.wait_ge(tpB_free, TPB * g + 2)
                project(g, 0, range(4))
                pe.wait_ge(rope_add, 2 * g + 2)
                if r is None:
                    pe.wait_ge(ready, 2)
                else:
                    pe.wait_ge(sc_free[0], SC[0] * r + 5)
                pe.matmul(sc0[:], identb[:], masks[:, 0:1, :].to_broadcast([P, 4, P]), start=True, stop=True,
                          skip_group_check=True)
                for b in range(GB):
                    s = slice(b * P, (b + 1) * P)
                    for c in range(KC):
                        last = pe.matmul(sc0[:, s], qr[:, c, s], kr[:, c, s], start=False,
                                         stop=(c == KC - 1), skip_group_check=True)
                last.then_inc(sc_full[0], 1)
                project(g, 0, range(4, 8))
                if r is not None:
                    turn_rows(r, SC[0] * r + 6, SC[1] * r + 4)
                else:
                    pe.wait_ge(sc_free[0], 1)
                for b in range(GB):
                    last = pe.transpose(tpA[:, b * P:(b + 1) * P], p1[:, b, :], ident)
                last.then_inc(tpA_full, 1)
                if r is None:
                    pe.wait_ge(w2_hi, 2)
                    pe.wait_ge(w2_lo, 2)
                project(g, 1, range(1))
                pe.wait_ge(tpA_free, TPA * g + 3)
                for i, (bank_, full, free, use) in enumerate(first):
                    pe.wait_ge(free, use + 1)
                    for b in (2 * i, 2 * i + 1):
                        last = pe.matmul(bank_[:, (b % 2) * D:(b % 2 + 1) * D], pT1[:, b, :], v1[:, b, :],
                                         start=True, stop=True)
                    last.then_inc(full, 1)
                project(g, 1, range(1, 4))
                if r is not None:
                    router_hidden(r, SC[0] * r + 6, SC[1] * r + 4)
                if r is None:
                    pe.wait_ge(wc_in, 16)
                    for h in range(H):
                        last = pe.matmul(sc1[:, 0:D], bias[:, 2 * H + h:2 * H + h + 1].to_broadcast([P, P]), wcf[:, h, :],
                                         start=(h == 0), stop=(h == H - 1))
                    last.then_inc(bv_full, 1)
                project(g, 1, range(4, 8))
                pe.wait_ge(ln[2]["hi"], g + 1)
                transposes(tpA, tpB, lambda b, c: nh[:, b, c * P:(c + 1) * P],
                           lambda b, c: nl[:, b, c * P:(c + 1) * P], tpA_full, tpB_full, ln[2]["lo"], g + 1)
                if r is not None:
                    logits(r, SC[0] * r + 6)

            def back(g, more):
                pe.wait_ge(tpA_free, TPA * g + 4)
                pe.wait_ge(tpB_free, TPB * g + 3)
                project(g, 2, range(5))

                def turn_quad(m):
                    dst, full, free, use = ((tpA, tpA_full, tpA_free, TPA * g + 4),
                                            (tpB, tpB_full, tpB_free, TPB * g + 3))[m % 2]
                    pe.wait_ge(norm2, 8 * g + m + 1)
                    pe.wait_ge(free, use + m // 2)
                    for i in range(4):
                        last = pe.transpose(dst[:, i * P:(i + 1) * P], pn2[:, m % 2, i, :], ident)
                    last.then_inc(full, 1)

                for n in range(8 + 4):
                    if n < 8:
                        s, b, h0 = n % 2, n // 2, 4 * (n % 2)
                        t = slice(b * P, (b + 1) * P)
                        if n == 1:
                            pe.wait_ge(bc_done, 1)
                        else:
                            pe.wait_ge(sc_free[s], (SC[0] * g + 1, SC[1] * g)[s] + n // 2)
                        pe.matmul(sc[s][:], identb[:],
                                  masks[:, 1 + 2 * (n % 2):3 + 2 * (n % 2), :].unsqueeze(2).to_broadcast([P, 2, 2, P]),
                                  start=True, stop=True, skip_group_check=True)
                        if n == 0:
                            pe.wait_ge(pj_free[1], PJ * g + 12)
                        for i in range(4):
                            last = pe.matmul(sc[s][:, i * P:(i + 1) * P], qT[:, h0 + i, t], kT[:, h0 + i, t],
                                             start=False, stop=True, skip_group_check=True)
                        last.then_inc(sc_full[s], 1)
                    if n == 0:
                        project(g, 2, range(5, 8))
                        turn_quad(0)
                        pe.wait_ge(pj_free[0], PJ * g + PROJ)
                        pe.wait_ge(pj_free[1], PJ * g + PROJ)
                    if 4 <= n < 10:
                        turn_quad(n - 2)
                    if n == 2 or 4 <= n < 11:
                        m = max(n - 3, 0)
                        b, h0 = m // 2, 4 * (m % 2)
                        free, use = ((tpA_free, TPA * g + 4), (tpB_free, TPB * g + 3))[m % 2]
                        pe.wait_ge(free, use + m // 2 + 1)
                        pe.wait_ge(pj_free[m % 2], PJ * g + PROJ + m // 2)
                        for i in range(4):
                            h = h0 + i
                            last = pe.matmul(pj[m % 2][:, i * P:(i + 1) * P], v2[:, b, h * DH:(h + 1) * DH],
                                             pT2[:, m % 2, i, :], start=True, stop=True)
                        last.then_inc(pj_full[m % 2], 1)
                    if n == 3:
                        turn_quad(1)
                    if n == 11 and more:
                        turn_tokens(g + 1)
                    if n in (6, 8, 10, 11):
                        b = (6, 8, 10, 11).index(n)
                        if b == 0:
                            pe.wait_ge(wc_lo, 1)
                        for k in range(2):
                            pe.wait_ge(pj_free[k], PJ * g + PROJ + b + 1)
                        pe.wait_ge(op_free, OP * g + 2 + b)
                        for h in range(H):
                            for k, (o, w) in enumerate(((oTh, wch), (oTl, wch), (oTh, wcl))):
                                last = pe.matmul(op[:, 0:D], o[:, b % 2, h, :], w[:, h, :],
                                                 start=(h == 0 and k == 0), stop=(h == H - 1 and k == 2))
                        last.then_inc(op_full, 1)
                if more:
                    turn_context(g + 1)

            pe.wait_ge(ready, 1)
            turn_tokens(0, after=False)
            pe.wait_ge(w1_hi, 1)
            pe.wait_ge(w1_lo, 1)
            front(0)
            pe.wait_ge(w2_hi, 3)
            pe.wait_ge(w2_lo, 3)
            with pe.Fori(0, G - 1) as g:
                back(g, True)
                front(g + 1, g)
            back(G - 1, False)

            def last_rows(h):
                pe.wait_ge(ln[3]["hi"], G + h)
                pe.wait_ge(tpA_free, TPA * G + h)
                pe.wait_ge(tpB_free, TPB * G + h)
                for dst, at, full in ((tpA, 0, tpA_full), (tpB, D, tpB_full)):
                    if at == D:
                        pe.wait_ge(ln[3]["lo"], G + h)
                    view = dst[:].bitcast(F16)
                    for c in range(KC):
                        for b in range(HALVES[h].start, HALVES[h].stop):
                            last = pe.transpose(view[:, c * TOK + b * P:c * TOK + (b + 1) * P],
                                                row[:, b, at + c * P:at + (c + 1) * P], identh[:])
                    last.then_inc(full, 1)

            def last_hidden(h):
                t = slice(h * 2 * P, (h + 1) * 2 * P)
                pe.wait_ge(tpA_free, TPA * G + h + 1)
                pe.wait_ge(tpB_free, TPB * G + h + 1)
                for m in range(KC):
                    name, use = LAST[h][m]
                    bank_, full, free = (x[m] for x in banks[name])
                    pe.wait_ge(free, use)
                    three(bank_[:, 0:2 * P], lambda c: r1h[:, c, m * P:(m + 1) * P], lambda c: r1l[:, c, m * P:(m + 1) * P],
                          lambda c: rTh[:, c, t], lambda c: rTl[:, c, t]).then_inc(full, 1)

            def last_logits(h):
                pe.wait_ge(last_hid, KC * (h + 1))
                for b in range(HALVES[h].start, HALVES[h].stop):
                    for m in range(KC):
                        last = pe.matmul(ov[:, b * E:(b + 1) * E], xb[:, m, b * P:(b + 1) * P], rw2s[:, m, :],
                                         start=(m == 0), stop=(m == KC - 1))
                return last

            last_rows(0)
            last_hidden(0)
            last_rows(1)
            last_hidden(1)
            pe.wait_ge(ov_free, OV * G)
            last_logits(0)
            last_logits(1).then_inc(ov_full, 1)


SLOTS = 3
STEPS = 6
LAG = 2
TILES = (B * L * 2 + E * (P - 1)) // P
TURNS = -(-TILES // STEPS)
assert TILES % SLOTS == 0 and STEPS % SLOTS == 0
SKIP = 8192
RW = ROW // 2


CONSTS = (("before", P), ("iota_p", P), ("iota_t", TILES), ("steps", B), ("less", E * E), ("token", B), ("iota8", E),
          ("ident", P), ("octal", STEPS))


def expert_phase(nc, shared, dram, out):
    (eb1, eb2, pick_expert) = dram
    base, eidx, rows, cols, identh, picked = (shared[k] for k in ("base", "eidx", "rows", "cols", "identh", "picked"))
    row, ge, gs, g1, g2, m1, m2 = (shared[k] for k in ("row", "ge", "gs", "g1", "g2", "m1", "m2"))
    up_f, up_h, up_l, up_hi, up_lo, row_out, down_in = (
        shared[k] for k in ("up_f", "up_h", "up_l", "up_hi", "up_lo", "row_out", "down_in"))
    before, iota_p, iota_t, steps, less, token, iota8, _, octal = (cols[k] for k, _ in CONSTS)
    with ExitStack() as ctx:
        def sb(name, shape, dt=F32):
            return ctx.enter_context(nc.sbuf_tensor(name, shape, dt))

        def bank(name):
            return ctx.enter_context(nc.psum_tensor(name, [P, 512], F32))

        def sem(name):
            return ctx.enter_context(nc.semaphore(name))

        down, down_hi, down_lo = (shared[k] for k in ("down", "down_hi", "down_lo"))
        b1 = sb("b1", [P, E * MC])
        b2f, b2, b2l = sb("b2f", [E, D]), sb("b2", [2 * E, D], F16), sb("b2l", [E, D], F16)
        pick = sb("pick", [2 * E, E * P], F16)
        hot = sb("hot", [P, 2, B, E])
        both = sb("both", [P, B, E], F16)
        beforeh, onesh = sb("beforeh", [P, P], F16), sb("onesh", [P, P], F16)
        iotah = sb("iotah", [P, P], F16)
        over = sb("over", [P, E, B])
        ntiles, mixed, first, last_t, first_s = (sb("ntiles", [P, E]), sb("mixed", [P, E, E]), sb("first", [P, E]),
                                                 sb("last_t", [P, E]), sb("first_s", [P, E]))
        count = sb("count", [P, E])
        place, placed = sb("place", [P, B, E]), sb("placed", [P, 2, B, E])
        slot, sloti = sb("slot", [P, 2 * B]), sb("sloti", [P, 2 * B], mybir.dt.int32)
        ti, ri = sb("ti", [P, 2 * B], mybir.dt.int32), sb("ri", [P, 2 * B], mybir.dt.int32)
        tf, rf = sb("tf", [P, 2 * B], F16), sb("rf", [P, 2 * B])
        ACT_ONES = 10
        ONES = (2 * B - ACT_ONES) // 2
        minus_r, apart = sb("minus_r", [P, ACT_ONES]), sb("apart", [P, ACT_ONES, P])
        hot_r = sb("hot_r", [P, 2 * B, P], F16)
        hot_t, pay = sb("hot_t", [P, 2 * B, TILES]), sb("pay", [P, 2 * B, TILES], F16)
        signed, sign = sb("signed", [P, 2, B]), sb("sign", [P, B])
        early, early_n = sb("early", [P, TILES // SLOTS]), sb("early_n", [P, 1])
        early_i = sb("early_i", [P, 1], mybir.dt.int32)
        inv, mag, size, isneg, iszero, dsum = (sb(n, [P, TILES]) for n in ("inv", "mag", "size", "isneg", "iszero", "dsum"))
        src_row, dst_row = sb("src_row", [P, TILES], U32), sb("dst_row", [P, TILES], U32)
        below, texp_all = sb("below", [P, TILES, E]), sb("texp", [P, TURNS * STEPS])
        texp = texp_all[:, 0:TILES]
        digits, packed = sb("digits", [P, TURNS, STEPS]), sb("packed", [P, TURNS])
        packed_i = sb("packed_i", [P, TURNS], mybir.dt.int32)
        texp_i = sb("texp_i", [P, TILES], mybir.dt.int32)
        got = [sb(f"got{s}", [P, RW], U32) for s in range(SLOTS)]
        xt = [sb(f"xt{s}", [P, 4, P], F16) for s in range(SLOTS)]
        gate = [sb(f"gate{s}", [P, 1]) for s in range(STEPS)]
        hT = [sb(f"hT{s}", [P, MC, P]) for s in range(SLOTS)]
        hTh = [sb(f"hTh{s}", [P, MC, P], F16) for s in range(SLOTS)]
        hTl = [sb(f"hTl{s}", [P, MC, P], F16) for s in range(SLOTS)]
        ys = [sb(f"ys{s}", [P, D]) for s in range(SLOTS)]
        z = up_f[:].rearrange("p e n -> p (e n)").rearrange("p (k b d) -> p k b d", k=2, b=B)

        rank = bank("rank")
        table = bank("table")
        tp = rank
        hb = [bank(f"h{s}") for s in range(SLOTS)]
        yb = [table, bank("y1"), bank("y2")]

        small_in, b2_lo_in, y_part = sem("small_in"), sem("b2_lo_in"), sem("y_part")
        b2_hi, b2_lo, hot_t_done, pay_done, dst_done = (
            sem(n) for n in ("b2_hi", "b2_lo", "hot_t_done", "pay_done", "dst_done"))
        row_ones, act_ones, apart_done, minus_done, packed_done = (
            sem(n) for n in ("row_ones", "act_ones", "apart_done", "minus_done", "packed_done"))
        chain = sem("chain")
        rank_full, table_full, idx_done, texp_done = (sem(n) for n in ("rank_full", "table_full", "idx_done", "texp_done"))
        gathered = [sem(f"gathered{s}") for s in range(SLOTS)]
        scattered = [sem(f"scattered{s}") for s in range(SLOTS)]
        tp_full, tp_free = sem("tp_full"), sem("tp_free")
        h_full, silu_done, h_hi, h_lo = (sem(n) for n in ("h_full", "silu_done", "h_hi", "h_lo"))
        y_full, y_free = sem("y_full"), sem("y_free")
        last_row = sem("last_row")
        z0_in, z1_in = ([sem(f"z{k}_in{g}") for g in range(G)] for k in range(2))
        early_done, out_done = sem("early_done"), sem("out_done")
        summed, fin_done = sem("summed"), sem("fin_done")

        picked_t = picked.rearrange("(k p g b) d -> k g p b d", k=2, b=GB, g=G)
        out_t = out.rearrange("(g b) p d -> g p b d", b=GB)

        block = ctx.enter_context(nc.Block())

        @block.sync
        def _(sp):
            sp.dma_start(b1[:], eb1).then_inc(small_in, 16)
            sp.dma_start(b2f[:], eb2).then_inc(small_in, 16)
            sp.dma_start(pick[:], pick_expert).then_inc(small_in, 16)
            sp.wait_ge(last_row, 1)
            sp.dma_start(rows.rearrange("(p g b) w -> g p b w", b=GB, g=G)[G - 1], row[:].bitcast(U32))\
                .then_inc(row_out, 16)
            sp.wait_ge(b2_lo, 1)
            sp.dma_start(b2[E:2 * E, :], b2l[:]).then_inc(b2_lo_in, 16)
            sp.wait_ge(down_lo, 4)
            sp.wait_ge(early_done, 1)
            n = sp.value_load(early_i[0:1, 0:1], min_val=16, max_val=16 * (TILES // SLOTS))
            for s in range(SLOTS):
                sp.wait_ge(scattered[s], n)
            for g in range(G):
                sp.dma_start(z[:, 0, g * GB:(g + 1) * GB], picked_t[0, g]).then_inc(z0_in[g], 16)
            for s in range(SLOTS):
                sp.wait_ge(scattered[s], 16 * (TILES // SLOTS))
            for g in range(0, G, 2):
                sp.dma_start(z[:, 1, g * GB:(g + 1) * GB], picked_t[1, g]).then_inc(z1_in[g], 16)
            for g in range(0, G, 2):
                sp.wait_ge(fin_done, g + 1)
                sp.dma_start(out_t[g], z[:, 0, g * GB:(g + 1) * GB]).then_inc(out_done, 16)
            sp.wait_ge(out_done, 16 * G)

        @block.gpsimd
        def _(pool):
            def gather(t):
                s = t % SLOTS
                if t >= SLOTS:
                    pool.wait_ge(tp_free, t - SLOTS + 1)
                pool.indirect_dma_start(got[s][:], None, rows,
                                        bass.IndirectOffsetOnAxis(src_row[:, t:t + 1], 0),
                                        bounds_check=B * L - 1, oob_is_err=False).then_inc(gathered[s], 16)

            def scatter(t):
                s = t % SLOTS
                if t == 0:
                    pool.wait_ge(dst_done, 1)
                pool.wait_ge(y_free, t + 2)
                pool.indirect_dma_start(picked, bass.IndirectOffsetOnAxis(dst_row[:, t:t + 1], 0), ys[s][:], None,
                                        bounds_check=2 * B * L - 1, oob_is_err=False).then_inc(scattered[s], 16)

            pool.wait_ge(down_hi, 3)
            pool.tensor_tensor(down[:, 4:6, :, 1, :].rearrange("p e m d -> p (e m) d"),
                               up_f[:, 4:6, :].rearrange("p e (m d) -> p (e m) d", m=MC),
                               down[:, 4:6, :, 0, :].rearrange("p e m d -> p (e m) d"), ALU.subtract)\
                .then_inc(down_lo, 1)
            pool.wait_ge(hot_t_done, 1)
            pool.tensor_tensor(pay[:], hot_t[:], signed[:].rearrange("p k b -> p (k b)").unsqueeze(2)
                               .to_broadcast([P, 2 * B, TILES]), ALU.mult).then_inc(pay_done, 1)
            pool.wait_ge(row_out, 16 * G + 16)
            pool.wait_ge(idx_done, 1)
            for t in range(TILES):
                gather(t)
                if t >= STEPS:
                    scatter(t - STEPS)
            for t in range(TILES - STEPS, TILES):
                scatter(t)

        @block.scalar
        def _(act):
            act.wait_ge(small_in, 48)
            act.activation(b2[0:E, :], b2f[:], ACT.Copy, scale=UP).then_inc(b2_hi, 1)
            act.wait_ge(down_in[3], 16)
            act.activation(down[:, 6:8, :, 0, :].rearrange("p e m d -> p (e m) d"),
                           up_f[:, 6:8, :].rearrange("p e (m d) -> p (e m) d", m=MC), ACT.Copy,
                           scale=UP).then_inc(down_hi, 1)
            act.wait_ge(minus_done, 1)
            for q in range(ACT_ONES):
                last = act.activation(apart[:, q, :], iota_p, ACT.Square, bias=minus_r[:, q:q + 1], scale=1.0)
            last.then_inc(apart_done, 1)
            act.wait_ge(apart_done, 1)
            act.activation(hot_r[:, 0:ACT_ONES, :], apart[:], ACT.Relu, bias=1.0, scale=-1.0).then_inc(act_ones, 1)
            act.preload_act_table(ACT.Silu)
            act.wait_ge(texp_done, 1)

            def silu(t, s, after=True):
                if after:
                    act.wait_ge(h_lo, t - SLOTS + 1)
                e = act.value_load(texp_i[0:1, bass.ds(t, 1)], min_val=0, max_val=E - 1)
                act.wait_ge(h_full, t + 1)
                for m in range(MC):
                    last = act.activation(hT[s][:, m, :], hb[s][:, m * P:(m + 1) * P], ACT.Silu,
                                          bias=b1[:, bass.ds(e * MC + m, 1)], scale=DOWN)
                last.then_inc(silu_done, 1)
                act.wait_ge(silu_done, t + 1)
                if after:
                    act.wait_ge(y_full, t - SLOTS + 1)
                act.activation(hTh[s][:], hT[s][:], ACT.Copy, scale=MID).then_inc(h_hi, 1)

            for s in range(SLOTS):
                silu(s, s, after=False)
            with act.Fori(1, TILES // SLOTS) as i:
                for s in range(SLOTS):
                    silu(i * SLOTS + s, s)
            for s in range(SLOTS):
                act.wait_ge(scattered[s], 16 * (TILES // SLOTS))
            for g in range(1, G, 2):
                act.dma_start(z[:, 1, g * GB:(g + 1) * GB], picked_t[1, g]).then_inc(z1_in[g], 16)
            for g in range(1, G, 2):
                act.wait_ge(fin_done, g + 1)
                act.dma_start(out_t[g], z[:, 0, g * GB:(g + 1) * GB]).then_inc(out_done, 16)

        @block.vector
        def _(dve):
            step = [0]

            def done(ins):
                step[0] += 1
                ins.then_inc(chain, 1)
                dve.wait_ge(chain, step[0])

            dve.sem_inc(y_free, 1)
            dve.tensor_scalar(gs[:], ge[:], 1.0, None, ALU.add)
            dve.tensor_copy(beforeh[:], before)
            dve.memset(onesh[:], 1.0)
            for k in range(2):
                ins = dve.tensor_tensor(hot[:, k], iota8.unsqueeze(1).to_broadcast([P, B, E]),
                                        eidx[:, :, k:k + 1].to_broadcast([P, B, E]), ALU.is_equal)
            done(ins)
            done(dve.tensor_tensor(both[:], hot[:, 0], hot[:, 1], ALU.add))
            dve.tensor_tensor(sign[:], eidx[:, :, 0], eidx[:, :, 1], ALU.is_lt)
            done(dve.reciprocal(g1[:], gs[:]))
            dve.tensor_scalar(sign[:], sign[:], 2.0, -1.0, ALU.mult, ALU.add)
            dve.tensor_copy(iotah[:], iota_p)
            done(dve.tensor_tensor(g2[:], ge[:], g1[:], ALU.mult))
            dve.tensor_tensor(m1[:], m1[:], g1[:].unsqueeze(2).to_broadcast([P, GB, E]), ALU.mult)
            dve.tensor_tensor(m2[:], m2[:], g2[:].unsqueeze(2).to_broadcast([P, GB, E]), ALU.mult)
            done(dve.tensor_tensor(signed[:, 0], sign[:], token, ALU.mult))
            dve.tensor_scalar(signed[:, 1], signed[:, 0], -1.0, None, ALU.mult)
            dve.tensor_tensor(row[:, :, 2 * D:ROW].bitcast(F32), m1[:], m2[:], ALU.add).then_inc(last_row, 1)
            dve.memset(texp_all[:], 0.0)
            dve.wait_ge(rank_full, 1)
            done(dve.tensor_copy(count[:], rank[:, B * E:(B + 1) * E]))
            done(dve.tensor_tensor(over[:], count[:].unsqueeze(2).to_broadcast([P, E, B]),
                                   steps.unsqueeze(1).to_broadcast([P, E, B]), ALU.is_gt))
            done(dve.tensor_reduce(ntiles[:], over[:], AX, ALU.add))
            done(dve.tensor_tensor(mixed[:], ntiles[:].unsqueeze(1).to_broadcast([P, E, E]),
                                   less.rearrange("p (a b) -> p a b", a=E), ALU.mult))
            done(dve.tensor_reduce(first[:], mixed[:], AX, ALU.add))
            done(dve.tensor_scalar(first_s[:], first[:], float(P), None, ALU.mult))
            done(dve.tensor_tensor(place[:], rank[:, 0:B * E].rearrange("p (b e) -> p b e", b=B),
                                   first_s[:].unsqueeze(1).to_broadcast([P, B, E]), ALU.add))
            done(dve.tensor_tensor(placed[:].rearrange("p k b e -> p k (b e)"),
                                   hot[:].rearrange("p k b e -> p k (b e)"),
                                   place[:].rearrange("p b e -> p (b e)").unsqueeze(1).to_broadcast([P, 2, B * E]),
                                   ALU.mult))
            done(dve.tensor_reduce(slot[:], placed[:].rearrange("p k b e -> p (k b) e"), AX, ALU.add))
            done(dve.tensor_copy(sloti[:], slot[:]))
            dve.tensor_scalar(ti[:], sloti[:], 7, None, ALU.arith_shift_right)
            done(dve.tensor_scalar(ri[:], sloti[:], P - 1, None, ALU.bitwise_and))
            dve.tensor_copy(tf[:], ti[:])
            dve.tensor_scalar(minus_r[:], ri[:, 0:ACT_ONES], -1.0, None, ALU.mult).then_inc(minus_done, 1)
            done(dve.tensor_copy(rf[:], ri[:]))
            dve.tensor_tensor(hot_t[:], iotah[:, 0:TILES].unsqueeze(1).to_broadcast([P, 2 * B, TILES]),
                              tf[:].unsqueeze(2).to_broadcast([P, 2 * B, TILES]), ALU.is_equal).then_inc(hot_t_done, 1)
            for q in range(ACT_ONES, 2 * B, ONES):
                dve.tensor_tensor(hot_r[:, q:q + ONES, :], iotah[:].unsqueeze(1).to_broadcast([P, ONES, P]),
                                  rf[:, q:q + ONES].unsqueeze(2).to_broadcast([P, ONES, P]), ALU.is_equal)\
                    .then_inc(row_ones, 1)
            dve.wait_ge(b2_hi, 1)
            dve.scalar_tensor_tensor(out=b2l[:], in0=b2f[:], scalar=UP, in1=b2[0:E, :], op0=ALU.mult,
                                     op1=ALU.subtract).then_inc(b2_lo, 1)
            dve.wait_ge(table_full, 1)
            done(dve.tensor_copy(inv[:], table[:, 0:TILES]))
            done(dve.scalar_tensor_tensor(out=mag[:], in0=inv[:], scalar=-1.0, in1=inv[:], op0=ALU.mult, op1=ALU.max))
            dve.tensor_scalar(src_row[:], mag[:], -1.0, 0.0, ALU.add, ALU.max).then_inc(idx_done, 1)
            done(dve.tensor_tensor(last_t[:], first[:], ntiles[:], ALU.add))
            done(dve.tensor_tensor(below[:], last_t[:].unsqueeze(1).to_broadcast([P, TILES, E]),
                                   iota_t.unsqueeze(2).to_broadcast([P, TILES, E]), ALU.is_le))
            done(dve.tensor_reduce(texp, below[:], AX, ALU.add))
            done(dve.tensor_scalar(texp, texp, float(E - 1), None, ALU.min))
            done(dve.tensor_copy(texp_i[:], texp))
            dve.sem_inc(texp_done, 1)
            done(dve.tensor_tensor(digits[:], texp_all[:].rearrange("p (i s) -> p i s", s=STEPS),
                                   octal.unsqueeze(1).to_broadcast([P, TURNS, STEPS]), ALU.mult))
            done(dve.tensor_reduce(packed[:], digits[:], AX, ALU.add))
            dve.tensor_copy(packed_i[:], packed[:]).then_inc(packed_done, 1)
            dve.tensor_scalar(size[:], mag[:], -1.0, None, ALU.add)
            dve.tensor_scalar(isneg[:], inv[:], 0.0, float(B * L), ALU.is_lt, ALU.mult)
            done(dve.tensor_scalar(iszero[:], inv[:], 0.0, float(SKIP), ALU.is_equal, ALU.mult))
            done(dve.tensor_tensor(dsum[:], size[:], isneg[:], ALU.add))
            dve.tensor_tensor(dst_row[:], dsum[:], iszero[:], ALU.add).then_inc(dst_done, 1)

            def hidden_low(t, k):
                s = k % SLOTS
                dve.wait_ge(h_hi, t + 1)
                dve.scalar_tensor_tensor(out=hTl[s][:], in0=hT[s][:], scalar=MID, in1=hTh[s][:], op0=ALU.mult,
                                         op1=ALU.subtract).then_inc(h_lo, 1)

            def take(t, k, after=True):
                s = k % SLOTS
                e = dve.value_load(texp_i[0:1, bass.ds(t, 1)], min_val=0, max_val=E - 1)
                dve.wait_ge(tp_full, t + 1)
                dve.tensor_copy(xt[s][:].rearrange("p a b -> p (a b)"), tp[:].bitcast(F16)[:, 0:4 * P])
                if after:
                    dve.wait_ge(y_free, t - STEPS + 2)
                dve.tensor_scalar(gate[k % STEPS][:], got[s][:].bitcast(F32)[:, bass.ds(e + D, 1)], MID_DOWN, None,
                                  ALU.mult).then_inc(tp_free, 1)

            def weigh(t, k, n, after=True):
                s = k % SLOTS
                if after:
                    dve.wait_ge(scattered[s], 16 * n)
                dve.wait_ge(y_full, t + 1)
                g = gate[k % STEPS]
                dve.tensor_scalar(ys[s][:], yb[s][:, 0:D], g[:], None, ALU.mult).then_inc(y_part, 1)
                dve.wait_ge(y_part, t + 1)
                dve.scalar_tensor_tensor(out=ys[s][:], in0=yb[s][:, D:2 * D], scalar=g[:], in1=ys[s][:],
                                         op0=ALU.mult, op1=ALU.add).then_inc(y_free, 1)

            take(0, 0, after=False)
            take(1, 1, after=False)
            dve.wait_ge(down_hi, 4)
            dve.scalar_tensor_tensor(out=down[:, 6:8, :, 1, :].rearrange("p e m d -> p (e m) d"),
                                     in0=up_f[:, 6:8, :].rearrange("p e (m d) -> p (e m) d", m=MC), scalar=UP,
                                     in1=down[:, 6:8, :, 0, :].rearrange("p e m d -> p (e m) d"),
                                     op0=ALU.mult, op1=ALU.subtract).then_inc(down_lo, 1)
            done(dve.tensor_scalar(early[:], iota_t.rearrange("p (n s) -> p n s", s=SLOTS)[:, :, 0], first[:, E - 1:E], None,
                                   ALU.is_lt))
            done(dve.tensor_reduce(early_n[:], early[:], AX, ALU.add))
            dve.tensor_scalar(early_i[:], early_n[:], 16.0, 16.0, ALU.mult, ALU.max).then_inc(early_done, 1)

            for t in range(STEPS):
                take(t + 2, t + 2, after=t + 2 >= STEPS)
                if t >= LAG:
                    weigh(t - LAG, t - LAG, (t - LAG) // SLOTS, after=t - LAG >= SLOTS)
                hidden_low(t, t)
            with dve.Fori(1, TILES // STEPS) as i:
                for s in range(STEPS):
                    t = i * STEPS + s
                    take(t + 2, s + 2)
                    weigh(t - LAG, s + STEPS - LAG, i * (STEPS // SLOTS) + (s - LAG) // SLOTS)
                    hidden_low(t, s)
            for t in range(TILES // STEPS * STEPS, TILES + LAG):
                if t + 2 < TILES:
                    take(t + 2, t + 2)
                weigh(t - LAG, t - LAG, (t - LAG) // SLOTS)
                if t < TILES:
                    hidden_low(t, t)

            for g in range(G):
                b = slice(g * GB, (g + 1) * GB)
                dve.wait_ge(z0_in[g], 16)
                dve.tensor_tensor(z[:, 0, b], z[:, 0, b], base[:, b, :], ALU.add).then_inc(summed, 1)
            for g in range(G):
                b = slice(g * GB, (g + 1) * GB)
                dve.wait_ge(summed, g + 1)
                dve.wait_ge(z1_in[g], 16)
                dve.tensor_tensor(z[:, 0, b], z[:, 0, b], z[:, 1, b], ALU.add).then_inc(fin_done, 1)

        @block.tensor
        def _(pe):
            LOAD_AT = 4
            pe.wait_ge(chain, 2)
            flat = both[:].rearrange("p b e -> p (b e)")
            pe.matmul(rank[:, 0:B * E], beforeh[:], flat, start=True, stop=True, skip_group_check=True)
            for b in range(B):
                n = B - b
                ins = pe.matmul(rank[:, (b + 1) * E:(B + 1) * E].rearrange("p (n e) -> p n e", n=n), onesh[:],
                                both[:, b:b + 1, :].to_broadcast([P, n, E]), start=False, stop=True,
                                skip_group_check=True)
            ins.then_inc(rank_full, 1)
            pe.wait_ge(pay_done, 1)
            for q in range(2 * B):
                j = (q + ACT_ONES) % (2 * B)
                if j == 0:
                    pe.wait_ge(act_ones, 1)
                elif j >= ACT_ONES and (j - ACT_ONES) % ONES == 0:
                    pe.wait_ge(row_ones, (j - ACT_ONES) // ONES + 1)
                ins = pe.matmul(table[:, 0:TILES], hot_r[:, j, :], pay[:, j, :], start=(q == 0), stop=(q == 2 * B - 1))
            ins.then_inc(table_full, 1)

            def turn(t, k, n):
                s = k % SLOTS
                pe.wait_ge(gathered[s], 16 * n)
                pe.wait_ge(tp_free, t)
                g = got[s][:].bitcast(F16)
                v = tp[:].bitcast(F16)
                for j in range(4):
                    ins = pe.transpose(v[:, j * P:(j + 1) * P], g[:, j * P:(j + 1) * P], identh[:])
                ins.then_inc(tp_full, 1)

            down_rows = down[:].rearrange("p e m k d -> p (e m k d)")

            next_turn = ctx.enter_context(pe.register("next_turn"))
            last = [ctx.enter_context(pe.register(f"last{k}")) for k in range(LAG)]

            def load(i, es=None):
                pe.reg_load(next_turn, packed_i[0:1, bass.ds(i, 1)])
                for k in range(LAG if es else 0):
                    pe.reg_mov(last[k], es[STEPS - LAG + k])

            def experts():
                w = pe.snap(next_turn, min_val=0, max_val=E ** STEPS - 1)
                return [(w >> (3 * k)) & (E - 1) for k in range(STEPS)]

            def earlier():
                return [pe.snap(r, min_val=0, max_val=E - 1) for r in last]

            def step(t, k, e, before, first=False):
                s, q = k % SLOTS, (k - LAG) % SLOTS
                if e is not None:
                    pe.wait_ge(tp_free, t + 1)
                for m in range(MC):
                    j = 0
                    for c in range(KC) if e is not None else ():
                        for w, x in ((up_h, c), (up_h, KC + c), (up_l, c)):
                            lhs = w[:, bass.ds(e, 1), c, m * P:(m + 1) * P].rearrange("p a n -> p (a n)")
                            ins = pe.matmul(hb[s][:, m * P:(m + 1) * P], lhs, xt[s][:, x, :],
                                            start=(j == 0), stop=(j == 3 * KC - 1))
                            j += 1
                    if m == MC - 1 and e is not None:
                        ins.then_inc(h_full, 1)
                    if before is None:
                        continue
                    if m == 0:
                        pe.wait_ge(h_lo, t - LAG + 1)
                        if not first:
                            pe.wait_ge(y_free, t - LAG - SLOTS + 2)
                    at = before * (2 * MC * D) + m * 2 * D
                    pe.matmul(yb[q][:], hTh[q][:, m, :], down_rows[:, bass.ds(at, 2 * D)],
                              start=(m == 0), stop=False, skip_group_check=True)
                    pe.matmul(yb[q][:, 0:D], hTl[q][:, m, :], down_rows[:, bass.ds(at, D)],
                              start=False, stop=False, skip_group_check=True)
                if before is not None:
                    pe.matmul(yb[q][:, 0:D], pick[:, bass.ds(before * P, P)], b2[:], start=False, stop=True,
                              skip_group_check=True).then_inc(y_full, 1)

            turn(0, 0, 1)
            turn(1, 1, 1)
            pe.wait_ge(up_hi, 4)
            pe.wait_ge(up_lo, 4)
            pe.wait_ge(packed_done, 1)

            load(0)
            own = experts()
            for t in range(STEPS):
                if t == LAG:
                    pe.wait_ge(down_hi, 4)
                    pe.wait_ge(down_lo, 4)
                    pe.wait_ge(b2_lo_in, 16)
                step(t, t, own[t], own[t - LAG] if t >= LAG else None, first=t - LAG < SLOTS)
                if t == LOAD_AT:
                    load(1, own)
                turn(t + 2, t + 2, (t + 2) // SLOTS + 1)
            with pe.Fori(1, TILES // STEPS) as i:
                t = i * STEPS
                before, own = earlier(), experts()
                for s in range(STEPS):
                    step(t + s, s, own[s], before[s] if s < LAG else own[s - LAG])
                    if s == LOAD_AT:
                        load(i + 1, own)
                    turn(t + s + 2, s + 2, i * (STEPS // SLOTS) + (s + 2) // SLOTS + 1)
            before, own = earlier(), experts()
            for s in range(TILES % STEPS + LAG):
                t = TILES // STEPS * STEPS + s
                step(t, t, own[s] if t < TILES else None, before[s] if s < LAG else own[s - LAG])
                if t + 2 < TILES:
                    turn(t + 2, t + 2, (t + 2) // SLOTS + 1)


def extra_data(np, n, data):
    f = np.float32
    p = np.arange(P)
    row = lambda v: np.tile(np.asarray(v, f), (P, 1))
    data["ew1"] = n["L0_ffn_ew1"].reshape(E, KC, P, HID).transpose(2, 0, 1, 3).reshape(P, E, KC * HID)
    data["eb1"] = n["L0_ffn_eb1"].reshape(E, MC, P).transpose(2, 0, 1).reshape(P, E * MC)
    data["ew2"] = n["L0_ffn_ew2"].reshape(E, MC, P, D).transpose(2, 0, 1, 3).reshape(P, E, MC * D)
    data["pick_expert"] = np.repeat(np.tile(16.0 * np.eye(E), (2, 1)), P, axis=1).astype(np.float16)
    data["eb2"] = n["L0_ffn_eb2"]
    data["disp"] = np.concatenate([
        (p[:, None] < p[None, :]).astype(f), row(p), row(np.arange(TILES)), row(P * np.arange(B)),
        row((np.arange(E)[None, :] < np.arange(E)[:, None]).reshape(-1)),
        (np.arange(B)[None, :] + B * p[:, None] + 1).astype(f), row(np.arange(E)), np.eye(P, dtype=f),
        row(float(E) ** np.arange(STEPS))], axis=1)


def build(nc, a, out):
    shared = {"rows": nc.dram_tensor("rows", [B * L, ROW // 2], U32, kind="Internal").ap(),
              "picked": nc.dram_tensor("picked", [2 * B * L, D], F32, kind="Internal").ap()}
    with ExitStack() as ctx:
        for name, shape, dt in (("base", [P, B, D], F32), ("eidx", [P, B, 2], F32),
                                ("dc", [P, sum(n for _, n in CONSTS)], F32), ("identh", [P, P], F16),
                                ("up_f", [P, E, KC * HID], F32), ("up_h", [P, E, KC, HID], F16),
                                ("up_l", [P, E, KC, HID], F16), ("down", [P, E, MC, 2, D], F16),
                                ("row", [P, GB, ROW], F16), ("ge", [P, GB], F32), ("gs", [P, GB], F32),
                                ("g1", [P, GB], F32), ("g2", [P, GB], F32), ("m1", [P, GB, E], F32),
                                ("m2", [P, GB, E], F32)):
            shared[name] = ctx.enter_context(nc.sbuf_tensor(name, shape, dt))
        for name in ("up_hi", "up_lo", "down_up", "down_hi", "down_lo", "row_out"):
            shared[name] = ctx.enter_context(nc.semaphore(name))
        for name in ("up_in", "down_in"):
            shared[name] = [ctx.enter_context(nc.semaphore(f"{name}{i}")) for i in range(4)]
        at, shared["cols"] = 0, {}
        for name, n in CONSTS:
            shared["cols"][name] = shared["dc"][:, at:at + n]
            at += n
        attention_phase(nc, shared, tuple(a[k] for k in ("x", "ctx", "w1", "w2", "wc", "xbias", "bc", "rw1", "rb1", "rw2",
                                                         "rb2", "consts", "disp", "ew1", "ew2")))
        expert_phase(nc, shared, tuple(a[k] for k in ("eb1", "eb2", "pick_expert")), out)


def shape_constants(np):
    f = np.float32
    i = np.arange(D // 2, dtype=f)
    theta = np.power(f(10000.0), (f(-2.0) * (i - f(1.0)) / f(D)).astype(f)).astype(f)
    ang = (np.arange(L, dtype=f)[:, None] * theta[None, :]).astype(f)
    q = np.arange(L)[:, None]
    k = np.arange(L)[None, :]
    masks = [np.where(k <= q, 0.0, NEG)]
    for d in (1, 2, 4, 8):
        off = k - q
        ok = (off % d == 0) & (off // d >= -((WIN - 1) // 2)) & (off // d <= WIN - 1 - (WIN - 1) // 2)
        masks.append(np.where(ok, 0.0, NEG))
    return np.concatenate([np.cos(ang).T, np.sin(ang).T] + masks, axis=1).astype(f)


def kernel(**inputs):
    import numpy as np
    import concourse.bacc as bacc
    from concourse.bass_utils import run_bass_kernel_spmd

    def chunks(a):
        return a.reshape(KC, P, -1).transpose(1, 0, 2)

    n = {k: np.asarray(v) for k, v in inputs.items()}
    wq, wk, wv = n["L0_attn_w_q"], n["L0_attn_w_k"], n["L0_attn_w_v"]
    data = {
        "x": n["x"],
        "ctx": n["ctx_1024"],
        "w1": chunks(np.concatenate([wq[0::2], wq[1::2], wk[0::2], wk[1::2], wv], axis=0).T),
        "w2": chunks(np.concatenate([n["L0_xattn_" + w].reshape(H * DH, D) for w in ("Wk", "Wv", "Wq")], axis=0).T),
        "wc": n["L0_xattn_Wc"].T.reshape(H, DH, D).transpose(1, 0, 2),
        "xbias": np.concatenate([n["L0_xattn_" + w].T for w in ("bq", "bk", "bv")], axis=1),
        "bc": n["L0_xattn_bc"],
        "rw1": chunks(n["L0_ffn_rw1"]),
        "rb1": n["L0_ffn_rb1"].reshape(KC, P).T,
        "rw2": chunks(n["L0_ffn_rw2"]),
        "rb2": n["L0_ffn_rb2"],
        "consts": shape_constants(np),
    }
    extra_data(np, n, data)
    nc = bacc.Bacc("TRN2", target_bir_lowering=False, num_devices=1)
    arrays, aps = {}, {}
    for name, a in data.items():
        arrays["in_" + name] = np.ascontiguousarray(a)
        aps[name] = nc.dram_tensor("in_" + name, a.shape, mybir.dt.from_np(a.dtype), kind="ExternalInput").ap()
    out = nc.dram_tensor("out", [B, L, D], F32, kind="ExternalOutput").ap()
    build(nc, aps, out)
    r = run_bass_kernel_spmd(nc, [arrays], core_ids=[0])
    return r.results[0]["out"]
```
